# Optimizing a Trainium2 kernel written in Bass

```python
import numpy as np
import jax
import jax.numpy as jnp

def _softmax(x, axis=-1):
    return jax.nn.softmax(x, axis=axis)

def _gelu(x):
    return jax.nn.gelu(x, approximate=True)

def _silu(x):
    return jax.nn.silu(x)

def _sigmoid(x):
    return jax.nn.sigmoid(x)

def _layernorm(x, axis=-1, eps=1e-05):
    m = jnp.mean(x, axis=axis, keepdims=True)
    v = jnp.var(x, axis=axis, keepdims=True)
    return (x - m) / jnp.sqrt(v + eps)

def _scatter_add(tgt, idx, src, axis=0):
    return tgt.at[idx].add(src)

def _segment_sum(src, seg, n):
    return jax.ops.segment_sum(src, seg, n)
kernel_name = 'mk_macaron_d4_jaxref_r8_d9d932'

def setup_inputs(seed: int=0):
    np.random.seed(seed)
    _w = jnp.asarray

    def _L0_attn_setup():
        import jax, jax.numpy as jnp
        import numpy as np
        N_HEADS = 16
        MAX_LEN = 128
        key = jax.random.key(seed)
        ks = jax.random.split(key, 6)
        B, T, C = (4, 128, 128)
        scale = 0.02
        return {'x': jax.random.normal(ks[0], (B, T, C), dtype=jnp.float32), 'qkv_w': jax.random.normal(ks[1], (3 * C, C), dtype=jnp.float32) * scale, 'qkv_b': jax.random.normal(ks[2], (3 * C,), dtype=jnp.float32) * scale, 'proj_w': jax.random.normal(ks[3], (C, C), dtype=jnp.float32) * scale, 'proj_b': jax.random.normal(ks[4], (C,), dtype=jnp.float32) * scale, 'rel_pos_emb': jax.random.normal(ks[5], (2 * MAX_LEN - 1, C), dtype=jnp.float32) * scale}
    _L0_attn_in = _L0_attn_setup()

    def _L0_ffn_setup():
        import jax, jax.numpy as jnp
        import numpy as np
        B, S, D = (4, 256, 128)
        E = 8
        DFF = 512
        CAP_FACTOR = 1.25
        key = jax.random.key(seed)
        ks = jax.random.split(key, 4)
        std_gate = float(np.sqrt(0.1 / D))
        inputs = jax.random.normal(ks[0], (B, S, D), dtype=jnp.float32)
        gate_w = jax.random.normal(ks[1], (E, D), dtype=jnp.float32) * std_gate
        w1 = jax.random.normal(ks[2], (E, D, DFF), dtype=jnp.float32) * (1.0 / np.sqrt(D))
        b1 = jnp.zeros((E, DFF), dtype=jnp.float32)
        w2 = jax.random.normal(ks[3], (E, DFF, D), dtype=jnp.float32) * (1.0 / np.sqrt(DFF))
        b2 = jnp.zeros((E, D), dtype=jnp.float32)
        return {'inputs': inputs, 'gate_w': gate_w, 'w1': w1, 'b1': b1, 'w2': w2, 'b2': b2}
    _L0_ffn_in = _L0_ffn_setup()

    def _L1_attn_setup():
        import jax, jax.numpy as jnp
        import numpy as np
        B, N, C, H = (2, 256, 128, 16)
        R1, R2 = (4, 8)
        HEAD_DIM = C // H
        SCALE = float((R1 * R2) ** (-0.5))
        key = jax.random.key(seed)
        ks = jax.random.split(key, 8)
        g = lambda k, shape, s: jax.random.normal(k, shape, jnp.float32) * s
        return {'x': g(ks[0], (B, N, C), 1.0), 'Wq1': g(ks[1], (H * R1, C), C ** (-0.5)), 'Wk1': g(ks[2], (H * R1, C), C ** (-0.5)), 'Wq2': g(ks[3], (H * R2, C), C ** (-0.5)), 'Wk2': g(ks[4], (H * R2, C), C ** (-0.5)), 'Wv': g(ks[5], (C, C), C ** (-0.5)), 'Wo': g(ks[6], (C, C), C ** (-0.5)), 'bo': jnp.zeros((C,), jnp.float32)}
    _L1_attn_in = _L1_attn_setup()

    def _L1_ffn_setup():
        import jax, jax.numpy as jnp
        import numpy as np
        H = 128
        I = 64
        E = 8
        TOP_K = 2
        N_SHARED = 2
        SHARED_I = I * N_SHARED
        SCALE = 2.5
        NORM_TOPK = True
        B, S = (2, 128)

        def _swiglu(x, wg, wu, wd):
            g = x @ wg.T
            u = x @ wu.T
            return jax.nn.silu(g) * u @ wd.T
        key = jax.random.key(seed)
        ks = jax.random.split(key, 8)
        std = 0.02
        return {'hidden_states': jax.random.normal(ks[0], (B, S, H), jnp.float32), 'gate_weight': jax.random.normal(ks[1], (E, H), jnp.float32) * std, 'w_gate': jax.random.normal(ks[2], (E, I, H), jnp.float32) * std, 'w_up': jax.random.normal(ks[3], (E, I, H), jnp.float32) * std, 'w_down': jax.random.normal(ks[4], (E, H, I), jnp.float32) * std, 'ws_gate': jax.random.normal(ks[5], (SHARED_I, H), jnp.float32) * std, 'ws_up': jax.random.normal(ks[6], (SHARED_I, H), jnp.float32) * std, 'ws_down': jax.random.normal(ks[7], (H, SHARED_I), jnp.float32) * std}
    _L1_ffn_in = _L1_ffn_setup()

    def _L2_attn_setup():
        import jax, jax.numpy as jnp
        import numpy as np
        from jax import lax
        D_MODEL = 128
        BATCH = 4
        SEQ = 512
        DECAY = 0.9
        INPUT_SCALE = 0.1
        key = jax.random.key(seed)
        k1, k2, k3 = jax.random.split(key, 3)
        scale_in = 1.0 / np.sqrt(D_MODEL)
        return {'x': jax.random.normal(k1, (BATCH, SEQ, D_MODEL), dtype=jnp.float32), 'W_in': jax.random.normal(k2, (D_MODEL, 2 * D_MODEL), dtype=jnp.float32) * scale_in, 'b_in': jnp.zeros((2 * D_MODEL,), dtype=jnp.float32), 'W_out': jax.random.normal(k3, (D_MODEL, D_MODEL), dtype=jnp.float32) * scale_in, 'b_out': jnp.zeros((D_MODEL,), dtype=jnp.float32)}
    _L2_attn_in = _L2_attn_setup()

    def _L2_ffn_setup():
        import jax, jax.numpy as jnp
        import numpy as np
        D_MODEL = 128
        HIDDEN = 512
        NUM_EXPERTS = 8
        TOP_K = 2
        key = jax.random.key(seed)
        k_x, k_g, k_in, k_out = jax.random.split(key, 4)
        bound_in = 1.0 / HIDDEN
        bound_out = 1.0 / D_MODEL
        x = jax.random.normal(k_x, (2, 256, D_MODEL), dtype=jnp.float32)
        w_gate = jax.random.uniform(k_g, (NUM_EXPERTS, D_MODEL), dtype=jnp.float32, minval=-D_MODEL ** (-0.5), maxval=D_MODEL ** (-0.5))
        w_in = jax.random.uniform(k_in, (NUM_EXPERTS, HIDDEN, D_MODEL), dtype=jnp.float32, minval=-bound_in, maxval=bound_in)
        w_out = jax.random.uniform(k_out, (NUM_EXPERTS, D_MODEL, HIDDEN), dtype=jnp.float32, minval=-bound_out, maxval=bound_out)
        return {'x': x, 'w_gate': w_gate, 'w_in': w_in, 'w_out': w_out}
    _L2_ffn_in = _L2_ffn_setup()

    def _L3_attn_setup():
        import jax, jax.numpy as jnp
        import numpy as np
        H = 128
        NH = 16
        HD = H // NH
        EPS = 1e-05

        def _attn_block(x, ln_gamma, ln_beta, W_qkv, b_qkv, W_out, b_out):
            B, S, _ = x.shape
            mu = jnp.mean(x, axis=-1, keepdims=True)
            var = jnp.mean(jnp.square(x - mu), axis=-1, keepdims=True)
            xn = (x - mu) / jnp.sqrt(var + EPS) * ln_gamma + ln_beta
            qkv = jnp.einsum('bsh,oh->bso', xn, W_qkv) + b_qkv
            qkv = qkv.reshape(B, S, 3, NH, HD).transpose(2, 0, 3, 1, 4)
            q, k, v = (qkv[0], qkv[1], qkv[2])
            scores = jnp.einsum('bhqd,bhkd->bhqk', q, k) / jnp.sqrt(jnp.asarray(HD, x.dtype))
            probs = jax.nn.softmax(scores, axis=-1)
            ctx = jnp.einsum('bhqk,bhkd->bhqd', probs, v)
            ctx = ctx.transpose(0, 2, 1, 3).reshape(B, S, H)
            out = jnp.einsum('bsh,oh->bso', ctx, W_out) + b_out
            return x + out
        key = jax.random.key(seed)
        ks = jax.random.split(key, 5)
        b_qkv = float(np.sqrt(6.0 / (H + 3 * H)))
        b_out = float(np.sqrt(6.0 / (H + H)))
        return {'hidden_states': jax.random.normal(ks[0], (2, 256, H), dtype=jnp.float32), 'ln_gamma': jnp.ones((H,), jnp.float32), 'ln_beta': jnp.zeros((H,), jnp.float32), 'W_qkv': jax.random.uniform(ks[1], (3 * H, H), jnp.float32, -b_qkv, b_qkv), 'b_qkv': jnp.zeros((3 * H,), jnp.float32), 'W_out': jax.random.uniform(ks[2], (H, H), jnp.float32, -b_out, b_out), 'b_out': jnp.zeros((H,), jnp.float32)}
    _L3_attn_in = _L3_attn_setup()

    def _L3_ffn_setup():
        import jax, jax.numpy as jnp
        import numpy as np
        B, S, D = (2, 256, 128)
        E, K, H = (8, 2, 512)
        CAP_FACTOR = 1.0

        def _moe_forward(x, wg, w1, b1, w2, b2):
            Bb, Ss, Dd = x.shape
            T = Bb * Ss
            cap = int(K * CAP_FACTOR * ((T + E - 1) // E))
            xt = x.reshape(T, Dd)
            logits = xt @ wg
            scores = jax.nn.softmax(logits, axis=-1)
            gates_k, idx_k = jax.lax.top_k(scores, K)
            gates_k = gates_k / jnp.sum(gates_k, axis=-1, keepdims=True)
            masks = jax.nn.one_hot(idx_k, E, dtype=jnp.int32)
            m = jnp.transpose(masks, (1, 0, 2)).reshape(K * T, E)
            locs_full = jnp.cumsum(m, axis=0) - 1
            loc = jnp.sum(locs_full * m, axis=-1)
            loc = loc.reshape(K, T).T
            valid = (loc < cap).astype(xt.dtype)
            loc_c = jnp.clip(loc, 0, cap - 1)
            contrib = (xt[:, None, :] * valid[:, :, None]).reshape(T * K, Dd)
            disp = jnp.zeros((E, cap, Dd), xt.dtype)
            disp = disp.at[idx_k.reshape(-1), loc_c.reshape(-1)].add(contrib)
            h = jax.nn.relu(jnp.einsum('ecd,edh->ech', disp, w1) + b1[:, None, :])
            out = jnp.einsum('ech,ehd->ecd', h, w2) + b2[:, None, :]
            gathered = out[idx_k, loc_c]
            y = jnp.einsum('tk,tkd->td', gates_k * valid, gathered)
            return y.reshape(Bb, Ss, Dd)
        key = jax.random.key(seed)
        ks = jax.random.split(key, 6)
        scale_in = 1.0 / np.sqrt(D)
        scale_h = 1.0 / np.sqrt(H)
        return {'x': jax.random.normal(ks[0], (B, S, D), jnp.float32), 'wg': jax.random.normal(ks[1], (D, E), jnp.float32) * scale_in, 'w1': jax.random.normal(ks[2], (E, D, H), jnp.float32) * scale_in, 'b1': jnp.zeros((E, H), jnp.float32), 'w2': jax.random.normal(ks[3], (E, H, D), jnp.float32) * scale_h, 'b2': jnp.zeros((E, D), jnp.float32)}
    _L3_ffn_in = _L3_ffn_setup()
    _d = {'L0_attn_x': _L0_attn_in['x'], 'L0_attn_qkv_w': _L0_attn_in['qkv_w'], 'L0_attn_qkv_b': _L0_attn_in['qkv_b'], 'L0_attn_proj_w': _L0_attn_in['proj_w'], 'L0_attn_proj_b': _L0_attn_in['proj_b'], 'L0_attn_rel_pos_emb': _L0_attn_in['rel_pos_emb'], 'L0_ffn_gate_w': _L0_ffn_in['gate_w'], 'L0_ffn_w1': _L0_ffn_in['w1'], 'L0_ffn_b1': _L0_ffn_in['b1'], 'L0_ffn_w2': _L0_ffn_in['w2'], 'L0_ffn_b2': _L0_ffn_in['b2'], 'L1_attn_Wq1': _L1_attn_in['Wq1'], 'L1_attn_Wk1': _L1_attn_in['Wk1'], 'L1_attn_Wq2': _L1_attn_in['Wq2'], 'L1_attn_Wk2': _L1_attn_in['Wk2'], 'L1_attn_Wv': _L1_attn_in['Wv'], 'L1_attn_Wo': _L1_attn_in['Wo'], 'L1_attn_bo': _L1_attn_in['bo'], 'L1_ffn_gate_weight': _L1_ffn_in['gate_weight'], 'L1_ffn_w_gate': _L1_ffn_in['w_gate'], 'L1_ffn_w_up': _L1_ffn_in['w_up'], 'L1_ffn_w_down': _L1_ffn_in['w_down'], 'L1_ffn_ws_gate': _L1_ffn_in['ws_gate'], 'L1_ffn_ws_up': _L1_ffn_in['ws_up'], 'L1_ffn_ws_down': _L1_ffn_in['ws_down'], 'L2_attn_W_in': _L2_attn_in['W_in'], 'L2_attn_b_in': _L2_attn_in['b_in'], 'L2_attn_W_out': _L2_attn_in['W_out'], 'L2_attn_b_out': _L2_attn_in['b_out'], 'L2_ffn_w_gate': _L2_ffn_in['w_gate'], 'L2_ffn_w_in': _L2_ffn_in['w_in'], 'L2_ffn_w_out': _L2_ffn_in['w_out'], 'L3_attn_ln_gamma': _L3_attn_in['ln_gamma'], 'L3_attn_ln_beta': _L3_attn_in['ln_beta'], 'L3_attn_W_qkv': _L3_attn_in['W_qkv'], 'L3_attn_b_qkv': _L3_attn_in['b_qkv'], 'L3_attn_W_out': _L3_attn_in['W_out'], 'L3_attn_b_out': _L3_attn_in['b_out'], 'L3_ffn_wg': _L3_ffn_in['wg'], 'L3_ffn_w1': _L3_ffn_in['w1'], 'L3_ffn_b1': _L3_ffn_in['b1'], 'L3_ffn_w2': _L3_ffn_in['w2'], 'L3_ffn_b2': _L3_ffn_in['b2']}
    _x0 = _d['L0_attn_x']
    _d['L0_attn_x'] = jax.random.normal(jax.random.fold_in(jax.random.key(seed), 1), (4, 512, 128), dtype=_x0.dtype)
    del _x0
    return _d

def reference(L0_attn_x, L0_attn_qkv_w, L0_attn_qkv_b, L0_attn_proj_w, L0_attn_proj_b, L0_attn_rel_pos_emb, L0_ffn_gate_w, L0_ffn_w1, L0_ffn_b1, L0_ffn_w2, L0_ffn_b2, L1_attn_Wq1, L1_attn_Wk1, L1_attn_Wq2, L1_attn_Wk2, L1_attn_Wv, L1_attn_Wo, L1_attn_bo, L1_ffn_gate_weight, L1_ffn_w_gate, L1_ffn_w_up, L1_ffn_w_down, L1_ffn_ws_gate, L1_ffn_ws_up, L1_ffn_ws_down, L2_attn_W_in, L2_attn_b_in, L2_attn_W_out, L2_attn_b_out, L2_ffn_w_gate, L2_ffn_w_in, L2_ffn_w_out, L3_attn_ln_gamma, L3_attn_ln_beta, L3_attn_W_qkv, L3_attn_b_qkv, L3_attn_W_out, L3_attn_b_out, L3_ffn_wg, L3_ffn_w1, L3_ffn_b1, L3_ffn_w2, L3_ffn_b2):

    def _L0_attn_ref(x, qkv_w, qkv_b, proj_w, proj_b, rel_pos_emb):
        import jax, jax.numpy as jnp
        import numpy as np
        N_HEADS = 16
        MAX_LEN = 128
        B, T, C = x.shape
        H = N_HEADS
        D = C // H
        qkv = (x @ qkv_w.T + qkv_b).reshape(B, T, 3, H, D)
        qkv = jnp.transpose(qkv, (2, 0, 3, 1, 4))
        q, k, v = (qkv[0], qkv[1], qkv[2])
        att = jnp.einsum('bhtd,bhsd->bhts', q, k) / np.sqrt(D).astype(np.float32)
        table = rel_pos_emb.reshape(2 * MAX_LEN - 1, H, D).sum(axis=-1)
        pos = jnp.arange(T)
        rel_idx = pos[:, None] - pos[None, :] + (MAX_LEN - 1)
        bias = jnp.transpose(table[rel_idx], (2, 0, 1))
        att = att + bias[None]
        causal = pos[None, :] > pos[:, None]
        att = jnp.where(causal[None, None], -jnp.inf, att)
        att = jax.nn.softmax(att, axis=-1)
        out = jnp.einsum('bhts,bhsd->bhtd', att, v)
        out = jnp.transpose(out, (0, 2, 1, 3)).reshape(B, T, C)
        return out @ proj_w.T + proj_b

    def _L0_ffn_ref(inputs, gate_w, w1, b1, w2, b2):
        import jax, jax.numpy as jnp
        import numpy as np
        B, S, D = (4, 256, 128)
        E = 8
        DFF = 512
        CAP_FACTOR = 1.25
        d_model = inputs.shape[-1]
        tokens = inputs.reshape(-1, d_model)
        T = tokens.shape[0]
        num_experts = gate_w.shape[0]
        capacity = int(np.ceil(CAP_FACTOR * T / num_experts))
        logits = jnp.einsum('td,ed->te', tokens.astype(jnp.float32), gate_w)
        probs = jax.nn.softmax(logits, axis=-1)
        expert_idx = jnp.argmax(probs, axis=-1)
        mask = jax.nn.one_hot(expert_idx, num_experts, dtype=jnp.float32)
        ranks = jnp.cumsum(mask, axis=0) - 1.0
        keep = (ranks < capacity) * mask
        pos = ranks.astype(jnp.int32)
        sec_mask = jax.nn.one_hot(pos, capacity, dtype=jnp.float32) * keep[:, :, None]
        combine_weights = probs[:, :, None] * sec_mask
        dispatch = jnp.einsum('tec,td->ecd', sec_mask, tokens)
        h = jax.nn.relu(jnp.einsum('ecd,edh->ech', dispatch, w1) + b1[:, None, :])
        expert_out = jnp.einsum('ech,ehd->ecd', h, w2) + b2[:, None, :]
        ans = jnp.einsum('tec,ecd->td', combine_weights, expert_out)
        return ans.reshape(inputs.shape)

    def _L1_attn_ref(x, Wq1, Wk1, Wq2, Wk2, Wv, Wo, bo):
        import jax, jax.numpy as jnp
        import numpy as np
        B, N, C, H = (2, 256, 128, 16)
        R1, R2 = (4, 8)
        HEAD_DIM = C // H
        SCALE = float((R1 * R2) ** (-0.5))
        b, n, c = x.shape
        q1 = (x @ Wq1.T).reshape(b, n, H, R1)
        k1 = (x @ Wk1.T).reshape(b, n, H, R1)
        q2 = (x @ Wq2.T).reshape(b, n, H, R2)
        k2 = (x @ Wk2.T).reshape(b, n, H, R2)
        v = (x @ Wv.T).reshape(b, n, H, HEAD_DIM)
        A1 = jnp.einsum('bnhr,bmhr->bhnm', q1, k1)
        A2 = jnp.einsum('bnhr,bmhr->bhnm', q2, k2)
        logits = A1 * A2 * SCALE
        causal = jnp.triu(jnp.ones((n, n), dtype=bool), 1)
        logits = jnp.where(causal[None, None], -jnp.inf, logits)
        attn = jax.nn.softmax(logits, axis=-1)
        out = jnp.einsum('bhnm,bmhd->bnhd', attn, v).reshape(b, n, c)
        return out @ Wo.T + bo

    def _L1_ffn_ref(hidden_states, gate_weight, w_gate, w_up, w_down, ws_gate, ws_up, ws_down):
        import jax, jax.numpy as jnp
        import numpy as np
        H = 128
        I = 64
        E = 8
        TOP_K = 2
        N_SHARED = 2
        SHARED_I = I * N_SHARED
        SCALE = 2.5
        NORM_TOPK = True
        B, S = (2, 128)

        def _swiglu(x, wg, wu, wd):
            g = x @ wg.T
            u = x @ wu.T
            return jax.nn.silu(g) * u @ wd.T
        b, s, h = hidden_states.shape
        x = hidden_states.reshape(-1, h)
        shared_out = _swiglu(x, ws_gate, ws_up, ws_down)
        logits = x.astype(jnp.float32) @ gate_weight.astype(jnp.float32).T
        scores = jax.nn.sigmoid(logits)
        topk_w, topk_idx = jax.lax.top_k(scores, TOP_K)
        if TOP_K > 1 and NORM_TOPK:
            topk_w = topk_w / (topk_w.sum(-1, keepdims=True) + 1e-20)
        topk_w = topk_w * SCALE
        onehot = jax.nn.one_hot(topk_idx, E, dtype=topk_w.dtype)
        combine = jnp.einsum('tk,tke->te', topk_w, onehot)
        g = jnp.einsum('th,eih->tei', x, w_gate)
        u = jnp.einsum('th,eih->tei', x, w_up)
        hmid = jax.nn.silu(g) * u
        y = jnp.einsum('tei,ehi->teh', hmid, w_down)
        routed_out = jnp.einsum('te,teh->th', combine, y)
        out = (routed_out + shared_out).reshape(b, s, h)
        return out

    def _L2_attn_ref(x, W_in, b_in, W_out, b_out):
        import jax, jax.numpy as jnp
        import numpy as np
        from jax import lax
        D_MODEL = 128
        BATCH = 4
        SEQ = 512
        DECAY = 0.9
        INPUT_SCALE = 0.1
        x_proj = jnp.einsum('bsd,de->bse', x, W_in) + b_in
        x_gate, x_hidden = jnp.split(x_proj, 2, axis=-1)
        x_gated = jax.nn.sigmoid(x_gate) * jax.nn.silu(x_hidden)

        def step(h, g_t):
            h = DECAY * h + INPUT_SCALE * g_t
            return (h, h)
        g_tm = jnp.swapaxes(x_gated, 0, 1)
        h0 = jnp.zeros((x.shape[0], x.shape[2]), dtype=x.dtype)
        _, hs = lax.scan(step, h0, g_tm)
        hidden_seq = jnp.swapaxes(hs, 0, 1)
        out = jnp.einsum('bsd,de->bse', hidden_seq, W_out) + b_out
        return out

    def _L2_ffn_ref(x, w_gate, w_in, w_out):
        import jax, jax.numpy as jnp
        import numpy as np
        D_MODEL = 128
        HIDDEN = 512
        NUM_EXPERTS = 8
        TOP_K = 2
        B, S, D = x.shape
        E = w_in.shape[0]
        xt = x.reshape(-1, D)
        logits = (xt @ w_gate.T).astype(jnp.float32)
        top_logits, top_idx = jax.lax.top_k(logits, TOP_K)
        top_gates = jax.nn.softmax(top_logits, axis=-1).astype(x.dtype)
        gates = (jax.nn.one_hot(top_idx, E, dtype=x.dtype) * top_gates[..., None]).sum(axis=1)
        y = jnp.zeros_like(xt)
        for e in range(E):
            h = xt @ w_in[e].T
            y = y + gates[:, e:e + 1] * (h @ w_out[e].T)
        return y.reshape(B, S, D)

    def _L3_attn_ref(hidden_states, ln_gamma, ln_beta, W_qkv, b_qkv, W_out, b_out):
        import jax, jax.numpy as jnp
        import numpy as np
        H = 128
        NH = 16
        HD = H // NH
        EPS = 1e-05

        def _attn_block(x, ln_gamma, ln_beta, W_qkv, b_qkv, W_out, b_out):
            B, S, _ = x.shape
            mu = jnp.mean(x, axis=-1, keepdims=True)
            var = jnp.mean(jnp.square(x - mu), axis=-1, keepdims=True)
            xn = (x - mu) / jnp.sqrt(var + EPS) * ln_gamma + ln_beta
            qkv = jnp.einsum('bsh,oh->bso', xn, W_qkv) + b_qkv
            qkv = qkv.reshape(B, S, 3, NH, HD).transpose(2, 0, 3, 1, 4)
            q, k, v = (qkv[0], qkv[1], qkv[2])
            scores = jnp.einsum('bhqd,bhkd->bhqk', q, k) / jnp.sqrt(jnp.asarray(HD, x.dtype))
            probs = jax.nn.softmax(scores, axis=-1)
            ctx = jnp.einsum('bhqk,bhkd->bhqd', probs, v)
            ctx = ctx.transpose(0, 2, 1, 3).reshape(B, S, H)
            out = jnp.einsum('bsh,oh->bso', ctx, W_out) + b_out
            return x + out
        return _attn_block(hidden_states, ln_gamma, ln_beta, W_qkv, b_qkv, W_out, b_out)

    def _L3_ffn_ref(x, wg, w1, b1, w2, b2):
        import jax, jax.numpy as jnp
        import numpy as np
        B, S, D = (2, 256, 128)
        E, K, H = (8, 2, 512)
        CAP_FACTOR = 1.0

        def _moe_forward(x, wg, w1, b1, w2, b2):
            Bb, Ss, Dd = x.shape
            T = Bb * Ss
            cap = int(K * CAP_FACTOR * ((T + E - 1) // E))
            xt = x.reshape(T, Dd)
            logits = xt @ wg
            scores = jax.nn.softmax(logits, axis=-1)
            gates_k, idx_k = jax.lax.top_k(scores, K)
            gates_k = gates_k / jnp.sum(gates_k, axis=-1, keepdims=True)
            masks = jax.nn.one_hot(idx_k, E, dtype=jnp.int32)
            m = jnp.transpose(masks, (1, 0, 2)).reshape(K * T, E)
            locs_full = jnp.cumsum(m, axis=0) - 1
            loc = jnp.sum(locs_full * m, axis=-1)
            loc = loc.reshape(K, T).T
            valid = (loc < cap).astype(xt.dtype)
            loc_c = jnp.clip(loc, 0, cap - 1)
            contrib = (xt[:, None, :] * valid[:, :, None]).reshape(T * K, Dd)
            disp = jnp.zeros((E, cap, Dd), xt.dtype)
            disp = disp.at[idx_k.reshape(-1), loc_c.reshape(-1)].add(contrib)
            h = jax.nn.relu(jnp.einsum('ecd,edh->ech', disp, w1) + b1[:, None, :])
            out = jnp.einsum('ech,ehd->ecd', h, w2) + b2[:, None, :]
            gathered = out[idx_k, loc_c]
            y = jnp.einsum('tk,tkd->td', gates_k * valid, gathered)
            return y.reshape(Bb, Ss, Dd)
        return _moe_forward(x, wg, w1, b1, w2, b2)
    x = L0_attn_x
    x = x + 0.5 * _L0_ffn_ref(_layernorm(x, axis=-1), L0_ffn_gate_w, L0_ffn_w1, L0_ffn_b1, L0_ffn_w2, L0_ffn_b2)
    x = x + _L0_attn_ref(_layernorm(x, axis=-1), L0_attn_qkv_w, L0_attn_qkv_b, L0_attn_proj_w, L0_attn_proj_b, L0_attn_rel_pos_emb)
    x = x + 0.5 * _L0_ffn_ref(_layernorm(x, axis=-1), L0_ffn_gate_w, L0_ffn_w1, L0_ffn_b1, L0_ffn_w2, L0_ffn_b2)
    x = x + 0.5 * _L1_ffn_ref(_layernorm(x, axis=-1), L1_ffn_gate_weight, L1_ffn_w_gate, L1_ffn_w_up, L1_ffn_w_down, L1_ffn_ws_gate, L1_ffn_ws_up, L1_ffn_ws_down)
    x = x + _L1_attn_ref(_layernorm(x, axis=-1), L1_attn_Wq1, L1_attn_Wk1, L1_attn_Wq2, L1_attn_Wk2, L1_attn_Wv, L1_attn_Wo, L1_attn_bo)
    x = x + 0.5 * _L1_ffn_ref(_layernorm(x, axis=-1), L1_ffn_gate_weight, L1_ffn_w_gate, L1_ffn_w_up, L1_ffn_w_down, L1_ffn_ws_gate, L1_ffn_ws_up, L1_ffn_ws_down)
    x = x + 0.5 * _L2_ffn_ref(_layernorm(x, axis=-1), L2_ffn_w_gate, L2_ffn_w_in, L2_ffn_w_out)
    x = x + _L2_attn_ref(_layernorm(x, axis=-1), L2_attn_W_in, L2_attn_b_in, L2_attn_W_out, L2_attn_b_out)
    x = x + 0.5 * _L2_ffn_ref(_layernorm(x, axis=-1), L2_ffn_w_gate, L2_ffn_w_in, L2_ffn_w_out)
    x = x + 0.5 * _L3_ffn_ref(_layernorm(x, axis=-1), L3_ffn_wg, L3_ffn_w1, L3_ffn_b1, L3_ffn_w2, L3_ffn_b2)
    x = x + _L3_attn_ref(_layernorm(x, axis=-1), L3_attn_ln_gamma, L3_attn_ln_beta, L3_attn_W_qkv, L3_attn_b_qkv, L3_attn_W_out, L3_attn_b_out)
    x = x + 0.5 * _L3_ffn_ref(_layernorm(x, axis=-1), L3_ffn_wg, L3_ffn_w1, L3_ffn_b1, L3_ffn_w2, L3_ffn_b2)
    return x

_drawn_inputs = setup_inputs


def setup_inputs(seed=0):
    import zlib

    import numpy as np

    out = dict(_drawn_inputs(seed))
    spreads = {'L0_ffn_b1': (0.0, 0.1),
     'L0_ffn_b2': (0.0, 0.1),
     'L1_attn_bo': (0.0, 0.1),
     'L2_attn_b_in': (0.0, 0.1),
     'L2_attn_b_out': (0.0, 0.1),
     'L3_attn_ln_gamma': (1.0, 0.6),
     'L3_attn_ln_beta': (0.0, 0.1),
     'L3_attn_b_qkv': (0.0, 0.1),
     'L3_attn_b_out': (0.0, 0.1),
     'L3_ffn_b1': (0.0, 0.1),
     'L3_ffn_b2': (0.0, 0.1)}
    factors = {'L0_attn_rel_pos_emb': 23.388,
     'L1_ffn_gate_weight': 3.191,
     'L1_ffn_w_gate': 2.797,
     'L1_ffn_w_up': 2.833,
     'L1_ffn_w_down': 2.984,
     'L1_ffn_ws_gate': 3.136,
     'L1_ffn_ws_up': 3.091,
     'L1_ffn_ws_down': 2.904,
     'L2_ffn_w_gate': 8.0,
     'L2_ffn_w_in': 8.0,
     'L2_ffn_w_out': 8.0}
    for name, (base, spread) in spreads.items():
        noise = np.random.default_rng([zlib.crc32(name.encode()), seed]).standard_normal(out[name].shape)
        drawn = base * np.exp(spread * noise) if base else spread * noise
        out[name] = jnp.asarray(drawn.astype(out[name].dtype))
    for name, factor in factors.items():
        out[name] = (out[name] * factor).astype(out[name].dtype)
    return out
```

```python
from contextlib import ExitStack

import concourse.bass as bass
from concourse import mybir
from concourse.bass import IndirectOffsetOnAxis

F32 = mybir.dt.float32
BF16 = mybir.dt.bfloat16
U32 = mybir.dt.uint32
ALU = mybir.AluOpType
ACT = mybir.ActivationFunctionType
AX = mybir.AxisListType.X

P = 128
B, T, D = 4, 512, 128
TOKENS = B * T
TILES = TOKENS // P
GROUP = T // P
E = 8
HID = 512
CH = HID // P
HEADS, HD = 16, 8
EPS = 1e-5
CAP0 = -(-5 * TOKENS // (4 * E))
CAP3 = 2 * -(-TOKENS // E)
OUT_OF_BOUNDS = 1.0e6
MASKED = -1.0e30


def semaphores(g, name):
    def sem(n):
        g.spent.append(g.nc.alloc_semaphore(f"{name}_{n}"))
        return g.spent[-1]

    return sem


def clear_semaphores(g):
    g.nc.clear_and_free_semaphores(g.spent)
    g.nc.all_engine_barrier(sem_only=True)
    g.spent.clear()


class LayerNormSems:
    def __init__(self, sem, twice=False):
        self.stats, self.moments, self.var_eps = sem("ln_stats"), sem("ln_moments"), sem("ln_var_eps")
        self.rstd, self.xn = sem("ln_rstd"), sem("ln_rows")
        self.xnt_psum, self.xnt = sem("ln_rows_transposed"), sem("ln_columns")
        self.twice = twice
        if twice:
            self.outer = LayerNormSems(lambda n: sem("outer_" + n))
            self.summed = sem("ln_summed")


def ln_stats(g, v, s, b, src=None):
    nc = g.nc
    src = g.x if src is None else src
    tiles = range(GROUP * b, GROUP * (b + 1))
    for i in tiles:
        nc.vector.bn_stats(g.stats[:, i, :], src[:, i, 0:D]).then_inc(s.stats, 1)
    v.wait_ge(s.stats, GROUP * (b + 1))
    for i in tiles:
        nc.vector.bn_aggr(g.moments[:, i, :], g.stats[:, i, :]).then_inc(s.moments, 1)
    v.wait_ge(s.moments, GROUP * (b + 1))
    nc.vector.tensor_scalar(g.var_eps[:, GROUP * b:GROUP * (b + 1)],
                            g.moments[:, GROUP * b:GROUP * (b + 1), 1],
                            EPS, None, ALU.add).then_inc(s.var_eps, 1)


def ln_rstd(g, pool, s, b):
    cols = slice(GROUP * b, GROUP * (b + 1))
    pool.wait_ge(s.var_eps, b + 1)
    g.nc.gpsimd.tensor_tensor(g.rstd[:, cols], g.var_eps[:, cols], g.neg_half[:, cols],
                              ALU.pow).then_inc(s.rstd, 1)


def ln_rows(g, v, s, b, src=None):
    src = g.x if src is None else src
    v.wait_ge(s.rstd, b + 1)
    for i in range(GROUP * b, GROUP * (b + 1)):
        g.nc.vector.tensor_scalar(g.xn[:, i, 0:D], src[:, i, 0:D], g.moments[:, i, 0:1],
                                  g.rstd[:, i:i + 1], ALU.subtract, ALU.mult).then_inc(s.xn, 1)


def ln_outer(g, v, s, b):
    ln_rows(g, v, s.outer, b)
    v.wait_ge(s.outer.xn, GROUP * (b + 1))
    tiles = slice(GROUP * b, GROUP * (b + 1))
    g.nc.vector.tensor_tensor(g.x[:, tiles, :], g.x[:, tiles, :], g.xn[:, tiles, 0:D], ALU.add).then_inc(s.summed, 1)
    ln_stats(g, v, s, b, src=g.xn)


def ln_inner(g, v, s, b):
    v.wait_ge(s.summed, b + 1)
    ln_rows(g, v, s, b, src=g.xn)


def ln_transpose(g, pe, s, b, bank, one_bank=False):
    pe.wait_ge(s.xn, GROUP * (b + 1))
    if one_bank and b >= 1:
        pe.wait_ge(s.xnt, b)
    for j in range(GROUP):
        mm = g.nc.tensor.transpose(bank[:, j * P:(j + 1) * P], g.xn[:, GROUP * b + j, 0:D], g.ident[:])
    mm.then_inc(s.xnt_psum, 1)


def ln_columns(g, act, s, b, bank):
    act.wait_ge(s.xnt_psum, b + 1)
    dst = g.xnt[:, b * T:(b + 1) * T]
    if s.twice:
        g.nc.scalar.activation(dst, bank[:], ACT.Identity, bias=g.gamma_beta[:, 1:2], scale=g.gamma_beta[:, 0:1]
                               ).then_inc(s.xnt, 1)
    else:
        g.nc.scalar.copy(dst, bank[:]).then_inc(s.xnt, 1)


def setup(g, beside):
    nc = g.nc
    with ExitStack() as ctx:
        sem = semaphores(g, "setup")
        loaded = [sem(f"x_loaded{b}") for b in range(B)]
        small_loaded, made, ident_made, masked = sem("small_loaded"), sem("made"), sem("ident_made"), sem("masks")
        ln = LayerNormSems(sem)
        block = ctx.enter_context(nc.Block(no_gpsimd_drain=True))

        @block.sync
        def _(sp):
            for b in range(B):
                sp.dma_start(g.x[:, GROUP * b:GROUP * (b + 1), :],
                             g.a["x"][b * T:(b + 1) * T, :].rearrange("(i p) d -> p i d", p=P)).then_inc(loaded[b], 16)
            beside.load(sp)
            for k, n in enumerate(("l0_gate", "l1_gate", "l2_gate", "l3_gate")):
                sp.dma_start(g.gates[:, k, :], g.a[n]).then_inc(small_loaded, 16)
            sp.dma_start(g.gamma_beta[:], g.a["l3_gamma_beta"]).then_inc(small_loaded, 16)
            sp.wait_ge(made, 2)
            for n, rows in enumerate(g.dispatched):
                of_partition = rows.shape[0] // P
                sp.dma_start(rows.rearrange("(p j) d -> p j d", p=P),
                             g.untaken[:, None, :].to_broadcast([P, of_partition, D + 1])).then_inc(g.untaken_written[n], 16)
            of_partition = g.returned.shape[0] // P
            sp.dma_start(g.returned.rearrange("(p j) d -> p j d", p=P),
                         g.untaken[:, None, 0:D].to_broadcast([P, of_partition, D])).then_inc(g.returned_zeroed, 16)
            sp.wait_ge(small_loaded, 16 * 5)

        @block.tensor
        def _(pe):
            pe.wait_ge(ident_made, 2)
            for b in range(B):
                ln_transpose(g, pe, ln, b, g.bank[b])
            beside.turn(pe, g.bank[B])

        @block.scalar
        def _(act):
            for b in range(B):
                ln_columns(g, act, ln, b, g.bank[b])
            beside.copy_lines(act, g.bank[B])
            beside.spread_lines(act)

        @block.vector
        def _(v):
            nc.vector.memset(g.neg_half[:], -0.5)
            nc.vector.memset(g.untaken[:], 0.0).then_inc(made, 1)
            v.wait_ge(made, 1)
            nc.vector.memset(g.untaken[:, D:D + 1], OUT_OF_BOUNDS).then_inc(made, 1)
            for e in range(E):
                nc.vector.memset(g.rev[:, :, e], float(E - e))
            nc.vector.memset(g.scan_keep[:], 1.0).then_inc(made, 1)
            nc.vector.memset(g.scan_keep1[:], 1.0).then_inc(made, 1)
            v.wait_ge(made, 4)
            nc.vector.memset(g.scan_keep[:, :, 0:1], 0.0)
            nc.vector.memset(g.scan_keep1[:, :, 0:1], 0.0)
            for b in range(B):
                v.wait_ge(loaded[b], 16)
                ln_stats(g, v, ln, b)
                if b >= 1:
                    ln_rows(g, v, ln, b - 1)
            ln_rows(g, v, ln, B - 1)
            beside.sum_heads(v)

        @block.gpsimd
        def _(pool):
            n = [0]

            def after(ins):
                n[0] += 1
                ins.then_inc(masked, 1)
                pool.wait_ge(masked, n[0])

            nc.gpsimd.memset(g.ident[:], 0.0).then_inc(ident_made, 1)
            pool.wait_ge(ident_made, 1)
            nc.gpsimd.affine_select(out=g.ident[:], in_=g.ident[:], compare_op=ALU.not_equal, fill=1.0,
                                    base=0, pattern=[[-1, P]], channel_multiplier=1).then_inc(ident_made, 1)
            pool.wait_ge(ident_made, 2)
            for b in range(B):
                ln_rstd(g, pool, ln, b)
            after(nc.gpsimd.tensor_copy(g.identb[:], g.ident[:]))
            after(nc.gpsimd.memset(g.onesb[:], 1.0))
            after(nc.gpsimd.affine_select(out=g.beforeb[:], in_=g.onesb[:], compare_op=ALU.is_ge, fill=0.0,
                                          base=-1, pattern=[[1, P]], channel_multiplier=-1))
            after(nc.gpsimd.iota(g.token_i[:], pattern=[[P, 2 * TILES]], base=0, channel_multiplier=1))
            after(nc.gpsimd.tensor_copy(g.token[:], g.token_i[:]))
            for t, base in ((g.head_selector, MAX_AT), (g.head_selector1, MAX_AT1)):
                after(nc.gpsimd.memset(t[:], 0.0))
                for part in range(PARTS):
                    after(nc.gpsimd.affine_select(out=t[:], in_=t[:], compare_op=ALU.not_equal, fill=1.0,
                                                  base=-(base + part * GH), pattern=[[-1, GH]], channel_multiplier=1))
            after(nc.gpsimd.memset(g.expert_selector[:], 0.0))
            chunks = g.expert_selector[:].rearrange("p c (h r) -> p c h r", h=2)
            for part in range(PARTS):
                after(nc.gpsimd.affine_select(out=chunks, in_=chunks, compare_op=ALU.not_equal, fill=1.0,
                                              base=-part * E, pattern=[[-2, E // 2], [-1, 2], [0, P // 2]], channel_multiplier=1))
            after(nc.gpsimd.memset(g.mask_kq[:], 0.0))
            after(nc.gpsimd.affine_select(out=g.mask_kq[:], in_=g.mask_kq[:], compare_op=ALU.is_ge, fill=MASKED,
                                          base=0, pattern=[[1, P]], channel_multiplier=-1))
            after(nc.gpsimd.memset(g.mask_qk[:], 0.0))
            after(nc.gpsimd.affine_select(out=g.mask_qk[:, T - P:T], in_=g.mask_qk[:, T - P:T],
                                          compare_op=ALU.is_ge, fill=MASKED,
                                          base=0, pattern=[[-1, P]], channel_multiplier=1))


def first_max(g, after, scores, best, work, onehot):
    v = g.nc.vector
    wide = [P, TILES, E]
    after(v.tensor_reduce(best, scores, axis=AX, op=ALU.max))
    after(v.tensor_tensor(work, scores, best[:, :, None].to_broadcast(wide), ALU.is_equal))
    after(v.tensor_tensor(work, work, g.rev[:, 0:TILES, :], ALU.mult))
    after(v.tensor_reduce(g.tie[:], work, axis=AX, op=ALU.max))
    after(v.tensor_tensor(onehot, work, g.tie[:, :, None].to_broadcast(wide), ALU.is_equal))


def moe_capacity(g, name, n, choices, cap, gate_sb, w1, b1, w2, b2, last=False, twice=False, beside=None):
    nc = g.nc
    slots = E * cap
    full, rest = cap // P, cap % P
    sizes = [P] * full + [rest] * (rest > 0)
    nt = len(sizes)
    picks = choices * TILES
    tile_loads = 1 + (rest > 0)
    dispatched = g.dispatched[n]
    scan_keep = g.scan_keep if choices == 2 else g.scan_keep1
    with ExitStack() as ctx:
        sem = semaphores(g, name)
        sb = lambda n, shape, dt=F32: ctx.enter_context(nc.sbuf_tensor(f"{name}_{n}", shape, dt))
        ln = None if last else LayerNormSems(sem, twice)
        small_loaded = sem("biases_loaded")
        w_loaded = [sem("w_loaded0"), sem("w_loaded1")]
        d_loaded = [sem("slots_loaded0"), sem("slots_loaded1")]
        logits_done, ranks_done = sem("logits_done"), sem("ranks_done")
        route, chosen, exp_in, exp_out = sem("route"), sem("chosen"), sem("exp_in"), sem("exp_out")
        slots_ready = sem("slots_ready")
        scattered = sem("scattered")
        dt_psum, dt_ready = sem("slots_transposed"), sem("slot_columns")
        h_psum, h_ready = sem("hidden_psum"), sem("hidden")
        o_psum, o_ready = sem("out_psum"), sem("out_rows")
        stored = [sem("stored0"), sem("stored1")]
        numbered, numbers_ready, added = sem("rows_numbered"), sem("slot_tokens"), sem("added")
        returned = [sem(f"rows_returned{b}") for b in range(B)]

        xn2 = sb("second_rows", [P, TILES, D + 1]) if choices == 2 else None
        b1_sb = sb("b1", [P, E * CH])
        b2_sb = sb("b2", [P, E, D])
        w1_sb = [sb(f"w1_{i}", [P, HID]) for i in range(2)]
        w2_sb = [sb(f"w2_{i}", [P, CH, D]) for i in range(2)]
        d_sb = [sb(f"slots_{i}", [P, nt, D + 1]) for i in range(2)]
        dt_sb = [sb(f"slot_columns_{i}", [P, cap]) for i in range(2)]
        h_sb = [sb(f"hidden_{i}", [P, CH, cap]) for i in range(2)]
        o_sb = [sb(f"out_{i}", [P, nt, D]) for i in range(2)]
        slot_token = [sb(f"slot_tokens_{i}", [P, nt], U32) for i in range(2)]
        logits = sb("logits", [P, TILES, E])
        rest_logits = sb("rest_logits", [P, TILES, E])
        work = sb("work", [P, TILES, E])
        best = sb("best", [P, choices, TILES])
        onehot = sb("onehot", [P, choices, TILES, E])
        onehotb = sb("onehotb", [P, picks, E], BF16)
        expd = sb("expd", [P, TILES, E])
        gates = sb("gates", [P, choices, TILES])
        denom = sb("denom", [P, TILES])
        totals = sb("totals", [P, E, picks])
        running = sb("running", [P, E, picks])
        offset = sb("offset", [P, E, picks])
        rank_all = sb("rank_all", [P, picks, E])
        rank = sb("rank", [P, picks])
        base = sb("base", [P, picks])
        keep = sb("keep", [P, picks])
        slot = sb("slot", [P, picks])
        scatter_f = sb("scatter_f", [P, picks])
        kept_slot = sb("kept_slot", [P, picks])
        scatter_i = sb("scatter_i", [P, picks], U32)
        weight = sb("weight", [P, picks])
        back = sb("back", [P, picks, D])

        xnt_bank = [g.bank[0], g.bank[1]]
        logits_bank, rank_bank, total_bank = g.bank[2], g.bank[3], g.bank[4]
        h_bank = g.bank[2:6]
        o_bank = g.bank[6:8]
        flat = lambda t: t[:].rearrange("p k t e -> p (k t) e")
        block = ctx.enter_context(nc.Block(no_gpsimd_drain=True))

        @block.sync
        def _(sp):
            sp.dma_start(b1_sb[:], b1).then_inc(small_loaded, 16)
            sp.dma_start(b2_sb[:], b2.rearrange("e d -> (e d)").partition_broadcast(P)).then_inc(small_loaded, 16)

            def load_weights(e, i):
                sp.dma_start(w1_sb[i][:], w1[bass.ds(e * P, P), :]).then_inc(w_loaded[i], 16)
                sp.dma_start(w2_sb[i][:], w2[bass.ds(e * HID, HID), :].rearrange("(c p) d -> p c d", p=P)
                             ).then_inc(w_loaded[i], 16)

            def load_slots(e, i):
                sp.dma_start(d_sb[i][:, 0:full, :],
                             dispatched[bass.ds(e * cap, full * P), :].rearrange("(t p) d -> p t d", p=P)
                             ).then_inc(d_loaded[i], 16)
                if rest:
                    sp.dma_start(d_sb[i][0:rest, full, :], dispatched[bass.ds(e * cap + full * P, rest), :]
                                 ).then_inc(d_loaded[i], 16)

            for i in range(2):
                load_weights(i, i)
            sp.wait_ge(scattered, 16 * picks)
            for i in range(2):
                load_slots(i, i)
            with sp.Fori(0, E // 2 - 1) as k:
                for i in range(2):
                    sp.wait_ge(dt_psum, 2 * k + i + 1)
                    sp.wait_ge(numbers_ready, 2 * k + i + 1)
                    load_slots(2 * k + i + 2, i)
                    sp.wait_ge(o_psum, 2 * k + i + 1)
                    load_weights(2 * k + i + 2, i)
            for i in range(2):
                sp.wait_ge(stored[i], 16 * nt * (E // 2))
            for b in range(B):
                for c in range(choices):
                    at = c * TILES + GROUP * b
                    sp.dma_start(back[:, at:at + GROUP, :],
                                 g.returned[c * TOKENS + b * T:c * TOKENS + (b + 1) * T, :].rearrange("(j p) d -> p j d", p=P)
                                 ).then_inc(returned[b], 16)

        @block.tensor
        def _(pe):
            for i in range(TILES):
                mm = nc.tensor.matmul(logits_bank[:, i * E:(i + 1) * E], g.xnt[:, i * P:(i + 1) * P],
                                      gate_sb, start=True, stop=True)
            mm.then_inc(logits_done, 1)
            pe.wait_ge(chosen, 1)
            hot = onehotb[:].rearrange("p k e -> p (k e)")
            nc.tensor.matmul(rank_bank[:, 0:picks * E], g.beforeb[:], hot, start=True, stop=True)
            nc.tensor.matmul(total_bank[:, 0:picks * E], g.onesb[:], hot, start=True, stop=True
                             ).then_inc(ranks_done, 1)
            pe.wait_ge(slots_ready, 1)

            def turn_slots(e, i, nth):
                pe.wait_ge(d_loaded[i], 16 * tile_loads * nth)
                for t, n in enumerate(sizes):
                    mm = nc.tensor.transpose(xnt_bank[i][:, t * P:t * P + n], d_sb[i][0:n, t, 0:D], g.ident[0:n, 0:n])
                mm.then_inc(dt_psum, 1)

            def hidden(e, i, nth):
                pe.wait_ge(dt_ready, e + 1)
                pe.wait_ge(w_loaded[i], 32 * nth)
                for c in range(CH):
                    nc.tensor.matmul(h_bank[c][:, 0:cap], w1_sb[i][:, c * P:(c + 1) * P], dt_sb[i][:],
                                     start=True, stop=True).then_inc(h_psum, 1)

            def output(e, i):
                pe.wait_ge(h_ready, CH * (e + 1))
                for t, n in enumerate(sizes):
                    for c in range(CH):
                        mm = nc.tensor.matmul(o_bank[i][0:n, t * D:(t + 1) * D],
                                              h_sb[i][:, c, t * P:t * P + n], w2_sb[i][:, c, :],
                                              start=(c == 0), stop=(c == CH - 1))
                mm.then_inc(o_psum, 1)

            turn_slots(0, 0, 1)
            with pe.Fori(0, E // 2 - 1) as k:
                for i in range(2):
                    hidden(2 * k + i, i, k + 1)
                    turn_slots(2 * k + i + 1, 1 - i, k + 1 + i)
                    pe.wait_ge(o_ready, 2 * k + i)
                    output(2 * k + i, i)
            for e in (E - 2, E - 1):
                hidden(e, e % 2, E // 2)
                if e == E - 2:
                    turn_slots(E - 1, 1, E // 2)
                pe.wait_ge(o_ready, e)
                output(e, e % 2)
            if not last:
                for b in range(B):
                    ln_transpose(g, pe, ln, b, g.bank[2 + b])

        @block.scalar
        def _(act):
            nc.scalar.copy(g.xn[:, :, D], g.token[:, 0:TILES]).then_inc(numbered, 1)
            if choices == 2:
                nc.scalar.copy(xn2[:, :, 0:D], g.xn[:, :, 0:D])
                nc.scalar.copy(xn2[:, :, D], g.token[:, TILES:2 * TILES]).then_inc(numbered, 1)
            act.wait_ge(exp_in, 1)
            nc.scalar.activation(expd[:] if choices == 1 else expd[:, :, 0], expd[:] if choices == 1 else expd[:, :, 0],
                                 ACT.Exp).then_inc(exp_out, 1)
            if beside:
                beside.load_tiles(act)
            act.wait_ge(small_loaded, 32)

            def copy_columns(e, i):
                act.wait_ge(dt_psum, e + 1)
                nc.scalar.copy(dt_sb[i][:], xnt_bank[i][:, 0:cap]).then_inc(dt_ready, 1)

            def hidden(e, i):
                for c in range(CH):
                    act.wait_ge(h_psum, CH * e + c + 1)
                    nc.scalar.activation(h_sb[i][:, c, :], h_bank[c][:, 0:cap], ACT.Relu,
                                         bias=b1_sb[:, bass.ds(e * CH + c, 1)]).then_inc(h_ready, 1)

            copy_columns(0, 0)
            with act.Fori(0, E // 2 - 1) as k:
                for i in range(2):
                    hidden(2 * k + i, i)
                    copy_columns(2 * k + i + 1, 1 - i)
            hidden(E - 2, 0)
            copy_columns(E - 1, 1)
            hidden(E - 1, 1)
            if not last:
                for b in range(B):
                    ln_columns(g, act, ln, b, g.bank[2 + b])

        @block.vector
        def _(v):
            n = [0]

            def after(ins):
                n[0] += 1
                ins.then_inc(route, 1)
                v.wait_ge(route, n[0])

            v.wait_ge(logits_done, 1)
            after(nc.vector.tensor_copy(logits[:], logits_bank[:, 0:TILES * E].rearrange("p (t e) -> p t e", e=E)))
            first_max(g, after, logits[:], best[:, 0, :], work[:], onehot[:, 0, :, :])
            if choices == 2:
                after(nc.vector.scalar_tensor_tensor(rest_logits[:], onehot[:, 0, :, :], MASKED, logits[:],
                                                     ALU.mult, ALU.add))
                first_max(g, after, rest_logits[:], best[:, 1, :], work[:], onehot[:, 1, :, :])
            nc.vector.tensor_copy(onehotb[:], flat(onehot)).then_inc(chosen, 1)
            v.wait_ge(ranks_done, 1)
            by_expert = lambda t: t[:].rearrange("p e k -> p k e")
            after(nc.vector.tensor_copy(by_expert(totals),
                                        total_bank[:, 0:picks * E].rearrange("p (k e) -> p k e", e=E)))
            after(nc.vector.tensor_tensor_scan(running[:].rearrange("p e k -> p (e k)"),
                                               scan_keep[:].rearrange("p e k -> p (e k)"),
                                               totals[:].rearrange("p e k -> p (e k)"), 0.0, ALU.mult, ALU.add))
            after(nc.vector.tensor_tensor(offset[:], running[:], totals[:], ALU.subtract))
            after(nc.vector.tensor_tensor(rank_all[:], rank_bank[:, 0:picks * E].rearrange("p (k e) -> p k e", e=E),
                                          by_expert(offset), ALU.add))
            after(nc.vector.tensor_tensor(rank_all[:], rank_all[:], flat(onehot), ALU.mult))
            after(nc.vector.tensor_reduce(rank[:], rank_all[:], axis=AX, op=ALU.add))
            after(nc.vector.tensor_tensor(rank_all[:], flat(onehot), g.rev[:, 0:picks, :], ALU.mult))
            after(nc.vector.tensor_reduce(base[:], rank_all[:], axis=AX, op=ALU.add))
            after(nc.vector.tensor_scalar(base[:], base[:], -float(cap), float(E * cap), ALU.mult, ALU.add))
            after(nc.vector.tensor_tensor(slot[:], base[:], rank[:], ALU.add))
            after(nc.vector.tensor_scalar(keep[:], rank[:], float(cap), None, ALU.is_lt))
            after(nc.vector.tensor_tensor(kept_slot[:], slot[:], keep[:], ALU.mult))
            after(nc.vector.tensor_scalar(scatter_f[:], keep[:], -OUT_OF_BOUNDS, OUT_OF_BOUNDS, ALU.mult, ALU.add))
            after(nc.vector.tensor_tensor(scatter_f[:], scatter_f[:], kept_slot[:], ALU.add))
            nc.vector.tensor_copy(scatter_i[:], scatter_f[:]).then_inc(slots_ready, 1)
            if choices == 1:
                nc.vector.tensor_tensor(expd[:], logits[:], best[:, 0, :, None].to_broadcast([P, TILES, E]),
                                        ALU.subtract).then_inc(exp_in, 1)
                v.wait_ge(exp_out, 1)
                after(nc.vector.tensor_reduce(denom[:], expd[:], axis=AX, op=ALU.add))
                after(nc.vector.reciprocal(gates[:, 0, :], denom[:]))
            else:
                nc.vector.tensor_tensor(expd[:, :, 0], best[:, 1, :], best[:, 0, :], ALU.subtract).then_inc(exp_in, 1)
                v.wait_ge(exp_out, 1)
                after(nc.vector.tensor_scalar(denom[:], expd[:, :, 0], 1.0, None, ALU.add))
                after(nc.vector.reciprocal(gates[:, 0, :], denom[:]))
                after(nc.vector.tensor_tensor(gates[:, 1, :], expd[:, :, 0], gates[:, 0, :], ALU.mult))
            after(nc.vector.scalar_tensor_tensor(weight[:], gates[:].rearrange("p k t -> p (k t)"), 0.5, keep[:],
                                                 ALU.mult, ALU.mult))
            if beside:
                beside.split(v)
            v.wait_ge(small_loaded, 32)
            with v.Fori(0, E // 2) as k:
                for i in range(2):
                    v.wait_ge(stored[i], 16 * nt * k)
                    v.wait_ge(d_loaded[i], 16 * tile_loads * (k + 1))
                    if rest:
                        nc.vector.tensor_copy(slot_token[i][0:rest, full:nt], d_sb[i][0:rest, full:nt, D])
                    nc.vector.tensor_copy(slot_token[i][:, 0:full], d_sb[i][:, 0:full, D]).then_inc(numbers_ready, 1)
                    v.wait_ge(o_psum, 2 * k + i + 1)
                    bias = b2_sb[:, bass.ds(2 * k + i, 1), :]
                    if rest:
                        nc.vector.tensor_tensor(o_sb[i][0:rest, full, :], o_bank[i][0:rest, full * D:(full + 1) * D],
                                                b2_sb[0:rest, bass.ds(2 * k + i, 1), :], ALU.add)
                    nc.vector.tensor_tensor(o_sb[i][:, 0:full, :],
                                            o_bank[i][:, 0:full * D].rearrange("p (t d) -> p t d", d=D),
                                            bias.to_broadcast([P, full, D]), ALU.add).then_inc(o_ready, 1)

            def add_rows(b):
                v.wait_ge(returned[b], 16 * choices)
                for c in range(choices):
                    if c:
                        v.wait_ge(added, (choices * b + c) * GROUP)
                    for j in range(GROUP * b, GROUP * (b + 1)):
                        k = c * TILES + j
                        nc.vector.scalar_tensor_tensor(g.x[:, j, :], back[:, k, :], weight[:, k:k + 1],
                                                       g.x[:, j, :], ALU.mult, ALU.add).then_inc(added, 1)

            for b in range(B + 2):
                if b < B:
                    add_rows(b)
                    if not last:
                        v.wait_ge(added, choices * GROUP * (b + 1))
                        ln_stats(g, v, ln.outer if twice else ln, b)
                if twice:
                    if 0 <= b - 1 < B:
                        ln_outer(g, v, ln, b - 1)
                    if 0 <= b - 2 < B:
                        ln_inner(g, v, ln, b - 2)
                elif not last and 0 <= b - 1 < B:
                    ln_rows(g, v, ln, b - 1)

        @block.gpsimd
        def _(pool):
            pool.wait_ge(g.untaken_written[n], 16)
            pool.wait_ge(numbered, choices)
            pool.wait_ge(slots_ready, 1)
            for k in range(picks):
                nc.gpsimd.indirect_dma_start(
                    out=dispatched[0:slots, :], out_offset=IndirectOffsetOnAxis(ap=scatter_i[:, k:k + 1], axis=0),
                    in_=(g.xn, xn2)[k // TILES][:, k % TILES, :], in_offset=None,
                    bounds_check=slots - 1, oob_is_err=False).then_inc(scattered, 16)
            pool.wait_ge(g.returned_zeroed, 16)
            for e in range(E):
                pool.wait_ge(o_ready, e + 1)
                for t, m in enumerate(sizes):
                    nc.gpsimd.indirect_dma_start(
                        out=g.returned[0:choices * TOKENS, :],
                        out_offset=IndirectOffsetOnAxis(ap=slot_token[e % 2][0:m, t:t + 1], axis=0),
                        in_=o_sb[e % 2][0:m, t, :], in_offset=None,
                        bounds_check=choices * TOKENS - 1, oob_is_err=False).then_inc(stored[e % 2], 16)
            if not last:
                for b in range(B + 1):
                    if b < B:
                        ln_rstd(g, pool, ln.outer if twice else ln, b)
                    if twice and b >= 1:
                        ln_rstd(g, pool, ln, b - 1)


def ffn1(g, name, beside=None):
    nc, a = g.nc, g.a
    routed, chunks = 4, 5
    wide = chunks * P
    with ExitStack() as ctx:
        sem = semaphores(g, name)
        sb = lambda n, shape, dt=F32: ctx.enter_context(nc.sbuf_tensor(f"{name}_{n}", shape, dt))
        ln = LayerNormSems(sem)
        loaded = sem("weights_loaded")
        logits_done, scores_done, route = sem("logits_done"), sem("scores_done"), sem("route")
        weights_ready, turned, columns_ready = sem("combine_ready"), sem("combine_turned"), sem("combine_columns")
        g_psum, u_psum, cb_psum, y_psum = sem("gate_psum"), sem("up_psum"), sem("combine_psum"), sem("y_psum")
        silu_done, gated, hidden, summed = sem("silu_done"), sem("gated"), sem("hidden"), sem("summed")

        xnt, gate_sb = g.xnt, g.gates[:, 1, :]
        wg_sb, wu_sb = sb("wg", [P, wide]), sb("wu", [P, wide])
        wd_sb = sb("wd", [P, chunks, D])
        scores, others, work = (sb(n, [P, TILES, E]) for n in ("scores", "others", "work"))
        best = sb("best", [P, 2, TILES])
        onehot = sb("onehot", [P, 2, TILES, E])
        denom = sb("denom", [P, TILES])
        combine = sb("combine", [P, TILES, E])
        combine_parts = sb("combine_parts", [P, TILES, P], BF16)
        combine_t = sb("combine_t", [P, TOKENS], BF16)
        silu = sb("silu", [P, 2, T])
        prod = sb("prod", [P, 2, T])
        hid = sb("hid", [P, 2, chunks, T])

        xnt_bank, turn_bank, logits_bank = g.bank[0], g.bank[1], g.bank[2]
        g_bank, u_bank = g.bank[2:4], g.bank[4:6]
        cb_bank, y_bank = g.bank[6], g.bank[7]
        units = [(b, c) for b in range(B) for c in range(chunks)]
        block = ctx.enter_context(nc.Block(no_gpsimd_drain=True))

        @block.sync
        def _(sp):
            sp.dma_start(wg_sb[:], a["l1_gate_w"]).then_inc(loaded, 16)
            sp.dma_start(wu_sb[:], a["l1_up_w"]).then_inc(loaded, 16)
            sp.dma_start(wd_sb[:], a["l1_down_w"].rearrange("(c p) d -> p c d", p=P)).then_inc(loaded, 16)
            if beside:
                beside.load(sp)

        @block.tensor
        def _(pe):
            for i in range(TILES):
                mm = nc.tensor.matmul(logits_bank[:, i * E:(i + 1) * E], xnt[:, i * P:(i + 1) * P],
                                      gate_sb, start=True, stop=True)
            mm.then_inc(logits_done, 1)
            if beside:
                beside.multiply(pe, g.bank[3:6:2])
            pe.wait_ge(loaded, 48)
            pe.wait_ge(scores_done, 1)

            def down(b):
                pe.wait_ge(hidden, chunks * (b + 1))
                if b >= 1:
                    pe.wait_ge(summed, b)
                for i in range(GROUP):
                    for c in range(chunks):
                        mm = nc.tensor.matmul(y_bank[:, i * D:(i + 1) * D], hid[:, b % 2, c, i * P:(i + 1) * P],
                                              wd_sb[:, c, :], start=(c == 0), stop=(c == chunks - 1))
                mm.then_inc(y_psum, 1)

            for k, (b, c) in enumerate(units):
                columns = xnt[:, b * T:(b + 1) * T]
                if beside and k == 1:
                    pe.wait_ge(beside.copied, 2)
                if k >= 2:
                    pe.wait_ge(silu_done, k - 1)
                    pe.wait_ge(gated, k - 1)
                nc.tensor.matmul(g_bank[k % 2][:], wg_sb[:, c * P:(c + 1) * P], columns,
                                 start=True, stop=True).then_inc(g_psum, 1)
                nc.tensor.matmul(u_bank[k % 2][:], wu_sb[:, c * P:(c + 1) * P], columns,
                                 start=True, stop=True).then_inc(u_psum, 1)
                if k == 0:
                    pe.wait_ge(weights_ready, 2)
                    for i in range(TILES):
                        mm = nc.tensor.transpose(turn_bank[:].bitcast(BF16)[:, (i % 8) * P:(i % 8 + 1) * P],
                                                 combine_parts[:, i, :], g.identb[:])
                        if i % 8 == 7:
                            mm.then_inc(turned, 1)
                            if i == 7:
                                pe.wait_ge(columns_ready, 1)
                if c < routed:
                    pe.wait_ge(columns_ready, 1 + b // 2)
                    if k >= 1:
                        pe.wait_ge(hidden, k)
                    nc.tensor.matmul(cb_bank[:], g.expert_selector[:, c, :], combine_t[:, b * T:(b + 1) * T],
                                     start=True, stop=True).then_inc(cb_psum, 1)
                if c == 1 and b >= 1:
                    down(b - 1)
                if c == 4 and b >= 1:
                    ln_transpose(g, pe, ln, b - 1, xnt_bank, one_bank=True)
            down(B - 1)
            ln_transpose(g, pe, ln, B - 1, xnt_bank, one_bank=True)

        @block.scalar
        def _(act):
            act.wait_ge(logits_done, 1)
            nc.scalar.activation(scores[:].rearrange("p t e -> p (t e)"), logits_bank[:, 0:TILES * E],
                                 ACT.Sigmoid).then_inc(scores_done, 1)
            if beside:
                beside.copy(act, g.bank[3:6:2])

            def copy_combine(half):
                act.wait_ge(turned, half + 1)
                nc.scalar.copy(combine_t[:, half * 2 * T:(half + 1) * 2 * T], turn_bank[:].bitcast(BF16)
                               ).then_inc(columns_ready, 1)

            for k, (b, c) in enumerate(units):
                act.wait_ge(g_psum, k + 1)
                if k >= 2:
                    act.wait_ge(gated, k - 1)
                nc.scalar.activation(silu[:, k % 2, :], g_bank[k % 2][:], ACT.Silu).then_inc(silu_done, 1)
                if k == 0:
                    copy_combine(0)
                    copy_combine(1)
                if c == 4 and b >= 1:
                    ln_columns(g, act, ln, b - 1, xnt_bank)
            ln_columns(g, act, ln, B - 1, xnt_bank)

        @block.vector
        def _(v):
            n = [0]

            def after(ins):
                n[0] += 1
                ins.then_inc(route, 1)
                v.wait_ge(route, n[0])

            nc.vector.memset(combine_parts[:].bitcast(F32), 0.0).then_inc(weights_ready, 1)
            v.wait_ge(scores_done, 1)
            first_max(g, after, scores[:], best[:, 0, :], work[:], onehot[:, 0, :, :])
            after(nc.vector.scalar_tensor_tensor(others[:], onehot[:, 0, :, :], MASKED, scores[:], ALU.mult, ALU.add))
            first_max(g, after, others[:], best[:, 1, :], work[:], onehot[:, 1, :, :])
            after(nc.vector.tensor_tensor(denom[:], best[:, 0, :], best[:, 1, :], ALU.add))
            after(nc.vector.tensor_scalar(denom[:], denom[:], 1e-20, None, ALU.add))
            after(nc.vector.reciprocal(denom[:], denom[:]))
            after(nc.vector.tensor_tensor(work[:], onehot[:, 0, :, :], onehot[:, 1, :, :], ALU.add))
            after(nc.vector.scalar_tensor_tensor(work[:], scores[:], 2.5, work[:], ALU.mult, ALU.mult))
            after(nc.vector.tensor_tensor(combine[:], work[:], denom[:, :, None].to_broadcast([P, TILES, E]), ALU.mult))
            part = lambda k: combine_parts[:, :, k * E:(k + 1) * E]
            v.wait_ge(weights_ready, 1)
            after(nc.vector.tensor_copy(part(0), combine[:]))
            after(nc.vector.tensor_tensor(combine[:], combine[:], part(0), ALU.subtract))
            after(nc.vector.tensor_copy(part(1), combine[:]))
            nc.vector.tensor_tensor(part(2), combine[:], part(1), ALU.subtract).then_inc(weights_ready, 1)

            def add(b):
                v.wait_ge(y_psum, b + 1)
                rows = g.x[:, GROUP * b:GROUP * (b + 1), :].rearrange("p t d -> p (t d)")
                nc.vector.scalar_tensor_tensor(rows, y_bank[:], 0.5, rows, ALU.mult, ALU.add).then_inc(summed, 1)
                v.wait_ge(summed, b + 1)
                ln_stats(g, v, ln, b)

            m = 0
            for k, (b, c) in enumerate(units):
                v.wait_ge(silu_done, k + 1)
                v.wait_ge(u_psum, k + 1)
                dst = hid[:, b % 2, c, :]
                if c == 0 and b >= 2:
                    v.wait_ge(y_psum, b - 1)
                if c < routed:
                    if k >= 2:
                        v.wait_ge(hidden, k - 1)
                    nc.vector.tensor_tensor(prod[:, k % 2, :], silu[:, k % 2, :], u_bank[k % 2][:],
                                            ALU.mult).then_inc(gated, 1)
                    m += 1
                    v.wait_ge(gated, k + 1)
                    v.wait_ge(cb_psum, m)
                    nc.vector.tensor_tensor(dst, prod[:, k % 2, :], cb_bank[:], ALU.mult).then_inc(hidden, 1)
                else:
                    nc.vector.tensor_tensor(dst, silu[:, k % 2, :], u_bank[k % 2][:], ALU.mult).then_inc(hidden, 1)
                    nc.vector.memset(g.spare[:], 0.0).then_inc(gated, 1)
                if c == 2 and b >= 1:
                    add(b - 1)
                if c == 3 and b >= 1:
                    ln_rows(g, v, ln, b - 1)
            add(B - 1)
            ln_rows(g, v, ln, B - 1)

        @block.gpsimd
        def _(pool):
            for b in range(B):
                ln_rstd(g, pool, ln, b)


class ExpertProducts:
    def __init__(self, g, ctx, name, products):
        sem = semaphores(g, name)
        self.g, self.products = g, products
        self.loaded = [sem(f"loaded{i}") for i in range(2)]
        self.product, self.copied = sem("product"), sem("copied")
        self.w_in = ctx.enter_context(g.nc.sbuf_tensor(f"{name}_in", [P, 2, 4 * CH, D], F32))
        self.w_out = ctx.enter_context(g.nc.sbuf_tensor(f"{name}_out", [P, 2, 4 * CH, D], F32))

    def load(self, sp):
        a = self.g.a
        for i in range(2):
            rows = slice(i * 4 * HID, (i + 1) * 4 * HID)
            for dst, src in ((self.w_in, a["l2_w_in"]), (self.w_out, a["l2_w_out"])):
                sp.dma_start(dst[:, i, :, :], src[rows, :].rearrange("(c p) d -> p c d", p=P)).then_inc(self.loaded[i], 16)

    def multiply(self, pe, banks):
        for i in range(2):
            pe.wait_ge(self.loaded[i], 32)
            for e in range(4):
                for c in range(CH):
                    mm = self.g.nc.tensor.matmul(banks[i][:, e * D:(e + 1) * D], self.w_in[:, i, e * CH + c, :],
                                                 self.w_out[:, i, e * CH + c, :], start=(c == 0), stop=(c == CH - 1))
            mm.then_inc(self.product, 1)

    def copy(self, act, banks):
        for i in range(2):
            act.wait_ge(self.product, i + 1)
            self.g.nc.scalar.copy(self.products[:, i, :], banks[i][:]).then_inc(self.copied, 1)


def ffn2(g, name, products):
    nc, a = g.nc, g.a
    with ExitStack() as ctx:
        sem = semaphores(g, name)
        sb = lambda n, shape, dt=F32: ctx.enter_context(nc.sbuf_tensor(f"{name}_{n}", shape, dt))
        ln = LayerNormSems(sem)
        logits_done, route, partial = sem("logits_done"), sem("route"), sem("partial_sums")
        exp_in, exp_out, y_psum, added = sem("exp_in"), sem("exp_out"), sem("y_psum"), sem("added")
        xnt, gate_sb = g.xnt, g.gates[:, 2, :]
        logits, others, work = (sb(n, [P, TILES, E]) for n in ("logits", "others", "work"))
        best = sb("best", [P, 2, TILES])
        onehot = sb("onehot", [P, 2, TILES, E])
        delta, denom = sb("delta", [P, TILES]), sb("denom", [P, TILES])
        gates = sb("gates", [P, 2, TILES])
        weight = sb("weight", [P, TILES, E])
        y_bank = [g.bank[0:2], g.bank[2:4], g.bank[4:6]]
        xnt_bank, logits_bank = g.bank[6], g.bank[7]
        block = ctx.enter_context(nc.Block(no_gpsimd_drain=True))

        @block.tensor
        def _(pe):
            for i in range(TILES):
                mm = nc.tensor.matmul(logits_bank[:, i * E:(i + 1) * E], xnt[:, i * P:(i + 1) * P],
                                      gate_sb, start=True, stop=True)
            mm.then_inc(logits_done, 1)
            for i in range(TILES):
                if i >= 3:
                    pe.wait_ge(added, i - 2)
                for half in range(2):
                    mm = nc.tensor.matmul(y_bank[i % 3][half][:], xnt[:, i * P:(i + 1) * P], products[:, half, :],
                                          start=True, stop=True)
                mm.then_inc(y_psum, 1)
                if i % GROUP == 2 and i > GROUP:
                    ln_transpose(g, pe, ln, i // GROUP - 1, xnt_bank, one_bank=True)
            ln_transpose(g, pe, ln, B - 1, xnt_bank, one_bank=True)

        @block.scalar
        def _(act):
            act.wait_ge(exp_in, 1)
            nc.scalar.activation(delta[:], delta[:], ACT.Exp).then_inc(exp_out, 1)
            for b in range(B):
                ln_columns(g, act, ln, b, xnt_bank)

        @block.vector
        def _(v):
            n = [0]

            def after(ins):
                n[0] += 1
                ins.then_inc(route, 1)
                v.wait_ge(route, n[0])

            v.wait_ge(logits_done, 1)
            after(nc.vector.tensor_copy(logits[:], logits_bank[:, 0:TILES * E].rearrange("p (t e) -> p t e", e=E)))
            first_max(g, after, logits[:], best[:, 0, :], work[:], onehot[:, 0, :, :])
            after(nc.vector.scalar_tensor_tensor(others[:], onehot[:, 0, :, :], MASKED, logits[:], ALU.mult, ALU.add))
            first_max(g, after, others[:], best[:, 1, :], work[:], onehot[:, 1, :, :])
            nc.vector.tensor_tensor(delta[:], best[:, 1, :], best[:, 0, :], ALU.subtract).then_inc(exp_in, 1)
            v.wait_ge(exp_out, 1)
            after(nc.vector.tensor_scalar(denom[:], delta[:], 1.0, None, ALU.add))
            after(nc.vector.reciprocal(gates[:, 0, :], denom[:]))
            after(nc.vector.tensor_tensor(gates[:, 1, :], delta[:], gates[:, 0, :], ALU.mult))
            spread = lambda c: gates[:, c, :, None].to_broadcast([P, TILES, E])
            after(nc.vector.scalar_tensor_tensor(work[:], onehot[:, 0, :, :], 0.5, spread(0), ALU.mult, ALU.mult))
            after(nc.vector.scalar_tensor_tensor(others[:], onehot[:, 1, :, :], 0.5, spread(1), ALU.mult, ALU.mult))
            after(nc.vector.tensor_tensor(weight[:], work[:], others[:], ALU.add))
            for pair in range(0, TILES, 2):
                for e in range(E):
                    for i in (pair, pair + 1):
                        if e == 0:
                            v.wait_ge(y_psum, i + 1)
                        else:
                            v.wait_ge(partial, pair * (E - 1) + 2 * (e - 1) + i - pair + 1)
                        ins = nc.vector.scalar_tensor_tensor(g.x[:, i, :], y_bank[i % 3][e // 4][:, (e % 4) * D:(e % 4 + 1) * D],
                                                             weight[:, i, e:e + 1], g.x[:, i, :], ALU.mult, ALU.add)
                        ins.then_inc(partial if e < E - 1 else added, 1)
                v.wait_ge(added, pair + 2)
                b = pair // GROUP
                if pair % GROUP == 2:
                    ln_stats(g, v, ln, b)
                elif b >= 1:
                    ln_rows(g, v, ln, b - 1)
            ln_rows(g, v, ln, B - 1)

        @block.gpsimd
        def _(pool):
            for b in range(B):
                ln_rstd(g, pool, ln, b)


def recurrence2(g, name):
    nc, a = g.nc, g.a
    with ExitStack() as ctx:
        sem = semaphores(g, name)
        sb = lambda n, shape, dt=F32: ctx.enter_context(nc.sbuf_tensor(f"{name}_{n}", shape, dt))
        ln = LayerNormSems(sem)
        loaded, proj, sig, step = sem("weights_loaded"), sem("projected"), sem("sigmoids"), sem("step")
        used, scanned, y_psum, added = sem("banks_used"), sem("scanned"), sem("y_psum"), sem("added")
        xnt = g.xnt
        win, wout = sb("win", [P, 2 * D]), sb("wout", [P, D])
        bin_sb, bout = sb("bin", [P, 2]), sb("bout", [P, D])
        sg, sh = sb("sig_gate", [P, 2, T]), sb("sig_hidden", [P, 2, T])
        silu, drive, states = sb("silu", [P, 2, T]), sb("drive", [P, 2, T]), sb("states", [P, 2, T])
        out = sb("out", [P, T])
        decay = sb("decay", [P, T])
        xnt_bank, gate_bank, hid_bank, y_bank = g.bank[0], g.bank[2:4], g.bank[4:6], g.bank[6:8]
        block = ctx.enter_context(nc.Block(no_gpsimd_drain=True))

        @block.sync
        def _(sp):
            sp.dma_start(win[:], a["l2_win"]).then_inc(loaded, 16)
            sp.dma_start(wout[:], a["l2_wout"]).then_inc(loaded, 16)
            sp.dma_start(bin_sb[:], a["l2_bin"]).then_inc(loaded, 16)
            sp.dma_start(bout[:], a["l2_bout"].partition_broadcast(P)).then_inc(loaded, 16)

        @block.tensor
        def _(pe):
            def project_out(b):
                pe.wait_ge(scanned, b + 1)
                if b >= 2:
                    pe.wait_ge(added, b - 1)
                for i in range(GROUP):
                    mm = nc.tensor.matmul(y_bank[b % 2][:, i * D:(i + 1) * D], states[:, b % 2, i * P:(i + 1) * P],
                                          wout[:], start=True, stop=True)
                mm.then_inc(y_psum, 1)

            for b in range(B):
                if b == 0:
                    pe.wait_ge(loaded, 64)
                if b >= 2:
                    pe.wait_ge(used, b - 1)
                columns = xnt[:, b * T:(b + 1) * T]
                nc.tensor.matmul(gate_bank[b % 2][:], win[:, 0:D], columns, start=True, stop=True)
                nc.tensor.matmul(hid_bank[b % 2][:], win[:, D:2 * D], columns, start=True, stop=True).then_inc(proj, 1)
                if b >= 1:
                    project_out(b - 1)
                if b >= 2:
                    ln_transpose(g, pe, ln, b - 2, xnt_bank, one_bank=True)
            project_out(B - 1)
            for b in (B - 2, B - 1):
                ln_transpose(g, pe, ln, b, xnt_bank, one_bank=True)

        @block.scalar
        def _(act):
            for b in range(B):
                act.wait_ge(proj, b + 1)
                act.wait_ge(loaded, 64)
                if b >= 2:
                    act.wait_ge(scanned, b - 1)
                nc.scalar.activation(sg[:, b % 2, :], gate_bank[b % 2][:], ACT.Sigmoid, bias=bin_sb[:, 0:1])
                nc.scalar.activation(sh[:, b % 2, :], hid_bank[b % 2][:], ACT.Sigmoid, bias=bin_sb[:, 1:2]).then_inc(sig, 1)
                if b >= 2:
                    ln_columns(g, act, ln, b - 2, xnt_bank)
            for b in (B - 2, B - 1):
                ln_columns(g, act, ln, b, xnt_bank)

        @block.vector
        def _(v):
            n = [0]

            def after(ins):
                n[0] += 1
                ins.then_inc(step, 1)
                v.wait_ge(step, n[0])

            def add(b):
                v.wait_ge(y_psum, b + 1)
                rows = g.x[:, GROUP * b:GROUP * (b + 1), :]
                after(nc.vector.tensor_tensor(out[:].rearrange("p (t d) -> p t d", d=D),
                                              y_bank[b % 2][:].rearrange("p (t d) -> p t d", d=D),
                                              bout[:, None, :].to_broadcast([P, GROUP, D]), ALU.add))
                nc.vector.tensor_tensor(rows, rows, out[:].rearrange("p (t d) -> p t d", d=D), ALU.add).then_inc(added, 1)
                v.wait_ge(added, b + 1)
                ln_stats(g, v, ln, b)

            after(nc.vector.memset(decay[:], 0.9))
            for b in range(B):
                v.wait_ge(sig, b + 1)
                after(nc.vector.scalar_tensor_tensor(silu[:, b % 2, :], hid_bank[b % 2][:], bin_sb[:, 1:2],
                                                     sh[:, b % 2, :], ALU.add, ALU.mult))
                nc.vector.scalar_tensor_tensor(drive[:, b % 2, :], silu[:, b % 2, :], 0.1, sg[:, b % 2, :],
                                               ALU.mult, ALU.mult).then_inc(used, 1)
                v.wait_ge(used, b + 1)
                if b >= 2:
                    v.wait_ge(y_psum, b - 1)
                nc.vector.tensor_tensor_scan(states[:, b % 2, :], decay[:], drive[:, b % 2, :], 0.0,
                                             ALU.mult, ALU.add).then_inc(scanned, 1)
                if b >= 2:
                    ln_rows(g, v, ln, b - 2)
                if b >= 1:
                    add(b - 1)
            ln_rows(g, v, ln, B - 2)
            add(B - 1)
            ln_rows(g, v, ln, B - 1)

        @block.gpsimd
        def _(pool):
            for b in range(B):
                ln_rstd(g, pool, ln, b)


GROUPS = 4
GH = HEADS // GROUPS
NG = B * GROUPS
RING = 4
VW = 32
PARTS, TERMS = 3, 6
MAX_ROWS = PARTS * GH
MAX_AT, K_ROWS = 64, 96
MAX_AT1 = 96
R1, R2 = 4, 8
KR = R1 * R2


def slots():
    return [(n, n // GROUPS, n % GROUPS) for n in range(-2 * GROUPS + 1, NG + GROUPS)]


class RelativeBias:
    L = 3 * P

    def __init__(self, g, ctx, name, kq, qk):
        sem = semaphores(g, name)
        sb = lambda n, shape, dt=F32: ctx.enter_context(g.nc.sbuf_tensor(f"{name}_{n}", shape, dt))
        self.g, self.kq, self.qk = g, kq, qk
        self.loaded, self.summed, self.less_last, self.turned, self.lined = (sem(n) for n in (
            "loaded", "summed", "less_last", "turned", "lined"))
        self.spread, self.tiled, self.cast = sem("spread"), sem("tiled"), sem("cast")
        self.tables = sb("tables", [P, 3, P])
        self.sums = sb("sums", [P, 3, HEADS])
        self.line = sb("line", [HEADS, 2, self.L])
        self.tile = sb("tile", [P, HEADS, 2 * P])

    def load(self, sp):
        a = self.g.a
        for k, src in enumerate((a["l0_rel"], a["l0_rel_back"], a["l0_rel"][P - 1, :].partition_broadcast(P))):
            sp.dma_start(self.tables[:, k, :], src).then_inc(self.loaded, 16)

    def sum_heads(self, v):
        nc, line = self.g.nc, self.line
        nc.vector.memset(line[:, 0, 0:P], MASKED)
        nc.vector.memset(line[:, 0, 2 * P:self.L], 0.0)
        nc.vector.memset(line[:, 1, 0:P], 0.0)
        nc.vector.memset(line[:, 1, 2 * P:self.L], MASKED)
        v.wait_ge(self.loaded, 48)
        nc.vector.tensor_reduce(self.sums[:].rearrange("p k h -> p (k h)"),
                                self.tables[:].rearrange("p k (h d) -> p (k h) d", d=HD), axis=AX, op=ALU.add
                                ).then_inc(self.summed, 1)
        v.wait_ge(self.summed, 1)
        nc.vector.tensor_tensor(self.sums[:, 0:2, :], self.sums[:, 0:2, :],
                                self.sums[:, 2:3, :].to_broadcast([P, 2, HEADS]), ALU.subtract).then_inc(self.less_last, 1)

    def turn(self, pe, bank):
        pe.wait_ge(self.less_last, 1)
        for way in range(2):
            mm = self.g.nc.tensor.transpose(bank[0:HEADS, way * P:(way + 1) * P], self.sums[:, way, :], self.g.ident[:])
        mm.then_inc(self.turned, 1)

    def copy_lines(self, act, bank):
        act.wait_ge(self.turned, 1)
        for way in range(2):
            self.g.nc.scalar.copy(self.line[:, way, P:2 * P], bank[0:HEADS, way * P:(way + 1) * P]).then_inc(self.lined, 1)

    def spread_lines(self, act):
        act.wait_ge(self.lined, 2)
        for way in range(2):
            act.dma_start(self.g.bias_lines[way].rearrange("h (p l) -> h p l", l=self.L),
                         self.line[:, way:way + 1, :].to_broadcast([HEADS, P, self.L])).then_inc(self.spread, 16)

    def load_tiles(self, act):
        act.wait_ge(self.spread, 32)
        for way, dst in enumerate((self.tile, self.qk)):
            start = P - way
            skewed = self.g.bias_lines[way][:, start:start + P * (self.L - 1)].rearrange("h (p l) -> p h l", l=self.L - 1)
            act.dma_start(dst[:], skewed[:, :, 0:2 * P]).then_inc(self.tiled, 16)

    def split(self, v):
        nc, tile = self.g.nc, self.tile
        part = lambda k: self.kq[:, :, k, :]
        v.wait_ge(self.tiled, 32)
        nc.vector.tensor_copy(part(0), tile[:]).then_inc(self.cast, 1)
        v.wait_ge(self.cast, 1)
        nc.vector.tensor_tensor(tile[:], tile[:], part(0), ALU.subtract).then_inc(self.cast, 1)
        v.wait_ge(self.cast, 2)
        nc.vector.tensor_copy(part(1), tile[:]).then_inc(self.cast, 1)
        v.wait_ge(self.cast, 3)
        nc.vector.tensor_tensor(part(2), tile[:], part(1), ALU.subtract).then_inc(self.cast, 1)


def attention(g, name, kind, bias=None):
    nc, a = g.nc, g.a
    causal = kind != 3
    split = kind != 1
    layer = f"l{kind}"
    scale = HD ** -0.5 if split else KR ** -0.5
    first_query = [P * s if causal else 0 for s in range(GROUP)]
    width = [T - f for f in first_query]
    units = [[0], [1, 3], [2]] if causal else [[0], [1], [2], [3]]
    offset, unit_at, at = {}, [], 0
    for u in units:
        unit_at.append(at)
        for s in u:
            offset[s], at = at, at + width[s]
    prob_width, U = at, len(units)
    keys_seen = [P * (i + 1) if causal else T for i in range(GROUP)]
    group_units, group_tiles = GH * U, GH * GROUP

    with ExitStack() as ctx:
        sem = semaphores(g, name)
        sb = lambda n, shape, dt=F32: ctx.enter_context(nc.sbuf_tensor(f"{name}_{n}", shape, dt))
        if kind == 0:
            bias_kq, bias_qk = bias
        ln = LayerNormSems(sem)
        loaded, prepared, zeroed, spare_rows, values_zeroed = (sem(n) for n in (
            "weights_loaded", "selectors_placed", "zeros_made", "zeros_placed", "values_zeroed"))
        proj, taken, hi_ready, rem_ready, mid_ready, parts_ready = (sem(n) for n in (
            "projected", "projections_taken", "high_parts", "remainders", "middle_parts", "parts"))
        v_psum, v_ready = sem("values_psum"), sem("values")
        written = sem("terms_written")
        op_loaded = [sem(f"operands{i}") for i in range(RING)]
        rows_psum, rows_taken = sem("rows_pass"), sem("rows_taken")
        max_step, max_split, max_psum, max_cols, max_loaded = (sem(n) for n in (
            "max_step", "max_split", "max_psum", "max_columns", "max_loaded"))
        cols_psum, probs_ready = sem("columns_pass"), sem("probs")
        o_psum, o_copied, t_psum, t_norm = sem("context_psum"), sem("context"), sem("context_turned"), sem("context_rows")
        norm_step = sem("norm_step")
        c_psum, c_ready, y_psum, added = sem("rows_turned"), sem("context_columns"), sem("out_psum"), sem("added")

        columns_of = lambda b: g.xnt[:, b * T:(b + 1) * T]
        wo, bo = sb("wo", [P, D]), sb("bo", [P, D])
        values = sb("values", [P, 2, GROUP, HEADS, VW])
        probs = sb("probs", [P, 2, GH, prob_width])
        maxima = sb("maxima", [P, 2, GROUP, GH])
        far = sb("far", [P, 2, GROUP, GH])
        max_rest = sb("max_rest", [P, GROUP, GH])
        max_parts = sb("max_parts", [P, GROUP, PARTS, GH], BF16)
        max_t = sb("max_t", [MAX_ROWS, T], BF16)
        context_t = sb("context_t", [P, T])
        recip = sb("recip", [P, GROUP, GH])
        context = sb("context", [P, GROUP, D])
        columns = sb("columns", [P, T])
        out = sb("out", [P, GROUP, D])
        if split:
            wq, wk, wv = sb("wq", [P, P]), sb("wk", [P, P]), sb("wv", [P, P])
            bq, bk, bv = sb("bq", [P, 1]), sb("bk", [P, 1]), sb("bv", [P, D])
            rest = sb("qk", [P, 2, T])
            parts = sb("parts", [P, 2, PARTS, T], BF16)
            q_op, k_op = sb("queries", [P, RING, GH, T], BF16), sb("keys", [P, RING, GH, T], BF16)
            zeros = sb("zeros", [P, T], BF16)
            weight_loads, op_loads = 8, 3
        else:
            wqk = sb("wqk", [P, T])
            pj = sb("pj", [P, 2, GROUP, T])
            outer = sb("outer", [P, 2, 2, GROUP, P])
            rest = sb("rest", [P, 2, T])
            parts = sb("parts", [P, 2, 2, PARTS, T], BF16)
            q_op, k_op = sb("queries", [P, RING, 2, GH, T], BF16), sb("keys", [P, RING, 2, GH, T], BF16)
            weight_loads, op_loads = 3, 6
            outer_ready, outer_psum = sem("outer_products"), sem("outer_products_turned")
        rows_bank, cols_bank = g.bank[0:2], g.bank[2:5]
        o_bank, prep_bank, misc_bank = g.bank[5], g.bank[6], g.bank[7]
        block = ctx.enter_context(nc.Block(no_gpsimd_drain=True))

        def low_parts(engine, ops, b, side):
            k = 2 * b + side
            engine.wait_ge(hi_ready, k + 1)
            ops.tensor_tensor(rest[:, side, :], rest[:, side, :], parts[:, side, 0, :], ALU.subtract).then_inc(rem_ready, 1)
            engine.wait_ge(rem_ready, k + 1)
            ops.tensor_copy(parts[:, side, 1, :], rest[:, side, :]).then_inc(mid_ready, 1)
            engine.wait_ge(mid_ready, k + 1)
            ops.tensor_tensor(parts[:, side, 2, :], rest[:, side, :], parts[:, side, 1, :], ALU.subtract
                              ).then_inc(parts_ready, 1)

        @block.sync
        def _(sp):
            def load(dst, src):
                sp.dma_start(dst, src).then_inc(loaded, 16)

            if split:
                load(wq[:], a[layer + "_wq"]); load(wk[:], a[layer + "_wk"]); load(wv[:], a[layer + "_wv"])
                load(bq[:], a[layer + "_bq"]); load(bk[:], a[layer + "_bk"])
                load(bv[:], a[layer + "_bv"].partition_broadcast(P))
            else:
                load(wqk[:], a["l1_wqk"])
            load(wo[:], a[layer + "_wo"]); load(bo[:], a[layer + "_bo"].partition_broadcast(P))
            if split:
                sp.wait_ge(zeroed, 1)
                pad = slice(TERMS * HD, K_ROWS)
                sp.dma_start(q_op[pad, :, :, :].rearrange("p i j t -> p (i j) t"),
                             zeros[pad, None, :].to_broadcast([K_ROWS - TERMS * HD, RING * GH, T])).then_inc(spare_rows, 16)
                pad = slice(TERMS * HD, MAX_AT)
                sp.dma_start(k_op[pad, :, :, :].rearrange("p i j t -> p (i j) t"),
                             zeros[pad, None, :].to_broadcast([MAX_AT - TERMS * HD, RING * GH, T])).then_inc(spare_rows, 16)

            def write_terms(b):
                if b >= 2:
                    for i in range(RING):
                        sp.wait_ge(op_loaded[i], 16 * op_loads * (b - 1))
                for side in range(2):
                    sp.wait_ge(parts_ready, 2 * b + side + 1)
                    dst = g.terms[b % 2][side]
                    if side == 0:
                        for at, part, times in ((0, 0, 3), (3, 1, 2), (5, 2, 1)):
                            sp.dma_start(dst[at:at + times].rearrange("j r t -> r j t"),
                                         parts[:, 0, part:part + 1, :].to_broadcast([P, times, T])).then_inc(written, 16)
                    else:
                        for at, times in ((0, 3), (3, 2), (5, 1)):
                            sp.dma_start(dst[at:at + times].rearrange("j r t -> r j t"),
                                         parts[:, 1, 0:times, :]).then_inc(written, 16)

            def write_parts(G):
                if G >= 2:
                    sp.wait_ge(op_loaded[(G - 2) % RING], 16 * op_loads * ((G - 2) // RING + 1))
                for side in range(2):
                    sp.wait_ge(parts_ready, 2 * G + side + 1)
                    sp.dma_start(g.terms[G % 2][side][0:PARTS].rearrange("k r t -> r k t"),
                                 parts[:, G % 2, side, :, :]).then_inc(written, 16)

            def load_operands(G):
                i, b, q = G % RING, G // GROUPS, G % GROUPS
                if G >= RING:
                    sp.wait_ge(cols_psum, group_units * (G - RING + 1))
                if split:
                    if G == 0:
                        sp.wait_ge(spare_rows, 32)
                    sp.wait_ge(written, 16 * 6 * (b + 1))
                    for side, op in enumerate((q_op, k_op)):
                        sp.dma_start(op[0:TERMS * HD, i, :, :],
                                     g.terms[b % 2][side].rearrange("j (d h) t -> (j d) h t", h=HEADS)[:, GH * q:GH * (q + 1), :]
                                     ).then_inc(op_loaded[i], 16)
                    sp.dma_start(q_op[MAX_AT:MAX_AT + MAX_ROWS, i, :, :], zeros[MAX_AT:MAX_AT + MAX_ROWS, None, :]
                                 .to_broadcast([MAX_ROWS, GH, T])).then_inc(op_loaded[i], 16)
                else:
                    sp.wait_ge(written, 32 * (G + 1))
                    stored = [g.terms[G % 2][side].rearrange("k (r j) t -> (k r) j t", j=GH) for side in range(2)]
                    part = lambda side, k: stored[side][KR * k:KR * (k + 1)]
                    sp.dma_start(q_op[0:KR, i, 0, :, :], part(0, 0)).then_inc(op_loaded[i], 16)
                    sp.dma_start(q_op[KR:3 * KR, i, 0, :, :], stored[0][0:2 * KR]).then_inc(op_loaded[i], 16)
                    sp.dma_start(q_op[0:3 * KR, i, 1, :, :], stored[0][0:3 * KR]).then_inc(op_loaded[i], 16)
                    sp.dma_start(k_op[0:KR, i, 0, :, :], part(1, 2)).then_inc(op_loaded[i], 16)
                    sp.dma_start(k_op[KR:3 * KR, i, 0, :, :], stored[1][KR:3 * KR]).then_inc(op_loaded[i], 16)
                    sp.dma_start(k_op[0:3 * KR, i, 1, :, :], stored[1][0:3 * KR]).then_inc(op_loaded[i], 16)

            def load_maxima(G):
                sp.wait_ge(max_cols, G + 1)
                dst = q_op[MAX_AT:MAX_AT + MAX_ROWS, G % RING, :, :] if split else \
                    q_op[MAX_AT1:MAX_AT1 + MAX_ROWS, G % RING, 1, :, :]
                sp.dma_start(dst, max_t[:, None, :].to_broadcast([MAX_ROWS, GH, T])).then_inc(max_loaded, 16)

            for n, b, q in slots():
                if 0 <= n + 1 < NG:
                    load_maxima(n + 1)
                if 0 <= n + 3 < NG:
                    load_operands(n + 3)
                if not split and 0 <= n + 4 < NG:
                    write_parts(n + 4)
                if split and q == 0 and 0 <= b + 1 < B:
                    write_terms(b + 1)
            sp.wait_ge(max_loaded, 16 * NG)

        @block.tensor
        def _(pe):
            misc_last, prep_last = [], []

            def bank_free(last, *reader):
                for s, value in last:
                    pe.wait_ge(s, value)
                last[:] = [reader]

            def columns_unit(G, j, u):
                i, k = G % RING, G * group_units + j * U + u
                h = GH * (G % GROUPS) + j
                if k >= 3:
                    pe.wait_ge(probs_ready, k - 2)
                bank = cols_bank[k % 3]
                c0 = 0
                for s in units[u]:
                    dst = bank[:, c0:c0 + width[s]]
                    q0 = first_query[s]
                    key = slice(s * P, (s + 1) * P)
                    if split:
                        mm = nc.tensor.matmul(dst, k_op[0:K_ROWS, i, j, key], q_op[0:K_ROWS, i, j, q0:T],
                                              start=True, stop=kind == 3)
                    else:
                        nc.tensor.matmul(dst, k_op[0:3 * KR, i, 0, j, key], q_op[0:3 * KR, i, 0, j, q0:T],
                                         start=True, stop=False)
                        nc.tensor.matmul(dst, k_op[0:MAX_AT1 + MAX_ROWS, i, 1, j, key],
                                         q_op[0:MAX_AT1 + MAX_ROWS, i, 1, j, q0:T], start=False, stop=False)
                        mm = nc.tensor.matmul(bank[:, c0:c0 + P], g.identb[:], g.mask_kq[:], start=False, stop=True)
                    if kind == 0:
                        w = min(2 * P, width[s])
                        for p in range(3):
                            mm = nc.tensor.matmul(bank[:, c0:c0 + w], g.identb[:], bias_kq[:, h, p, 0:w],
                                                  start=False, stop=p == 2)
                    c0 += width[s]
                mm.then_inc(cols_psum, 1)

            def rows_tile(G, j, t):
                i, k = G % RING, G * group_tiles + j * GROUP + t
                if k >= 2:
                    pe.wait_ge(rows_taken, k - 1)
                query = slice(t * P, (t + 1) * P)
                dst = rows_bank[k % 2][:, 0:keys_seen[t]]
                if split:
                    mm = nc.tensor.matmul(dst, q_op[0:K_ROWS, i, j, query], k_op[0:K_ROWS, i, j, 0:keys_seen[t]],
                                          start=True, stop=True)
                else:
                    mm = nc.tensor.matmul(dst, q_op[0:3 * KR, i, 0, j, query], k_op[0:3 * KR, i, 0, j, 0:keys_seen[t]],
                                          start=True, stop=True)
                mm.then_inc(rows_psum, 1)

            def context_step(G, s):
                b = G // GROUPS
                if s == 0:
                    pe.wait_ge(probs_ready, group_units * (G + 1))
                    pe.wait_ge(v_ready, b + 1)
                    if G >= 1:
                        pe.wait_ge(o_copied, G)
                for j in range(GH):
                    mm = nc.tensor.matmul(o_bank[VW * j:VW * (j + 1), first_query[s]:T],
                                          values[:, b % 2, s, GH * (G % GROUPS) + j, :],
                                          probs[:, G % 2, j, offset[s]:offset[s] + width[s]],
                                          start=(s == 0), stop=(s == GROUP - 1))
                if s == GROUP - 1:
                    mm.then_inc(o_psum, 1)

            def turn_context(G):
                pe.wait_ge(o_copied, G + 1)
                bank_free(misc_last, t_norm, G + 1)
                for t in range(GROUP):
                    mm = nc.tensor.transpose(misc_bank[:, t * P:(t + 1) * P], context_t[:, t * P:(t + 1) * P], g.ident[:])
                mm.then_inc(t_psum, 1)

            def turn_rows(b):
                pe.wait_ge(t_norm, GROUPS * (b + 1))
                bank_free(misc_last, c_ready, b + 1)
                for t in range(GROUP):
                    mm = nc.tensor.transpose(misc_bank[:, t * P:(t + 1) * P], context[:, t, :], g.ident[:])
                mm.then_inc(c_psum, 1)

            def project_out(b):
                pe.wait_ge(c_ready, b + 1)
                bank_free(misc_last, added, b + 1)
                for t in range(GROUP):
                    mm = nc.tensor.matmul(misc_bank[:, t * D:(t + 1) * D], columns[:, t * P:(t + 1) * P], wo[:],
                                          start=True, stop=True)
                mm.then_inc(y_psum, 1)

            def turn_maxima(G):
                pe.wait_ge(max_split, G + 1)
                bank_free(misc_last, max_cols, G + 1)
                bank = misc_bank[:].bitcast(BF16)
                for t in range(GROUP):
                    mm = nc.tensor.transpose(bank[0:MAX_ROWS, t * P:(t + 1) * P],
                                             max_parts[:, t, :, :].rearrange("p k h -> p (k h)"), g.identb[:])
                mm.then_inc(max_psum, 1)

            def turn_norm(b):
                bank_free(prep_last, ln.xnt, b + 1)
                ln_transpose(g, pe, ln, b, prep_bank)

            def project_qk(b, side):
                pe.wait_ge(loaded, 16 * weight_loads)
                bank_free(prep_last, taken, 2 * b + side + 1)
                nc.tensor.matmul(prep_bank[:], (wq, wk)[side][:], columns_of(b), start=True, stop=True).then_inc(proj, 1)

            def project_values(b):
                bank_free(prep_last, v_ready, b + 1)
                for t in range(GROUP):
                    mm = nc.tensor.matmul(prep_bank[:, t * D:(t + 1) * D], columns_of(b)[:, t * P:(t + 1) * P], wv[:],
                                          start=True, stop=True)
                mm.then_inc(v_psum, 1)

            def project_tile(b, t):
                pe.wait_ge(loaded, 16 * weight_loads)
                bank_free(prep_last, taken, GROUP * b + t + 1)
                nc.tensor.matmul(prep_bank[:], columns_of(b)[:, t * P:(t + 1) * P], wqk[:], start=True, stop=True
                                 ).then_inc(proj, 1)

            def turn_outer(G, side):
                pe.wait_ge(outer_ready, 2 * G + side + 1)
                bank_free(prep_last, rem_ready, 2 * G + side + 1)
                for t in range(GROUP):
                    mm = nc.tensor.transpose(prep_bank[:, t * P:(t + 1) * P], outer[:, G % 2, side, t, :], g.ident[:])
                mm.then_inc(outer_psum, 1)

            for n, b, q in slots():
                C, R = 0 <= n < NG, 0 <= n + 2 < NG
                if C:
                    pe.wait_ge(max_loaded, 16 * (n + 1))
                if R:
                    pe.wait_ge(op_loaded[(n + 2) % RING], 16 * op_loads * ((n + 2) // RING + 1))
                    if n + 2 < RING:
                        pe.wait_ge(prepared, 1)
                if not split and 0 <= n + 5 < NG:
                    turn_outer(n + 5, 0)
                for j in range(GH):
                    for t in range(GROUP):
                        if C and t < U:
                            columns_unit(n, j, t)
                        if R:
                            rows_tile(n + 2, j, t)
                        if t == 1 and 0 <= n - 1 < NG:
                            context_step(n - 1, j)
                    if j == 0:
                        if 0 <= n + 1 < NG:
                            turn_maxima(n + 1)
                        if not split and q == 1 and 0 <= b + 2 < B:
                            project_tile(b + 2, 0)
                        if not split and q == 2 and 0 <= b + 2 < B:
                            project_tile(b + 2, 3)
                    elif j == 1:
                        if 0 <= n - 2 < NG:
                            turn_context(n - 2)
                        if split and q in (2, 3) and 0 <= b + 2 < B:
                            project_qk(b + 2, q - 2)
                        if not split and 0 <= n + 5 < NG:
                            turn_outer(n + 5, 1)
                    elif j == 2:
                        if (n - 3) % GROUPS == GROUPS - 1 and 0 <= n - 3 < NG:
                            project_out((n - 3) // GROUPS)
                        if split and q == 0 and 0 <= b + 1 < B:
                            project_values(b + 1)
                        if q == 3 and 0 <= b - 1 < B:
                            turn_norm(b - 1)
                        if not split and q == 1 and 0 <= b + 2 < B:
                            project_tile(b + 2, 1)
                    else:
                        if (n - 2) % GROUPS == GROUPS - 1 and 0 <= n - 2 < NG:
                            turn_rows((n - 2) // GROUPS)
                        if not split and q == 1 and 0 <= b + 2 < B:
                            project_tile(b + 2, 2)

        @block.scalar
        def _(act):
            def exponentials(G, j):
                for u, at in zip(range(U), unit_at):
                    k = G * group_units + j * U + u
                    w = sum(width[s] for s in units[u])
                    act.wait_ge(cols_psum, k + 1)
                    if G >= 2 and j == 0 and u == 0:
                        act.wait_ge(o_psum, G - 1)
                    nc.scalar.activation(probs[:, G % 2, j, at:at + w], cols_bank[k % 3][:, 0:w], ACT.Exp
                                         ).then_inc(probs_ready, 1)

            def copy_context(G):
                act.wait_ge(o_psum, G + 1)
                if G >= 1:
                    act.wait_ge(t_psum, G)
                nc.scalar.copy(context_t[:], o_bank[:]).then_inc(o_copied, 1)

            def copy_columns(b):
                act.wait_ge(c_psum, b + 1)
                if b >= 1:
                    act.wait_ge(y_psum, b)
                nc.scalar.copy(columns[:], misc_bank[:]).then_inc(c_ready, 1)

            def copy_maxima(G):
                act.wait_ge(max_psum, G + 1)
                if G >= 1:
                    act.wait_ge(max_loaded, 16 * G)
                nc.scalar.copy(max_t[:], misc_bank[:].bitcast(BF16)[0:MAX_ROWS, 0:T]).then_inc(max_cols, 1)

            def high_part(b, side):
                act.wait_ge(taken, 2 * b + side + 1)
                if b >= 1:
                    act.wait_ge(written, 16 * 6 * b)
                nc.scalar.copy(parts[:, side, 0, :], rest[:, side, :]).then_inc(hi_ready, 1)

            def take_tile(b, t):
                act.wait_ge(proj, GROUP * b + t + 1)
                if b >= 2:
                    act.wait_ge(outer_ready, 2 * GROUPS * (b - 1))
                    act.wait_ge(v_ready, b - 1)
                nc.scalar.mul(pj[:, b % 2, t, 0:HEADS * R1], prep_bank[:, 0:HEADS * R1], scale)
                nc.scalar.copy(pj[:, b % 2, t, HEADS * R1:T], prep_bank[:, HEADS * R1:T]).then_inc(taken, 1)

            def high_outer(G, side):
                act.wait_ge(outer_psum, 2 * G + side + 1)
                if G >= 2:
                    act.wait_ge(written, 32 * (G - 1))
                nc.scalar.copy(parts[:, G % 2, side, 2 * side, :], prep_bank[:]).then_inc(hi_ready, 1)

            def middle_outer(G, side):
                act.wait_ge(rem_ready, 2 * G + side + 1)
                nc.scalar.copy(parts[:, G % 2, side, 1, :], rest[:, side, :]).then_inc(mid_ready, 1)

            if split:
                nc.scalar.copy(k_op[MAX_AT:K_ROWS, :, :, :].rearrange("p i j t -> p i j t"),
                               g.head_selector[MAX_AT:K_ROWS, None, :, None].to_broadcast([K_ROWS - MAX_AT, RING, GH, T])
                               ).then_inc(prepared, 1)
            else:
                nc.scalar.copy(k_op[MAX_AT1:P, :, 1, :, :],
                               g.head_selector1[MAX_AT1:P, None, :, None].to_broadcast([P - MAX_AT1, RING, GH, T])
                               ).then_inc(prepared, 1)
            for n, b, q in slots():
                C, O = 0 <= n < NG, 0 <= n + 5 < NG
                if 0 <= n - 2 < NG:
                    copy_context(n - 2)
                if not split and O:
                    high_outer(n + 5, 0)
                for j in range(GH):
                    if C:
                        exponentials(n, j)
                    if j == 0:
                        if (n - 3) % GROUPS == GROUPS - 1 and 0 <= n - 3 < NG:
                            copy_columns((n - 3) // GROUPS)
                        if not split and q == 1 and 0 <= b + 2 < B:
                            take_tile(b + 2, 0)
                        if not split and q == 2 and 0 <= b + 2 < B:
                            take_tile(b + 2, 3)
                    elif j == 1:
                        if 0 <= n + 1 < NG:
                            copy_maxima(n + 1)
                        if not split and O:
                            middle_outer(n + 5, 0)
                            high_outer(n + 5, 1)
                    elif j == 2:
                        if q == 3 and 0 <= b - 1 < B:
                            ln_columns(g, act, ln, b - 1, prep_bank)
                        if split and q in (2, 3) and 0 <= b + 2 < B:
                            high_part(b + 2, q - 2)
                        if not split and q == 1 and 0 <= b + 2 < B:
                            take_tile(b + 2, 1)
                    else:
                        if not split and O:
                            middle_outer(n + 5, 1)
                        if not split and q == 1 and 0 <= b + 2 < B:
                            take_tile(b + 2, 2)

        @block.vector
        def _(v):
            steps = [0]

            def after(ins):
                steps[0] += 1
                ins.then_inc(norm_step, 1)
                v.wait_ge(norm_step, steps[0])

            def row_maxima(G, j):
                h = GH * (G % GROUPS) + j
                for t in range(GROUP):
                    k = G * group_tiles + j * GROUP + t
                    v.wait_ge(rows_psum, k + 1)
                    bank = rows_bank[k % 2]
                    best = maxima[:, G % 2, t, j:j + 1]
                    w = keys_seen[t]
                    if kind == 3:
                        ins = nc.vector.tensor_reduce(best, bank[:], axis=AX, op=ALU.max)
                    elif kind == 1:
                        ins = nc.vector.tensor_tensor_reduce(out=bank[:, 0:w], in0=bank[:, 0:w], in1=g.mask_qk[:, T - w:T],
                                                             scale=1.0, scalar=-3.0e38, op0=ALU.add, op1=ALU.max, accum_out=best)
                    else:
                        near = min(2 * P, w)
                        if t >= 2:
                            nc.vector.tensor_reduce(far[:, G % 2, t, j:j + 1], bank[:, 0:w - near], axis=AX, op=ALU.max)
                        ins = nc.vector.tensor_tensor_reduce(out=bank[:, w - near:w], in0=bank[:, w - near:w],
                                                             in1=bias_qk[:, h, 2 * P - near:2 * P], scale=1.0, scalar=-3.0e38,
                                                             op0=ALU.add, op1=ALU.max, accum_out=best)
                    ins.then_inc(rows_taken, 1)

            def split_maxima(G):
                v.wait_ge(rows_taken, group_tiles * (G + 1))
                best = maxima[:, G % 2, :, :]
                if G >= 1:
                    v.wait_ge(max_psum, G)
                if kind == 0:
                    after(nc.vector.tensor_tensor(maxima[:, G % 2, 2:GROUP, :], maxima[:, G % 2, 2:GROUP, :],
                                                  far[:, G % 2, 2:GROUP, :], ALU.max))
                part = lambda k: max_parts[:, :, k, :]
                after(nc.vector.tensor_scalar(part(0), best, -1.0, None, ALU.mult))
                after(nc.vector.scalar_tensor_tensor(max_rest[:], best, -1.0, part(0), ALU.mult, ALU.subtract))
                after(nc.vector.tensor_copy(part(1), max_rest[:]))
                nc.vector.tensor_tensor(part(2), max_rest[:], part(1), ALU.subtract).then_inc(max_split, 1)

            def normalise(G):
                v.wait_ge(t_psum, G + 1)
                q = G % GROUPS
                by_head = misc_bank[:].rearrange("p (t j w) -> p t j w", t=GROUP, j=GH)
                after(nc.vector.reciprocal(recip[:], by_head[:, :, :, HD]))
                if q == 0 and G >= GROUPS:
                    v.wait_ge(c_psum, G // GROUPS)
                dst = context[:, :, GH * q * HD:GH * (q + 1) * HD].rearrange("p t (j d) -> p t j d", d=HD)
                nc.vector.tensor_tensor(dst, by_head[:, :, :, 0:HD], recip[:, :, :, None].to_broadcast([P, GROUP, GH, HD]),
                                        ALU.mult).then_inc(t_norm, 1)

            def add_out(b):
                v.wait_ge(y_psum, b + 1)
                after(nc.vector.tensor_tensor(out[:], misc_bank[:].rearrange("p (t d) -> p t d", d=D),
                                              bo[:, None, :].to_broadcast([P, GROUP, D]), ALU.add))
                tiles = slice(GROUP * b, GROUP * (b + 1))
                nc.vector.tensor_tensor(g.x[:, tiles, :], g.x[:, tiles, :], out[:], ALU.add).then_inc(added, 1)
                v.wait_ge(added, b + 1)

            def take_qk(b, side):
                v.wait_ge(proj, 2 * b + side + 1)
                if b >= 1:
                    v.wait_ge(parts_ready, 2 * (b - 1) + side + 1)
                if side == 0:
                    ins = nc.vector.tensor_scalar(rest[:, 0, :], prep_bank[:], bq[:], scale, ALU.add, ALU.mult)
                else:
                    ins = nc.vector.tensor_scalar(rest[:, 1, :], prep_bank[:], bk[:], None, ALU.add)
                ins.then_inc(taken, 1)
                if b == 0:
                    low_parts(v, nc.vector, b, side)

            def take_values(b):
                v.wait_ge(v_psum, b + 1)
                if b == 0:
                    v.wait_ge(values_zeroed, 2)
                if b >= 2:
                    v.wait_ge(o_psum, GROUPS * (b - 1))
                nc.vector.tensor_tensor(values[:, b % 2, :, :, 0:HD],
                                        prep_bank[:].rearrange("p (t h d) -> p t h d", t=GROUP, h=HEADS),
                                        bv[:].rearrange("p (h d) -> p h d", d=HD)[:, None, :, :]
                                        .to_broadcast([P, GROUP, HEADS, HD]), ALU.add).then_inc(v_ready, 1)

            def outer_rest(G, side):
                v.wait_ge(hi_ready, 2 * G + side + 1)
                if G >= 1:
                    v.wait_ge(parts_ready, 2 * (G - 1) + side + 1)
                nc.vector.tensor_tensor(rest[:, side, :], prep_bank[:], parts[:, G % 2, side, 2 * side, :], ALU.subtract
                                        ).then_inc(rem_ready, 1)

            if split:
                nc.vector.memset(zeros[:].bitcast(F32), 0.0).then_inc(zeroed, 1)
            for n, b, q in slots():
                if 0 <= n + 1 < NG:
                    split_maxima(n + 1)
                for j in range(GH):
                    if 0 <= n + 2 < NG:
                        row_maxima(n + 2, j)
                    if j == 0:
                        if split and q == 1 and 0 <= b + 1 < B:
                            take_values(b + 1)
                        if q == 3 and 0 <= b - 1 < B:
                            ln_rows(g, v, ln, b - 1)
                        if not split and 0 <= n + 5 < NG:
                            outer_rest(n + 5, 0)
                    elif j == 2:
                        if 0 <= n - 2 < NG:
                            normalise(n - 2)
                        if split and q in (2, 3) and 0 <= b + 2 < B:
                            take_qk(b + 2, q - 2)
                        if not split and 0 <= n + 5 < NG:
                            outer_rest(n + 5, 1)
                    elif j == 3:
                        if (n - 3) % GROUPS == GROUPS - 1 and 0 <= n - 3 < NG:
                            add_out((n - 3) // GROUPS)
                            ln_stats(g, v, ln, (n - 3) // GROUPS)

        @block.gpsimd
        def _(pool):
            def make_outer(G):
                b, c = G // GROUPS, G % GROUPS
                pool.wait_ge(taken, GROUP * (b + 1))
                if G >= 2:
                    pool.wait_ge(outer_psum, 2 * (G - 1))
                for side in range(2):
                    for t in range(GROUP):
                        at1 = side * HEADS * R1 + c * GH * R1
                        at2 = 2 * HEADS * R1 + side * HEADS * R2 + c * GH * R2
                        one = pj[:, b % 2, t, at1:at1 + GH * R1].rearrange("p (j r) -> p r j", r=R1)
                        two = pj[:, b % 2, t, at2:at2 + GH * R2].rearrange("p (j s) -> p s j", s=R2)
                        wide = [P, R1, R2, GH]
                        ins = nc.gpsimd.tensor_tensor(outer[:, G % 2, side, t, :].rearrange("p (r s j) -> p r s j", r=R1, s=R2),
                                                      one[:, :, None, :].to_broadcast(wide),
                                                      two[:, None, :, :].to_broadcast(wide), ALU.mult)
                    ins.then_inc(outer_ready, 1)

            def low_outer(G, side):
                pool.wait_ge(mid_ready, 2 * G + side + 1)
                nc.gpsimd.tensor_tensor(parts[:, G % 2, side, 2 - 2 * side, :], rest[:, side, :], parts[:, G % 2, side, 1, :],
                                        ALU.subtract).then_inc(parts_ready, 1)

            def copy_values(b):
                pool.wait_ge(taken, GROUP * (b + 1))
                if b >= 2:
                    pool.wait_ge(o_psum, GROUPS * (b - 1))
                nc.gpsimd.tensor_copy(values[:, b % 2, :, :, 0:HD],
                                      pj[:, b % 2, :, T - D:T].rearrange("p t (h d) -> p t h d", d=HD)).then_inc(v_ready, 1)

            nc.gpsimd.memset(values[:], 0.0).then_inc(values_zeroed, 1)
            pool.wait_ge(values_zeroed, 1)
            nc.gpsimd.memset(values[:, :, :, :, HD:HD + 1].rearrange("p b t h w -> p (b t h) w"), 1.0
                             ).then_inc(values_zeroed, 1)
            pool.wait_ge(values_zeroed, 2)
            for n, b, q in slots():
                if not split and 0 <= n + 6 < NG:
                    make_outer(n + 6)
                if not split and 0 <= n + 5 < NG:
                    for side in range(2):
                        low_outer(n + 5, side)
                if not split and (n + 3) % GROUPS == 0 and 0 <= n + 3 < NG:
                    copy_values((n + 3) // GROUPS)
                if q == 2 and 0 <= b - 1 < B:
                    ln_rstd(g, pool, ln, b - 1)
                if split and q in (2, 3) and 1 <= b + 2 < B:
                    low_parts(pool, nc.gpsimd, b + 2, q - 2)


class Shared:
    def __init__(self, nc, a):
        sb = lambda n, shape, dt=F32: nc.alloc_sbuf_tensor(n, shape, dt)
        self.nc = nc
        self.a = a
        self.spent = []
        self.x = sb("x_rows", [P, TILES, D])
        self.xn = sb("normalised_rows", [P, TILES, D + 1])
        self.xnt = sb("normalised_columns", [P, TOKENS])
        self.gates = sb("gates", [P, 4, E])
        self.gamma_beta = sb("gamma_beta", [P, 2])
        self.untaken = sb("untaken", [P, D + 1])
        self.token_i = sb("token_numbers_i", [P, 2 * TILES], U32)
        self.token = sb("token_numbers", [P, 2 * TILES])
        self.expert_selector = sb("expert_selector", [P, E // 2, P], BF16)
        self.stats = sb("stats", [P, TILES, 6])
        self.moments = sb("moments", [P, TILES, 2])
        self.var_eps = sb("var_eps", [P, TILES])
        self.rstd = sb("rstd", [P, TILES])
        self.neg_half = sb("neg_half", [P, TILES])
        self.ident = sb("ident", [P, P])
        self.identb = sb("identb", [P, P], BF16)
        self.onesb = sb("onesb", [P, P], BF16)
        self.beforeb = sb("beforeb", [P, P], BF16)
        self.mask_kq = sb("mask_kq", [P, P], BF16)
        self.mask_qk = sb("mask_qk", [P, T])
        self.rev = sb("rev", [P, 2 * TILES, E])
        self.scan_keep = sb("scan_keep", [P, E, 2 * TILES])
        self.scan_keep1 = sb("scan_keep1", [P, E, TILES])
        self.tie = sb("tie", [P, TILES])
        self.spare = sb("spare", [P, 1])
        self.bank = [nc.alloc_psum_tensor(f"bank{i}", [P, T], F32) for i in range(8)]
        self.head_selector = sb("head_selector", [P, GH], BF16)
        self.head_selector1 = sb("head_selector1", [P, GH], BF16)
        self.terms = [[nc.dram_tensor(f"score_terms{i}_{side}", (TERMS, P, T), BF16).ap() for side in range(2)]
                      for i in range(2)]
        self.bias_lines = [nc.dram_tensor(f"bias_lines{i}", (HEADS, P * 3 * P), F32).ap() for i in range(2)]
        self.dispatched = [nc.dram_tensor(f"dispatched{n}", (slots, D + 1), F32).ap()
                           for n, slots in enumerate((E * CAP0, E * CAP0, E * CAP3, E * CAP3))]
        self.returned = nc.dram_tensor("returned", (2 * TOKENS, D), F32).ap()
        self.untaken_written = [nc.alloc_semaphore(f"untaken_written{n}") for n in range(4)]
        self.returned_zeroed = nc.alloc_semaphore("returned_zeroed")


def program(nc, a, out, wanted=range(12)):
    g = Shared(nc, a)
    mixture = lambda n, name, layer, choices, cap, at, **more: moe_capacity(
        g, name, n, choices, cap, g.gates[:, at, :], a[layer + "_w1"], a[layer + "_b1"], a[layer + "_w2"], a[layer + "_b2"], **more)
    with ExitStack() as ctx:
        bias_kq = ctx.enter_context(nc.sbuf_tensor("bias_kq", [P, HEADS, 3, 2 * P], BF16))
        bias_qk = ctx.enter_context(nc.sbuf_tensor("bias_qk", [P, HEADS, 2 * P], F32))
        with ExitStack() as beside:
            bias = RelativeBias(g, beside, "bias", bias_kq, bias_qk)
            setup(g, bias)
            mixture(0, "moe0_0", "l0", 1, CAP0, 0, beside=bias)
        attention(g, "att0", 0, (bias_kq, bias_qk))
    mixture(1, "moe0_1", "l0", 1, CAP0, 0)
    clear_semaphores(g)
    ffn1(g, "ffn1_0")
    attention(g, "att1", 1)
    with nc.sbuf_tensor("products2", [P, 2, 4 * D], F32) as products:
        with ExitStack() as beside:
            ffn1(g, "ffn1_1", ExpertProducts(g, beside, "products2", products))
        clear_semaphores(g)
        ffn2(g, "ffn2_0", products)
        recurrence2(g, "rec2")
        ffn2(g, "ffn2_1", products)
    clear_semaphores(g)
    mixture(2, "moe3_0", "l3", 2, CAP3, 3, twice=True)
    attention(g, "att3", 3)
    mixture(3, "moe3_1", "l3", 2, CAP3, 3, last=True)
    store(g, out)


def store(g, out):
    nc = g.nc
    with ExitStack() as ctx:
        stored = ctx.enter_context(nc.semaphore("x_stored"))
        block = ctx.enter_context(nc.Block(no_gpsimd_drain=True))

        @block.sync
        def _(sp):
            sp.dma_start(out.rearrange("(i p) d -> p i d", p=P), g.x[:]).then_inc(stored, 16)
            sp.wait_ge(stored, 16)


def lay_out(i):
    import numpy as np
    t = lambda a: np.ascontiguousarray(np.asarray(a).T)
    n = lambda a: np.ascontiguousarray(np.asarray(a))
    by_chunk = lambda b: n(np.asarray(b).reshape(E * CH, P).T)
    dh = lambda w: n(np.asarray(w).reshape(HEADS, HD, -1).transpose(1, 0, 2).reshape(HEADS * HD, -1).T)
    dhb = lambda b: n(np.asarray(b).reshape(HEADS, HD).T.reshape(P, 1))
    ins = {"x": n(np.asarray(i["L0_attn_x"]).reshape(TOKENS, D))}
    ins["l0_gate"] = t(i["L0_ffn_gate_w"])
    ins["l3_gate"] = n(i["L3_ffn_wg"])
    for layer, f in (("l0", "L0_ffn"), ("l3", "L3_ffn")):
        ins[layer + "_w1"] = n(np.asarray(i[f + "_w1"]).reshape(E * P, HID))
        ins[layer + "_b1"] = by_chunk(i[f + "_b1"])
        ins[layer + "_w2"] = n(np.asarray(i[f + "_w2"]).reshape(E * HID, D))
        ins[layer + "_b2"] = n(i[f + "_b2"])
    for layer, w, bias, wo, bo in (("l0", "L0_attn_qkv_w", "L0_attn_qkv_b", "L0_attn_proj_w", "L0_attn_proj_b"),
                                   ("l3", "L3_attn_W_qkv", "L3_attn_b_qkv", "L3_attn_W_out", "L3_attn_b_out")):
        q, k, v = np.split(np.asarray(i[w]), 3)
        bq, bk, bv = np.split(np.asarray(i[bias]), 3)
        ins[layer + "_wq"], ins[layer + "_wk"], ins[layer + "_wv"] = dh(q), dh(k), t(v)
        ins[layer + "_bq"], ins[layer + "_bk"], ins[layer + "_bv"] = dhb(bq), dhb(bk), n(bv)
        ins[layer + "_wo"], ins[layer + "_bo"] = t(i[wo]), n(i[bo])
    ins["l3_gamma_beta"] = n(np.stack([np.asarray(i["L3_attn_ln_gamma"]), np.asarray(i["L3_attn_ln_beta"])], axis=1))
    ins["l0_rel"] = n(np.asarray(i["L0_attn_rel_pos_emb"])[P - 1:2 * P - 1])
    ins["l0_rel_back"] = n(np.asarray(i["L0_attn_rel_pos_emb"])[P - 1:2 * P - 1][::-1])
    ins["l1_gate"] = t(i["L1_ffn_gate_weight"])
    for m, shared in (("gate", "ws_gate"), ("up", "ws_up")):
        ins["l1_" + m + "_w"] = n(np.concatenate([np.asarray(i["L1_ffn_w_" + m]).reshape(-1, D).T,
                                                  np.asarray(i["L1_ffn_" + shared]).T], axis=1))
    ins["l1_down_w"] = n(np.concatenate([np.asarray(i["L1_ffn_w_down"]).transpose(0, 2, 1).reshape(-1, D),
                                         np.asarray(i["L1_ffn_ws_down"]).T], axis=0))
    ins["l1_wqk"] = n(np.concatenate([np.asarray(i["L1_attn_" + w]).T for w in ("Wq1", "Wk1", "Wq2", "Wk2", "Wv")], axis=1))
    ins["l1_wo"], ins["l1_bo"] = t(i["L1_attn_Wo"]), n(i["L1_attn_bo"])
    ins["l2_gate"] = t(i["L2_ffn_w_gate"])
    ins["l2_w_in"] = n(np.asarray(i["L2_ffn_w_in"]).reshape(E * HID, D))
    ins["l2_w_out"] = n(np.asarray(i["L2_ffn_w_out"]).transpose(0, 2, 1).reshape(E * HID, D))
    ins["l2_win"], ins["l2_wout"] = n(i["L2_attn_W_in"]), n(i["L2_attn_W_out"])
    ins["l2_bin"] = n(np.asarray(i["L2_attn_b_in"]).reshape(2, P).T)
    ins["l2_bout"] = n(i["L2_attn_b_out"])
    return ins


def kernel(**inputs):
    import concourse.bacc as bacc
    from concourse.bass_utils import run_bass_kernel_spmd
    arrays = lay_out(inputs)
    nc = bacc.Bacc("TRN2", target_bir_lowering=False, num_devices=1)
    a = {n: nc.dram_tensor(n, v.shape, F32, kind="ExternalInput").ap() for n, v in arrays.items()}
    out = nc.dram_tensor("x_out", (TOKENS, D), F32, kind="ExternalOutput").ap()
    program(nc, a, out)
    got = run_bass_kernel_spmd(nc, [arrays], core_ids=[0]).results[0]["x_out"]
    return got.reshape(B, T, D)
```

```python
from contextlib import ExitStack

import concourse.bass as bass
from concourse import mybir
from concourse.bass import IndirectOffsetOnAxis

F32 = mybir.dt.float32
BF16 = mybir.dt.bfloat16
U32 = mybir.dt.uint32
ALU = mybir.AluOpType
ACT = mybir.ActivationFunctionType
AX = mybir.AxisListType.X

P = 128
B, T, D = 4, 512, 128
TOKENS = B * T
TILES = TOKENS // P
GROUP = T // P
E = 8
HID = 512
CH = HID // P
HEADS, HD = 16, 8
EPS = 1e-5
CAP0 = -(-5 * TOKENS // (4 * E))
CAP3 = 2 * -(-TOKENS // E)
OUT_OF_BOUNDS = 1.0e6
MASKED = -1.0e30


def semaphores(g, name):
    def sem(n):
        g.spent.append(g.nc.alloc_semaphore(f"{name}_{n}"))
        return g.spent[-1]

    return sem


def clear_semaphores(g):
    g.nc.clear_and_free_semaphores(g.spent)
    g.nc.all_engine_barrier(sem_only=True)
    g.spent.clear()


class LayerNormSems:
    def __init__(self, sem, twice=False, gate=None):
        self.stats, self.moments, self.var_eps = sem("ln_stats"), sem("ln_moments"), sem("ln_var_eps")
        self.rstd, self.xn = sem("ln_rstd"), sem("ln_rows")
        self.xnt_psum, self.xnt = sem("ln_rows_transposed"), sem("ln_columns")
        self.twice = twice
        self.gate = gate
        if gate is not None:
            self.logits_psum, self.logits = sem("ln_logits_psum"), sem("ln_logits")
        if twice:
            self.outer = LayerNormSems(lambda n: sem("outer_" + n))
            self.summed = sem("ln_summed")


def ln_stats(g, v, s, b, src=None):
    nc = g.nc
    src = g.x if src is None else src
    tiles = range(GROUP * b, GROUP * (b + 1))
    for i in tiles:
        nc.vector.bn_stats(g.stats[:, i, :], src[:, i, 0:D]).then_inc(s.stats, 1)
    v.wait_ge(s.stats, GROUP * (b + 1))
    for i in tiles:
        nc.vector.bn_aggr(g.moments[:, i, :], g.stats[:, i, :]).then_inc(s.moments, 1)
    v.wait_ge(s.moments, GROUP * (b + 1))
    nc.vector.tensor_scalar(g.var_eps[:, GROUP * b:GROUP * (b + 1)],
                            g.moments[:, GROUP * b:GROUP * (b + 1), 1],
                            EPS, None, ALU.add).then_inc(s.var_eps, 1)


def ln_rstd(g, pool, s, b):
    cols = slice(GROUP * b, GROUP * (b + 1))
    pool.wait_ge(s.var_eps, b + 1)
    g.nc.gpsimd.tensor_tensor(g.rstd[:, cols], g.var_eps[:, cols], g.neg_half[:, cols],
                              ALU.pow).then_inc(s.rstd, 1)


def ln_rows(g, v, s, b, src=None):
    src = g.x if src is None else src
    v.wait_ge(s.rstd, b + 1)
    for i in range(GROUP * b, GROUP * (b + 1)):
        g.nc.vector.tensor_scalar(g.xn[:, i, 0:D], src[:, i, 0:D], g.moments[:, i, 0:1],
                                  g.rstd[:, i:i + 1], ALU.subtract, ALU.mult).then_inc(s.xn, 1)


def ln_outer(g, v, s, b):
    ln_rows(g, v, s.outer, b)
    v.wait_ge(s.outer.xn, GROUP * (b + 1))
    tiles = slice(GROUP * b, GROUP * (b + 1))
    g.nc.vector.tensor_tensor(g.x[:, tiles, :], g.x[:, tiles, :], g.xn[:, tiles, 0:D], ALU.add).then_inc(s.summed, 1)
    ln_stats(g, v, s, b, src=g.xn)


def ln_inner(g, v, s, b):
    v.wait_ge(s.summed, b + 1)
    ln_rows(g, v, s, b, src=g.xn)


def ln_transpose(g, pe, s, b, bank, one_bank=False):
    pe.wait_ge(s.xn, GROUP * (b + 1))
    if one_bank and b >= 1:
        pe.wait_ge(s.xnt if s.gate is None else s.logits, b)
    for j in range(GROUP):
        mm = g.nc.tensor.transpose(bank[:, j * P:(j + 1) * P], g.xn[:, GROUP * b + j, 0:D], g.ident[:])
    mm.then_inc(s.xnt_psum, 1)


def ln_columns(g, act, s, b, bank):
    act.wait_ge(s.xnt_psum, b + 1)
    dst = g.xnt[:, b * T:(b + 1) * T]
    if s.twice:
        g.nc.scalar.activation(dst, bank[:], ACT.Identity, bias=g.gamma_beta[:, 1:2], scale=g.gamma_beta[:, 0:1]
                               ).then_inc(s.xnt, 1)
    else:
        g.nc.scalar.copy(dst, bank[:]).then_inc(s.xnt, 1)


def ln_logits(g, pe, s, b, bank):
    if s.gate is None:
        return
    pe.wait_ge(s.xnt, b + 1)
    for j in range(GROUP):
        i = GROUP * b + j
        mm = g.nc.tensor.matmul(bank[:, j * E:(j + 1) * E], g.xnt[:, i * P:(i + 1) * P], s.gate, start=True, stop=True)
    mm.then_inc(s.logits_psum, 1)


def ln_copy_logits(g, act, s, b, bank):
    if s.gate is None:
        return
    act.wait_ge(s.logits_psum, b + 1)
    g.nc.scalar.copy(g.logits[:, GROUP * b:GROUP * (b + 1), :],
                     bank[:, 0:GROUP * E].rearrange("p (t e) -> p t e", e=E)).then_inc(s.logits, 1)


def ln_columns_and_logits(g, act, s, groups, banks):
    for b in groups:
        ln_columns(g, act, s, b, banks(b))
        if b - 1 in groups:
            ln_copy_logits(g, act, s, b - 1, banks(b - 1))
    ln_copy_logits(g, act, s, groups[-1], banks(groups[-1]))


def ln_transpose_and_logits(g, pe, s, groups, banks):
    for b in groups:
        ln_transpose(g, pe, s, b, banks(b))
        if b - 1 in groups:
            ln_logits(g, pe, s, b - 1, banks(b - 1))
    ln_logits(g, pe, s, groups[-1], banks(groups[-1]))


def write_untaken(g, sp, mixtures):
    for n in mixtures:
        rows = g.dispatched[n]
        sp.dma_start(rows.rearrange("(p j) d -> p j d", p=P),
                     g.untaken[:, None, :].to_broadcast([P, rows.shape[0] // P, D + 1])).then_inc(g.untaken_written[n], 16)


def setup(g, beside):
    nc = g.nc
    with ExitStack() as ctx:
        sem = semaphores(g, "setup")
        loaded = [sem(f"x_loaded{b}") for b in range(B)]
        small_loaded, made, ident_made, masked = sem("small_loaded"), sem("made"), sem("ident_made"), sem("masks")
        ln = LayerNormSems(sem, gate=g.gates[:, 0, :])
        block = ctx.enter_context(nc.Block(no_gpsimd_drain=True))

        @block.sync
        def _(sp):
            for b in range(B):
                sp.dma_start(g.x[:, GROUP * b:GROUP * (b + 1), :],
                             g.a["x"][b * T:(b + 1) * T, :].rearrange("(i p) d -> p i d", p=P)).then_inc(loaded[b], 16)
            for k, n in enumerate(("l0_gate", "l1_gate", "l2_gate", "l3_gate")):
                sp.dma_start(g.gates[:, k, :], g.a[n]).then_inc(small_loaded, 16)
            beside.load(sp)
            sp.dma_start(g.gamma_beta[:], g.a["l3_gamma_beta"]).then_inc(small_loaded, 16)
            sp.wait_ge(made, 2)
            write_untaken(g, sp, (0,))
            of_partition = g.returned.shape[0] // P
            sp.dma_start(g.returned.rearrange("(p j) d -> p j d", p=P),
                         g.untaken[:, None, 0:D].to_broadcast([P, of_partition, D])).then_inc(g.returned_zeroed, 16)
            sp.wait_ge(small_loaded, 16 * 5)

        @block.tensor
        def _(pe):
            pe.wait_ge(ident_made, 2)
            pe.wait_ge(small_loaded, 16 * 5)
            ln_transpose_and_logits(g, pe, ln, range(B), lambda b: g.bank[b])
            beside.turn(pe, g.bank[B])

        @block.scalar
        def _(act):
            ln_columns_and_logits(g, act, ln, range(B), lambda b: g.bank[b])
            beside.copy_lines(act, g.bank[B])
            beside.store_lines(act)

        @block.vector
        def _(v):
            nc.vector.memset(g.neg_half[:], -0.5)
            nc.vector.memset(g.untaken[:], 0.0).then_inc(made, 1)
            v.wait_ge(made, 1)
            nc.vector.memset(g.untaken[:, D:D + 1], OUT_OF_BOUNDS).then_inc(made, 1)
            for e in range(E):
                nc.vector.memset(g.rev[:, :, e], float(E - e))
            nc.vector.memset(g.scan_keep[:], 1.0).then_inc(made, 1)
            v.wait_ge(made, 3)
            nc.vector.memset(g.scan_keep[:, :, 0:1], 0.0)
            for b in range(B):
                v.wait_ge(loaded[b], 16)
                ln_stats(g, v, ln, b)
                if b >= 1:
                    ln_rows(g, v, ln, b - 1)
            ln_rows(g, v, ln, B - 1)
            beside.sum_heads(v)

        @block.gpsimd
        def _(pool):
            n = [0]

            def after(ins):
                n[0] += 1
                ins.then_inc(masked, 1)
                pool.wait_ge(masked, n[0])

            nc.gpsimd.memset(g.ident[:], 0.0).then_inc(ident_made, 1)
            pool.wait_ge(ident_made, 1)
            nc.gpsimd.affine_select(out=g.ident[:], in_=g.ident[:], compare_op=ALU.not_equal, fill=1.0,
                                    base=0, pattern=[[-1, P]], channel_multiplier=1).then_inc(ident_made, 1)
            pool.wait_ge(ident_made, 2)
            for b in range(B):
                ln_rstd(g, pool, ln, b)
            after(nc.gpsimd.tensor_copy(g.identb[:], g.ident[:]))
            after(nc.gpsimd.memset(g.flip[:], 0.0))
            after(nc.gpsimd.affine_select(out=g.flip[:], in_=g.flip[:], compare_op=ALU.not_equal, fill=1.0,
                                          base=1 - P, pattern=[[1, P]], channel_multiplier=1))
            after(nc.gpsimd.memset(g.onesb[:], 1.0))
            after(nc.gpsimd.affine_select(out=g.beforeb[:], in_=g.onesb[:], compare_op=ALU.is_ge, fill=0.0,
                                          base=-1, pattern=[[1, P]], channel_multiplier=-1))
            after(nc.gpsimd.iota(g.token_i[:], pattern=[[P, 2 * TILES]], base=0, channel_multiplier=1))
            after(nc.gpsimd.tensor_copy(g.token[:], g.token_i[:]))
            for t, base in ((g.head_selector, MAX_AT), (g.head_selector1, MAX_AT1)):
                after(nc.gpsimd.memset(t[:], 0.0))
                for part in range(PARTS):
                    after(nc.gpsimd.affine_select(out=t[:], in_=t[:], compare_op=ALU.not_equal, fill=1.0,
                                                  base=-(base + part * GH), pattern=[[-1, GH]], channel_multiplier=1))
            after(nc.gpsimd.memset(g.expert_selector[:], 0.0))
            chunks = g.expert_selector[:].rearrange("p c (h r) -> p c h r", h=2)
            for part in range(PARTS):
                after(nc.gpsimd.affine_select(out=chunks, in_=chunks, compare_op=ALU.not_equal, fill=1.0,
                                              base=-part * E, pattern=[[-2, E // 2], [-1, 2], [0, P // 2]], channel_multiplier=1))
            after(nc.gpsimd.memset(g.mask_kq[:], 0.0))
            after(nc.gpsimd.affine_select(out=g.mask_kq[:], in_=g.mask_kq[:], compare_op=ALU.is_ge, fill=MASKED,
                                          base=0, pattern=[[1, P]], channel_multiplier=-1))
            after(nc.gpsimd.memset(g.mask_qk[:], 0.0))
            after(nc.gpsimd.affine_select(out=g.mask_qk[:, T - P:T], in_=g.mask_qk[:, T - P:T],
                                          compare_op=ALU.is_ge, fill=MASKED,
                                          base=0, pattern=[[-1, P]], channel_multiplier=1))


def first_max(g, after, scores, best, work, onehot):
    v = g.nc.vector
    wide = [P, TILES, E]
    after(v.tensor_reduce(best, scores, axis=AX, op=ALU.max))
    after(v.tensor_tensor(work, scores, best[:, :, None].to_broadcast(wide), ALU.is_equal))
    after(v.tensor_tensor(work, work, g.rev[:, 0:TILES, :], ALU.mult))
    after(v.tensor_reduce(g.tie[:], work, axis=AX, op=ALU.max))
    after(v.tensor_tensor(onehot, work, g.tie[:, :, None].to_broadcast(wide), ALU.is_equal))


def moe_capacity(g, name, n, choices, cap, w1, b1, w2, b2, last=False, twice=False, gate=None, beside=None, prefetch=None):
    nc = g.nc
    slots = E * cap
    full, rest = cap // P, cap % P
    sizes = [P] * full + [rest] * (rest > 0)
    nt = len(sizes)
    picks = choices * TILES
    tile_loads = 1 + (rest > 0)
    dispatched = g.dispatched[n]
    with ExitStack() as ctx:
        sem = semaphores(g, name)
        sb = lambda n, shape, dt=F32: ctx.enter_context(nc.sbuf_tensor(f"{name}_{n}", shape, dt))
        ln = None if last else LayerNormSems(sem, twice, gate)
        small_loaded = sem("biases_loaded")
        w_loaded = [sem("w_loaded0"), sem("w_loaded1")]
        d_loaded = [sem("slots_loaded0"), sem("slots_loaded1")]
        ranks_done = sem("ranks_done")
        route, chosen, exp_in, exp_out = sem("route"), sem("chosen"), sem("exp_in"), sem("exp_out")
        slots_ready = sem("slots_ready")
        scattered = sem("scattered")
        dt_psum, dt_ready = sem("slots_transposed"), sem("slot_columns")
        h_psum, h_ready = sem("hidden_psum"), sem("hidden")
        o_psum, o_ready = sem("out_psum"), sem("out_rows")
        stored = [sem("stored0"), sem("stored1")]
        numbered, numbers_ready, added = sem("rows_numbered"), sem("slot_tokens"), sem("added")
        returned = [sem(f"rows_returned{b}") for b in range(B)]

        xn2 = sb("second_rows", [P, TILES, D + 1]) if choices == 2 else None
        b1_sb = sb("b1", [P, E * CH])
        b2_sb = sb("b2", [P, E, D])
        w1_sb = [sb(f"w1_{i}", [P, HID]) for i in range(2)]
        w2_sb = [sb(f"w2_{i}", [P, CH, D]) for i in range(2)]
        d_sb = [sb(f"slots_{i}", [P, nt, D + 1]) for i in range(2)]
        dt_sb = [sb(f"slot_columns_{i}", [P, cap]) for i in range(2)]
        h_sb = [sb(f"hidden_{i}", [P, CH, cap]) for i in range(2)]
        o_sb = [sb(f"out_{i}", [P, nt, D]) for i in range(2)]
        slot_token = [sb(f"slot_tokens_{i}", [P, nt], U32) for i in range(2)]
        logits = g.logits
        rest_logits = sb("rest_logits", [P, TILES, E])
        work = sb("work", [P, TILES, E])
        best = sb("best", [P, choices, TILES])
        onehot = sb("onehot", [P, choices, TILES, E])
        onehotb = sb("onehotb", [P, picks, E], BF16)
        expd = sb("expd", [P, TILES, E])
        gates = sb("gates", [P, choices, TILES])
        denom = sb("denom", [P, TILES])
        totals = sb("totals", [P, choices, E, TILES])
        running = sb("running", [P, choices, E, TILES])
        offset = sb("offset", [P, choices, E, TILES])
        rank_all = sb("rank_all", [P, picks, E])
        rank = sb("rank", [P, picks])
        base = sb("base", [P, picks])
        keep = sb("keep", [P, picks])
        slot = sb("slot", [P, picks])
        scatter_f = sb("scatter_f", [P, picks])
        kept_slot = sb("kept_slot", [P, picks])
        scatter_i = sb("scatter_i", [P, picks], U32)
        weight = sb("weight", [P, picks])
        back = sb("back", [P, picks, D])

        xnt_bank = [g.bank[0], g.bank[1]]
        beside_banks = (g.bank[6:8], g.bank[0:2])
        rank_bank, total_bank = g.bank[2:4], g.bank[4:6]
        h_bank = g.bank[2:6]
        o_bank = g.bank[6:8]
        block = ctx.enter_context(nc.Block(no_gpsimd_drain=True))

        @block.sync
        def _(sp):
            if prefetch:
                prefetch.load(sp)
            sp.dma_start(b1_sb[:], b1).then_inc(small_loaded, 16)
            sp.dma_start(b2_sb[:], b2.rearrange("e d -> (e d)").partition_broadcast(P)).then_inc(small_loaded, 16)

            def load_weights(e, i):
                sp.dma_start(w1_sb[i][:], w1[bass.ds(e * P, P), :]).then_inc(w_loaded[i], 16)
                sp.dma_start(w2_sb[i][:], w2[bass.ds(e * HID, HID), :].rearrange("(c p) d -> p c d", p=P)
                             ).then_inc(w_loaded[i], 16)

            def load_slots(e, i):
                sp.dma_start(d_sb[i][:, 0:full, :],
                             dispatched[bass.ds(e * cap, full * P), :].rearrange("(t p) d -> p t d", p=P)
                             ).then_inc(d_loaded[i], 16)
                if rest:
                    sp.dma_start(d_sb[i][0:rest, full, :], dispatched[bass.ds(e * cap + full * P, rest), :]
                                 ).then_inc(d_loaded[i], 16)

            for i in range(2):
                load_weights(i, i)
            sp.wait_ge(scattered, 16 * picks)
            for i in range(2):
                load_slots(i, i)
            with sp.Fori(0, E // 2 - 1) as k:
                for i in range(2):
                    sp.wait_ge(dt_psum, 2 * k + i + 1)
                    sp.wait_ge(numbers_ready, 2 * k + i + 1)
                    load_slots(2 * k + i + 2, i)
                    sp.wait_ge(o_psum, 2 * k + i + 1)
                    load_weights(2 * k + i + 2, i)
            for i in range(2):
                sp.wait_ge(stored[i], 16 * nt * (E // 2))
            for b in range(B):
                for c in range(choices):
                    at = c * TILES + GROUP * b
                    sp.dma_start(back[:, at:at + GROUP, :],
                                 g.returned[c * TOKENS + b * T:c * TOKENS + (b + 1) * T, :].rearrange("(j p) d -> p j d", p=P)
                                 ).then_inc(returned[b], 16)

        @block.tensor
        def _(pe):
            for c in range(choices):
                pe.wait_ge(chosen, c + 1)
                hot = onehotb[:, c * TILES:(c + 1) * TILES, :].rearrange("p k e -> p (k e)")
                nc.tensor.matmul(rank_bank[c][:, 0:TILES * E], g.beforeb[:], hot, start=True, stop=True)
                nc.tensor.matmul(total_bank[c][:, 0:TILES * E], g.onesb[:], hot, start=True, stop=True
                                 ).then_inc(ranks_done, 1)
            pe.wait_ge(slots_ready, choices)
            if beside:
                beside.flip(pe, beside_banks)

            def turn_slots(e, i, nth):
                pe.wait_ge(d_loaded[i], 16 * tile_loads * nth)
                for t, n in enumerate(sizes):
                    mm = nc.tensor.transpose(xnt_bank[i][:, t * P:t * P + n], d_sb[i][0:n, t, 0:D], g.ident[0:n, 0:n])
                mm.then_inc(dt_psum, 1)

            def hidden(e, i, nth):
                pe.wait_ge(dt_ready, e + 1)
                pe.wait_ge(w_loaded[i], 32 * nth)
                for c in range(CH):
                    nc.tensor.matmul(h_bank[c][:, 0:cap], w1_sb[i][:, c * P:(c + 1) * P], dt_sb[i][:],
                                     start=True, stop=True).then_inc(h_psum, 1)

            def output(e, i):
                pe.wait_ge(h_ready, CH * (e + 1))
                for t, n in enumerate(sizes):
                    for c in range(CH):
                        mm = nc.tensor.matmul(o_bank[i][0:n, t * D:(t + 1) * D],
                                              h_sb[i][:, c, t * P:t * P + n], w2_sb[i][:, c, :],
                                              start=(c == 0), stop=(c == CH - 1))
                mm.then_inc(o_psum, 1)

            if beside:
                pe.wait_ge(beside.copied, HEADS // 2)
                pe.wait_ge(beside.split_done, HEADS // 2)
            turn_slots(0, 0, 1)
            with pe.Fori(0, E // 2 - 1) as k:
                for i in range(2):
                    hidden(2 * k + i, i, k + 1)
                    turn_slots(2 * k + i + 1, 1 - i, k + 1 + i)
                    pe.wait_ge(o_ready, 2 * k + i + 1)
                    output(2 * k + i, i)
            for e in (E - 2, E - 1):
                hidden(e, e % 2, E // 2)
                if e == E - 2:
                    turn_slots(E - 1, 1, E // 2)
                pe.wait_ge(o_ready, e + 1)
                output(e, e % 2)
            if not last:
                ln_transpose_and_logits(g, pe, ln, range(B), lambda b: g.bank[2 + b])

        @block.scalar
        def _(act):
            if beside:
                beside.load_tiles(act)
            nc.scalar.copy(g.xn[:, :, D], g.token[:, 0:TILES]).then_inc(numbered, 1)
            if choices == 2:
                nc.scalar.copy(xn2[:, :, 0:D], g.xn[:, :, 0:D])
                nc.scalar.copy(xn2[:, :, D], g.token[:, TILES:2 * TILES]).then_inc(numbered, 1)
            act.wait_ge(exp_in, 1)
            nc.scalar.activation(expd[:] if choices == 1 else expd[:, :, 0], expd[:] if choices == 1 else expd[:, :, 0],
                                 ACT.Exp).then_inc(exp_out, 1)
            if beside:
                beside.copy(act, beside_banks)
            act.wait_ge(small_loaded, 32)

            def copy_columns(e, i):
                act.wait_ge(dt_psum, e + 1)
                nc.scalar.copy(dt_sb[i][:], xnt_bank[i][:, 0:cap]).then_inc(dt_ready, 1)

            def hidden(e, i):
                for c in range(CH):
                    act.wait_ge(h_psum, CH * e + c + 1)
                    nc.scalar.activation(h_sb[i][:, c, :], h_bank[c][:, 0:cap], ACT.Relu,
                                         bias=b1_sb[:, bass.ds(e * CH + c, 1)]).then_inc(h_ready, 1)

            copy_columns(0, 0)
            with act.Fori(0, E // 2 - 1) as k:
                for i in range(2):
                    hidden(2 * k + i, i)
                    copy_columns(2 * k + i + 1, 1 - i)
            hidden(E - 2, 0)
            copy_columns(E - 1, 1)
            hidden(E - 1, 1)
            if not last:
                ln_columns_and_logits(g, act, ln, range(B), lambda b: g.bank[2 + b])

        @block.vector
        def _(v):
            n = [0]

            def after(ins):
                n[0] += 1
                ins.then_inc(route, 1)
                v.wait_ge(route, n[0])

            nc.vector.memset(g.spare[:], 0.0).then_inc(o_ready, 2)
            by_expert = lambda t, c: t[:, c, :, :].rearrange("p e k -> p k e")

            def choose(c):
                scores = logits if c == 0 else rest_logits
                if c == 1:
                    after(nc.vector.scalar_tensor_tensor(rest_logits[:], onehot[:, 0, :, :], MASKED, logits[:],
                                                         ALU.mult, ALU.add))
                first_max(g, after, scores[:], best[:, c, :], work[:], onehot[:, c, :, :])
                nc.vector.tensor_copy(onehotb[:, c * TILES:(c + 1) * TILES, :], onehot[:, c, :, :]).then_inc(chosen, 1)

            def place(c):
                mine = slice(c * TILES, (c + 1) * TILES)
                after(nc.vector.tensor_tensor(rank_all[:, mine, :], onehot[:, c, :, :], g.rev[:, 0:TILES, :], ALU.mult))
                after(nc.vector.tensor_reduce(base[:, mine], rank_all[:, mine, :], axis=AX, op=ALU.add))
                after(nc.vector.tensor_scalar(base[:, mine], base[:, mine], -float(cap), float(E * cap), ALU.mult, ALU.add))
                v.wait_ge(ranks_done, c + 1)
                after(nc.vector.tensor_copy(by_expert(totals, c),
                                            total_bank[c][:, 0:TILES * E].rearrange("p (k e) -> p k e", e=E)))
                after(nc.vector.tensor_tensor_scan(running[:, c, :, :].rearrange("p e k -> p (e k)"),
                                                   g.scan_keep[:].rearrange("p e k -> p (e k)"),
                                                   totals[:, c, :, :].rearrange("p e k -> p (e k)"), 0.0, ALU.mult, ALU.add))
                after(nc.vector.tensor_tensor(offset[:, c, :, :], running[:, c, :, :], totals[:, c, :, :], ALU.subtract))
                if c == 1:
                    after(nc.vector.tensor_tensor(offset[:, 1, :, :], offset[:, 1, :, :],
                                                  running[:, 0, :, TILES - 1:TILES].to_broadcast([P, E, TILES]), ALU.add))
                after(nc.vector.tensor_tensor(rank_all[:, mine, :], rank_bank[c][:, 0:TILES * E].rearrange("p (k e) -> p k e", e=E),
                                              by_expert(offset, c), ALU.add))
                after(nc.vector.tensor_tensor(rank_all[:, mine, :], rank_all[:, mine, :], onehot[:, c, :, :], ALU.mult))
                after(nc.vector.tensor_reduce(rank[:, mine], rank_all[:, mine, :], axis=AX, op=ALU.add))
                after(nc.vector.tensor_tensor(slot[:, mine], base[:, mine], rank[:, mine], ALU.add))
                after(nc.vector.tensor_scalar(keep[:, mine], rank[:, mine], float(cap), None, ALU.is_lt))
                after(nc.vector.tensor_scalar(scatter_f[:, mine], keep[:, mine], -OUT_OF_BOUNDS, OUT_OF_BOUNDS, ALU.mult, ALU.add))
                after(nc.vector.tensor_tensor(kept_slot[:, mine], slot[:, mine], keep[:, mine], ALU.mult))
                after(nc.vector.tensor_tensor(scatter_f[:, mine], scatter_f[:, mine], kept_slot[:, mine], ALU.add))
                nc.vector.tensor_copy(scatter_i[:, mine], scatter_f[:, mine]).then_inc(slots_ready, 1)

            for c in range(choices):
                choose(c)
                place(c)
            if choices == 1:
                nc.vector.tensor_tensor(expd[:], logits[:], best[:, 0, :, None].to_broadcast([P, TILES, E]),
                                        ALU.subtract).then_inc(exp_in, 1)
                v.wait_ge(exp_out, 1)
                after(nc.vector.tensor_reduce(denom[:], expd[:], axis=AX, op=ALU.add))
                after(nc.vector.reciprocal(gates[:, 0, :], denom[:]))
            else:
                nc.vector.tensor_tensor(expd[:, :, 0], best[:, 1, :], best[:, 0, :], ALU.subtract).then_inc(exp_in, 1)
                v.wait_ge(exp_out, 1)
                after(nc.vector.tensor_scalar(denom[:], expd[:, :, 0], 1.0, None, ALU.add))
                after(nc.vector.reciprocal(gates[:, 0, :], denom[:]))
                after(nc.vector.tensor_tensor(gates[:, 1, :], expd[:, :, 0], gates[:, 0, :], ALU.mult))
            after(nc.vector.scalar_tensor_tensor(weight[:], gates[:].rearrange("p k t -> p (k t)"), 0.5, keep[:],
                                                 ALU.mult, ALU.mult))
            if beside:
                beside.split(v, beside_banks)
            v.wait_ge(small_loaded, 32)
            for e in range(E):
                i, nth = e % 2, e // 2 + 1
                if e >= 2:
                    v.wait_ge(stored[i], 16 * nt * (nth - 1))
                v.wait_ge(d_loaded[i], 16 * tile_loads * nth)
                if rest:
                    nc.vector.tensor_copy(slot_token[i][0:rest, full:nt], d_sb[i][0:rest, full:nt, D])
                nc.vector.tensor_copy(slot_token[i][:, 0:full], d_sb[i][:, 0:full, D]).then_inc(numbers_ready, 1)
                v.wait_ge(o_psum, e + 1)
                if rest:
                    nc.vector.tensor_tensor(o_sb[i][0:rest, full, :], o_bank[i][0:rest, full * D:(full + 1) * D],
                                            b2_sb[0:rest, e, :], ALU.add)
                nc.vector.tensor_tensor(o_sb[i][:, 0:full, :], o_bank[i][:, 0:full * D].rearrange("p (t d) -> p t d", d=D),
                                        b2_sb[:, e:e + 1, :].to_broadcast([P, full, D]), ALU.add).then_inc(o_ready, 1)

            def add_rows(b):
                v.wait_ge(returned[b], 16 * choices)
                for c in range(choices):
                    if c:
                        v.wait_ge(added, (choices * b + c) * GROUP)
                    for j in range(GROUP * b, GROUP * (b + 1)):
                        k = c * TILES + j
                        nc.vector.scalar_tensor_tensor(g.x[:, j, :], back[:, k, :], weight[:, k:k + 1],
                                                       g.x[:, j, :], ALU.mult, ALU.add).then_inc(added, 1)

            for b in range(B + 2):
                if b < B:
                    add_rows(b)
                    if not last:
                        v.wait_ge(added, choices * GROUP * (b + 1))
                        ln_stats(g, v, ln.outer if twice else ln, b)
                if twice:
                    if 0 <= b - 1 < B:
                        ln_outer(g, v, ln, b - 1)
                    if 0 <= b - 2 < B:
                        ln_inner(g, v, ln, b - 2)
                elif not last and 0 <= b - 1 < B:
                    ln_rows(g, v, ln, b - 1)

        @block.gpsimd
        def _(pool):
            pool.wait_ge(g.untaken_written[n], 16)
            pool.wait_ge(numbered, choices)
            for k in range(picks):
                pool.wait_ge(slots_ready, k // TILES + 1)
                nc.gpsimd.indirect_dma_start(
                    out=dispatched[0:slots, :], out_offset=IndirectOffsetOnAxis(ap=scatter_i[:, k:k + 1], axis=0),
                    in_=(g.xn, xn2)[k // TILES][:, k % TILES, :], in_offset=None,
                    bounds_check=slots - 1, oob_is_err=False).then_inc(scattered, 16)
            pool.wait_ge(g.returned_zeroed, 16)
            for e in range(E):
                pool.wait_ge(o_ready, e + 3)
                for t, m in enumerate(sizes):
                    nc.gpsimd.indirect_dma_start(
                        out=g.returned[0:choices * TOKENS, :],
                        out_offset=IndirectOffsetOnAxis(ap=slot_token[e % 2][0:m, t:t + 1], axis=0),
                        in_=o_sb[e % 2][0:m, t, :], in_offset=None,
                        bounds_check=choices * TOKENS - 1, oob_is_err=False).then_inc(stored[e % 2], 16)
            if not last:
                for b in range(B + 1):
                    if b < B:
                        ln_rstd(g, pool, ln.outer if twice else ln, b)
                    if twice and b >= 1:
                        ln_rstd(g, pool, ln, b - 1)


def ffn1(g, name, gate=None, beside=None, prefetch=None):
    nc, a = g.nc, g.a
    routed, chunks = 4, 5
    wide = chunks * P
    with ExitStack() as ctx:
        sem = semaphores(g, name)
        sb = lambda n, shape, dt=F32: ctx.enter_context(nc.sbuf_tensor(f"{name}_{n}", shape, dt))
        ln = LayerNormSems(sem, gate=gate)
        loaded = sem("weights_loaded")
        scores_done, route = sem("scores_done"), sem("route")
        weights_ready, turned, columns_ready = sem("combine_ready"), sem("combine_turned"), sem("combine_columns")
        g_psum, u_psum, cb_psum, y_psum = sem("gate_psum"), sem("up_psum"), sem("combine_psum"), sem("y_psum")
        silu_done, gated, hidden, summed = sem("silu_done"), sem("gated"), sem("hidden"), sem("summed")

        xnt = g.xnt
        wg_sb, wu_sb = sb("wg", [P, wide]), sb("wu", [P, wide])
        wd_sb = sb("wd", [P, chunks, D])
        scores, others, work = (sb(n, [P, TILES, E]) for n in ("scores", "others", "work"))
        best = sb("best", [P, 2, TILES])
        onehot = sb("onehot", [P, 2, TILES, E])
        denom = sb("denom", [P, TILES])
        combine = sb("combine", [P, TILES, E])
        combine_parts = sb("combine_parts", [P, TILES, P], BF16)
        combine_t = sb("combine_t", [P, TOKENS], BF16)
        silu = sb("silu", [P, 2, T])
        prod = sb("prod", [P, 2, T])
        hid = sb("hid", [P, 2, chunks, T])

        xnt_bank, turn_bank = g.bank[0], g.bank[1]
        g_bank, u_bank = g.bank[2:4], g.bank[4:6]
        cb_bank, y_bank = g.bank[6], g.bank[7]
        units = [(b, c) for b in range(B) for c in range(chunks)]
        block = ctx.enter_context(nc.Block(no_gpsimd_drain=True))

        @block.sync
        def _(sp):
            sp.dma_start(wg_sb[:], a["l1_gate_w"]).then_inc(loaded, 16)
            sp.dma_start(wu_sb[:], a["l1_up_w"]).then_inc(loaded, 16)
            sp.dma_start(wd_sb[:], a["l1_down_w"].rearrange("(c p) d -> p c d", p=P)).then_inc(loaded, 16)
            if beside:
                beside.load(sp)
            if prefetch:
                prefetch.load(sp)

        @block.tensor
        def _(pe):
            pe.wait_ge(loaded, 48)

            def down(b):
                pe.wait_ge(hidden, chunks * (b + 1))
                if b >= 1:
                    pe.wait_ge(summed, b)
                for i in range(GROUP):
                    for c in range(chunks):
                        mm = nc.tensor.matmul(y_bank[:, i * D:(i + 1) * D], hid[:, b % 2, c, i * P:(i + 1) * P],
                                              wd_sb[:, c, :], start=(c == 0), stop=(c == chunks - 1))
                mm.then_inc(y_psum, 1)

            def gate_up(k):
                b, c = units[k]
                columns = xnt[:, b * T:(b + 1) * T]
                if k >= 2:
                    pe.wait_ge(silu_done, k - 1)
                    pe.wait_ge(gated, k - 1)
                nc.tensor.matmul(g_bank[k % 2][:], wg_sb[:, c * P:(c + 1) * P], columns,
                                 start=True, stop=True).then_inc(g_psum, 1)
                nc.tensor.matmul(u_bank[k % 2][:], wu_sb[:, c * P:(c + 1) * P], columns,
                                 start=True, stop=True).then_inc(u_psum, 1)

            gate_up(0)
            gate_up(1)
            pe.wait_ge(weights_ready, 2)
            for i in range(TILES):
                if i == 8:
                    pe.wait_ge(columns_ready, 1)
                mm = nc.tensor.transpose(turn_bank[:].bitcast(BF16)[:, (i % 8) * P:(i % 8 + 1) * P],
                                         combine_parts[:, i, :], g.identb[:])
                if i % 8 == 7:
                    mm.then_inc(turned, 1)
            for k, (b, c) in enumerate(units):
                if 2 <= k + 1 < len(units):
                    gate_up(k + 1)
                if c < routed:
                    pe.wait_ge(columns_ready, 1 + b // 2)
                    if k >= 1:
                        pe.wait_ge(hidden, k)
                    nc.tensor.matmul(cb_bank[:], g.expert_selector[:, c, :], combine_t[:, b * T:(b + 1) * T],
                                     start=True, stop=True).then_inc(cb_psum, 1)
                if beside and c == 2 and b in (1, 2):
                    beside.multiply(pe, turn_bank, b - 1)
                if c == 1 and b >= 1:
                    down(b - 1)
                if c == 0 and b >= 2:
                    ln_transpose(g, pe, ln, b - 2, xnt_bank, one_bank=True)
                if c == 2 and b >= 2:
                    ln_logits(g, pe, ln, b - 2, xnt_bank)
            ln_transpose(g, pe, ln, B - 2, xnt_bank, one_bank=True)
            down(B - 1)
            ln_logits(g, pe, ln, B - 2, xnt_bank)
            ln_transpose(g, pe, ln, B - 1, xnt_bank, one_bank=True)
            ln_logits(g, pe, ln, B - 1, xnt_bank)

        @block.scalar
        def _(act):
            nc.scalar.activation(scores[:], g.logits[:], ACT.Sigmoid).then_inc(scores_done, 1)

            def copy_combine(half):
                act.wait_ge(turned, half + 1)
                nc.scalar.copy(combine_t[:, half * 2 * T:(half + 1) * 2 * T], turn_bank[:].bitcast(BF16)
                               ).then_inc(columns_ready, 1)

            for k, (b, c) in enumerate(units):
                act.wait_ge(g_psum, k + 1)
                if k >= 2:
                    act.wait_ge(gated, k - 1)
                nc.scalar.activation(silu[:, k % 2, :], g_bank[k % 2][:], ACT.Silu).then_inc(silu_done, 1)
                if beside and c == 3 and b in (1, 2):
                    beside.copy(act, turn_bank, b - 1)
                if k == 1:
                    copy_combine(0)
                    copy_combine(1)
                if c == 1 and b >= 2:
                    ln_columns(g, act, ln, b - 2, xnt_bank)
                if c == 3 and b >= 2:
                    ln_copy_logits(g, act, ln, b - 2, xnt_bank)
            ln_columns(g, act, ln, B - 2, xnt_bank)
            ln_copy_logits(g, act, ln, B - 2, xnt_bank)
            ln_columns(g, act, ln, B - 1, xnt_bank)
            ln_copy_logits(g, act, ln, B - 1, xnt_bank)

        @block.vector
        def _(v):
            n = [0]

            def after(ins):
                n[0] += 1
                ins.then_inc(route, 1)
                v.wait_ge(route, n[0])

            nc.vector.memset(combine_parts[:].bitcast(F32), 0.0).then_inc(weights_ready, 1)
            v.wait_ge(scores_done, 1)
            first_max(g, after, scores[:], best[:, 0, :], work[:], onehot[:, 0, :, :])
            after(nc.vector.scalar_tensor_tensor(others[:], onehot[:, 0, :, :], MASKED, scores[:], ALU.mult, ALU.add))
            first_max(g, after, others[:], best[:, 1, :], work[:], onehot[:, 1, :, :])
            after(nc.vector.tensor_tensor(denom[:], best[:, 0, :], best[:, 1, :], ALU.add))
            after(nc.vector.tensor_scalar(denom[:], denom[:], 1e-20, None, ALU.add))
            after(nc.vector.reciprocal(denom[:], denom[:]))
            after(nc.vector.tensor_tensor(work[:], onehot[:, 0, :, :], onehot[:, 1, :, :], ALU.add))
            after(nc.vector.scalar_tensor_tensor(work[:], scores[:], 2.5, work[:], ALU.mult, ALU.mult))
            after(nc.vector.tensor_tensor(combine[:], work[:], denom[:, :, None].to_broadcast([P, TILES, E]), ALU.mult))
            part = lambda k: combine_parts[:, :, k * E:(k + 1) * E]
            v.wait_ge(weights_ready, 1)
            after(nc.vector.tensor_copy(part(0), combine[:]))
            after(nc.vector.tensor_tensor(combine[:], combine[:], part(0), ALU.subtract))
            after(nc.vector.tensor_copy(part(1), combine[:]))
            nc.vector.tensor_tensor(part(2), combine[:], part(1), ALU.subtract).then_inc(weights_ready, 1)

            def add(b):
                v.wait_ge(y_psum, b + 1)
                rows = g.x[:, GROUP * b:GROUP * (b + 1), :].rearrange("p t d -> p (t d)")
                nc.vector.scalar_tensor_tensor(rows, y_bank[:], 0.5, rows, ALU.mult, ALU.add).then_inc(summed, 1)
                v.wait_ge(summed, b + 1)

            m = 0
            for k, (b, c) in enumerate(units):
                v.wait_ge(silu_done, k + 1)
                v.wait_ge(u_psum, k + 1)
                dst = hid[:, b % 2, c, :]
                if c == 0 and b >= 2:
                    v.wait_ge(y_psum, b - 1)
                if c < routed:
                    if k >= 2:
                        v.wait_ge(hidden, k - 1)
                    nc.vector.tensor_tensor(prod[:, k % 2, :], silu[:, k % 2, :], u_bank[k % 2][:],
                                            ALU.mult).then_inc(gated, 1)
                    m += 1
                    v.wait_ge(gated, k + 1)
                    v.wait_ge(cb_psum, m)
                    nc.vector.tensor_tensor(dst, prod[:, k % 2, :], cb_bank[:], ALU.mult).then_inc(hidden, 1)
                else:
                    nc.vector.tensor_tensor(dst, silu[:, k % 2, :], u_bank[k % 2][:], ALU.mult).then_inc(hidden, 1)
                    nc.vector.memset(g.spare[:], 0.0).then_inc(gated, 1)
                if c == 2 and b >= 1:
                    add(b - 1)
                if c == 3 and b >= 1:
                    ln_stats(g, v, ln, b - 1)
                if c == 4 and b >= 1:
                    ln_rows(g, v, ln, b - 1)
            add(B - 1)
            ln_stats(g, v, ln, B - 1)
            ln_rows(g, v, ln, B - 1)

        @block.gpsimd
        def _(pool):
            for b in range(B):
                ln_rstd(g, pool, ln, b)


class ExpertProducts:
    def __init__(self, g, ctx, name, products):
        sem = semaphores(g, name)
        self.g, self.products = g, products
        self.loaded = [sem(f"loaded{i}") for i in range(2)]
        self.product, self.copied = sem("product"), sem("copied")
        self.w_in = ctx.enter_context(g.nc.sbuf_tensor(f"{name}_in", [P, 2, 4 * CH, D], F32))
        self.w_out = ctx.enter_context(g.nc.sbuf_tensor(f"{name}_out", [P, 2, 4 * CH, D], F32))

    def load(self, sp):
        a = self.g.a
        for i in range(2):
            rows = slice(i * 4 * HID, (i + 1) * 4 * HID)
            for dst, src in ((self.w_in, a["l2_w_in"]), (self.w_out, a["l2_w_out"])):
                sp.dma_start(dst[:, i, :, :], src[rows, :].rearrange("(c p) d -> p c d", p=P)).then_inc(self.loaded[i], 16)

    def multiply(self, pe, bank, i):
        pe.wait_ge(self.loaded[i], 32)
        if i >= 1:
            pe.wait_ge(self.copied, i)
        for e in range(4):
            for c in range(CH):
                mm = self.g.nc.tensor.matmul(bank[:, e * D:(e + 1) * D], self.w_in[:, i, e * CH + c, :],
                                             self.w_out[:, i, e * CH + c, :], start=(c == 0), stop=(c == CH - 1))
        mm.then_inc(self.product, 1)

    def copy(self, act, bank, i):
        act.wait_ge(self.product, i + 1)
        self.g.nc.scalar.copy(self.products[:, i, :], bank[:]).then_inc(self.copied, 1)


def ffn2(g, name, products, gate=None):
    nc, a = g.nc, g.a
    with ExitStack() as ctx:
        sem = semaphores(g, name)
        sb = lambda n, shape, dt=F32: ctx.enter_context(nc.sbuf_tensor(f"{name}_{n}", shape, dt))
        ln = LayerNormSems(sem, gate=gate)
        route, partial = sem("route"), sem("partial_sums")
        exp_in, exp_out, y_psum, added = sem("exp_in"), sem("exp_out"), sem("y_psum"), sem("added")
        xnt, logits = g.xnt, g.logits
        others, work = sb("others", [P, TILES, E]), sb("work", [P, TILES, E])
        best = sb("best", [P, 2, TILES])
        onehot = sb("onehot", [P, 2, TILES, E])
        delta, denom = sb("delta", [P, TILES]), sb("denom", [P, TILES])
        gates = sb("gates", [P, 2, TILES])
        weight = sb("weight", [P, TILES, E])
        units = [(pair + i, half) for pair in range(0, TILES, 2) for half in range(2) for i in range(2)]
        y_bank, xnt_bank = g.bank[0:7], g.bank[7]
        Y = len(y_bank)
        block = ctx.enter_context(nc.Block(no_gpsimd_drain=True))

        @block.tensor
        def _(pe):
            for k, (i, half) in enumerate(units):
                if k >= Y:
                    pe.wait_ge(added, k - Y + 1)
                nc.tensor.matmul(y_bank[k % Y][:], xnt[:, i * P:(i + 1) * P], products[:, half, :],
                                 start=True, stop=True).then_inc(y_psum, 1)
                b, at = divmod(k, 2 * GROUP)
                if at == 5 and b >= 1:
                    ln_transpose(g, pe, ln, b - 1, xnt_bank, one_bank=True)
                if at == 7 and b >= 1:
                    ln_logits(g, pe, ln, b - 1, xnt_bank)
            ln_transpose(g, pe, ln, B - 1, xnt_bank, one_bank=True)
            ln_logits(g, pe, ln, B - 1, xnt_bank)

        @block.scalar
        def _(act):
            act.wait_ge(exp_in, 1)
            nc.scalar.activation(delta[:], delta[:], ACT.Exp).then_inc(exp_out, 1)
            for b in range(B):
                ln_columns(g, act, ln, b, xnt_bank)
                ln_copy_logits(g, act, ln, b, xnt_bank)

        @block.vector
        def _(v):
            n = [0]

            def after(ins):
                n[0] += 1
                ins.then_inc(route, 1)
                v.wait_ge(route, n[0])

            first_max(g, after, logits[:], best[:, 0, :], work[:], onehot[:, 0, :, :])
            after(nc.vector.scalar_tensor_tensor(others[:], onehot[:, 0, :, :], MASKED, logits[:], ALU.mult, ALU.add))
            first_max(g, after, others[:], best[:, 1, :], work[:], onehot[:, 1, :, :])
            nc.vector.tensor_tensor(delta[:], best[:, 1, :], best[:, 0, :], ALU.subtract).then_inc(exp_in, 1)
            v.wait_ge(exp_out, 1)
            after(nc.vector.tensor_scalar(denom[:], delta[:], 1.0, None, ALU.add))
            after(nc.vector.reciprocal(gates[:, 0, :], denom[:]))
            after(nc.vector.tensor_tensor(gates[:, 1, :], delta[:], gates[:, 0, :], ALU.mult))
            spread = lambda c: gates[:, c, :, None].to_broadcast([P, TILES, E])
            after(nc.vector.scalar_tensor_tensor(work[:], onehot[:, 0, :, :], 0.5, spread(0), ALU.mult, ALU.mult))
            after(nc.vector.scalar_tensor_tensor(others[:], onehot[:, 1, :, :], 0.5, spread(1), ALU.mult, ALU.mult))
            after(nc.vector.tensor_tensor(weight[:], work[:], others[:], ALU.add))
            sums = 0
            for k in range(0, len(units), 2):
                for e in range(GROUP):
                    for j in range(2):
                        i, half = units[k + j]
                        if e == 0:
                            v.wait_ge(y_psum, k + j + 1)
                        if e or half:
                            v.wait_ge(partial, sums - 1)
                        nc.vector.scalar_tensor_tensor(g.x[:, i, :], y_bank[(k + j) % Y][:, e * D:(e + 1) * D],
                                                       weight[:, i, half * GROUP + e:half * GROUP + e + 1], g.x[:, i, :],
                                                       ALU.mult, ALU.add).then_inc(partial, 1)
                        sums += 1
                v.wait_ge(partial, sums)
                nc.vector.memset(g.spare[:], 0.0).then_inc(added, 2)
                b, at = divmod(k, 2 * GROUP)
                if at == 6:
                    ln_stats(g, v, ln, b)
                elif at == 0 and b >= 1:
                    ln_rows(g, v, ln, b - 1)
            ln_rows(g, v, ln, B - 1)

        @block.gpsimd
        def _(pool):
            for b in range(B):
                ln_rstd(g, pool, ln, b)


def recurrence2(g, name, gate):
    nc, a = g.nc, g.a
    with ExitStack() as ctx:
        sem = semaphores(g, name)
        sb = lambda n, shape, dt=F32: ctx.enter_context(nc.sbuf_tensor(f"{name}_{n}", shape, dt))
        ln = LayerNormSems(sem, gate=gate)
        loaded, proj, sig, step = sem("weights_loaded"), sem("projected"), sem("sigmoids"), sem("step")
        used, scanned, y_psum, added = sem("banks_used"), sem("scanned"), sem("y_psum"), sem("added")
        xnt = g.xnt
        win, wout = sb("win", [P, 2 * D]), sb("wout", [P, D])
        bin_sb, bout = sb("bin", [P, 2]), sb("bout", [P, D])
        sg, sh = sb("sig_gate", [P, 2, T]), sb("sig_hidden", [P, 2, T])
        silu, drive, states = sb("silu", [P, 2, T]), sb("drive", [P, 2, T]), sb("states", [P, 2, T])
        out = sb("out", [P, T])
        decay = sb("decay", [P, T])
        xnt_bank, gate_bank, hid_bank, y_bank = g.bank[0:2], g.bank[2:4], g.bank[4:6], g.bank[6:8]
        block = ctx.enter_context(nc.Block(no_gpsimd_drain=True))

        @block.sync
        def _(sp):
            sp.dma_start(win[:], a["l2_win"]).then_inc(loaded, 16)
            sp.dma_start(wout[:], a["l2_wout"]).then_inc(loaded, 16)
            sp.dma_start(bin_sb[:], a["l2_bin"]).then_inc(loaded, 16)
            sp.dma_start(bout[:], a["l2_bout"].partition_broadcast(P)).then_inc(loaded, 16)

        @block.tensor
        def _(pe):
            def project_out(b):
                pe.wait_ge(scanned, b + 1)
                if b >= 2:
                    pe.wait_ge(added, b - 1)
                for i in range(GROUP):
                    mm = nc.tensor.matmul(y_bank[b % 2][:, i * D:(i + 1) * D], states[:, b % 2, i * P:(i + 1) * P],
                                          wout[:], start=True, stop=True)
                mm.then_inc(y_psum, 1)

            for b in range(B):
                if b == 0:
                    pe.wait_ge(loaded, 64)
                if b >= 2:
                    pe.wait_ge(used, b - 1)
                columns = xnt[:, b * T:(b + 1) * T]
                nc.tensor.matmul(gate_bank[b % 2][:], win[:, 0:D], columns, start=True, stop=True)
                nc.tensor.matmul(hid_bank[b % 2][:], win[:, D:2 * D], columns, start=True, stop=True).then_inc(proj, 1)
                if b >= 1:
                    project_out(b - 1)
                if b >= 2:
                    ln_transpose(g, pe, ln, b - 2, xnt_bank[b % 2])
                if b >= 3:
                    ln_logits(g, pe, ln, b - 3, xnt_bank[(b + 1) % 2])
            project_out(B - 1)
            for b in (B - 2, B - 1):
                ln_logits(g, pe, ln, b - 1, xnt_bank[(b + 1) % 2])
                pe.wait_ge(ln.logits, b - 1)
                ln_transpose(g, pe, ln, b, xnt_bank[b % 2])
            ln_logits(g, pe, ln, B - 1, xnt_bank[(B - 1) % 2])

        @block.scalar
        def _(act):
            for b in range(B):
                act.wait_ge(proj, b + 1)
                act.wait_ge(loaded, 64)
                if b >= 2:
                    act.wait_ge(scanned, b - 1)
                nc.scalar.activation(sg[:, b % 2, :], gate_bank[b % 2][:], ACT.Sigmoid, bias=bin_sb[:, 0:1])
                nc.scalar.activation(sh[:, b % 2, :], hid_bank[b % 2][:], ACT.Sigmoid, bias=bin_sb[:, 1:2]).then_inc(sig, 1)
                if b >= 2:
                    ln_columns(g, act, ln, b - 2, xnt_bank[b % 2])
                if b >= 3:
                    ln_copy_logits(g, act, ln, b - 3, xnt_bank[(b + 1) % 2])
            for b in (B - 2, B - 1):
                ln_copy_logits(g, act, ln, b - 1, xnt_bank[(b + 1) % 2])
                ln_columns(g, act, ln, b, xnt_bank[b % 2])
            ln_copy_logits(g, act, ln, B - 1, xnt_bank[(B - 1) % 2])

        @block.vector
        def _(v):
            n = [0]

            def after(ins):
                n[0] += 1
                ins.then_inc(step, 1)
                v.wait_ge(step, n[0])

            def add(b):
                v.wait_ge(y_psum, b + 1)
                rows = g.x[:, GROUP * b:GROUP * (b + 1), :]
                after(nc.vector.tensor_tensor(out[:].rearrange("p (t d) -> p t d", d=D),
                                              y_bank[b % 2][:].rearrange("p (t d) -> p t d", d=D),
                                              bout[:, None, :].to_broadcast([P, GROUP, D]), ALU.add))
                nc.vector.tensor_tensor(rows, rows, out[:].rearrange("p (t d) -> p t d", d=D), ALU.add).then_inc(added, 1)
                v.wait_ge(added, b + 1)
                ln_stats(g, v, ln, b)

            after(nc.vector.memset(decay[:], 0.9))
            for b in range(B):
                v.wait_ge(sig, b + 1)
                after(nc.vector.scalar_tensor_tensor(silu[:, b % 2, :], hid_bank[b % 2][:], bin_sb[:, 1:2],
                                                     sh[:, b % 2, :], ALU.add, ALU.mult))
                nc.vector.scalar_tensor_tensor(drive[:, b % 2, :], silu[:, b % 2, :], 0.1, sg[:, b % 2, :],
                                               ALU.mult, ALU.mult).then_inc(used, 1)
                v.wait_ge(used, b + 1)
                if b >= 2:
                    v.wait_ge(y_psum, b - 1)
                nc.vector.tensor_tensor_scan(states[:, b % 2, :], decay[:], drive[:, b % 2, :], 0.0,
                                             ALU.mult, ALU.add).then_inc(scanned, 1)
                if b >= 2:
                    ln_rows(g, v, ln, b - 2)
                if b >= 1:
                    add(b - 1)
            ln_rows(g, v, ln, B - 2)
            add(B - 1)
            ln_rows(g, v, ln, B - 1)

        @block.gpsimd
        def _(pool):
            for b in range(B):
                ln_rstd(g, pool, ln, b)


GROUPS = 4
GH = HEADS // GROUPS
NG = B * GROUPS
RING = 4
VW = 32
PARTS, TERMS = 3, 6
MAX_ROWS = PARTS * GH
MAX_AT, K_ROWS = 64, 96
MAX_AT1 = 96
R1, R2 = 4, 8
KR = R1 * R2


def slots():
    return [(n, n // GROUPS, n % GROUPS) for n in range(-2 * GROUPS + 1, NG + GROUPS)]


class RelativeBias:
    L = 3 * P

    def __init__(self, g, ctx, name, kq, qk):
        sem = semaphores(g, name)
        sb = lambda n, shape, dt=F32: ctx.enter_context(g.nc.sbuf_tensor(f"{name}_{n}", shape, dt))
        self.g, self.kq, self.qk = g, kq, qk
        self.loaded, self.summed, self.less_last, self.turned, self.lined = (sem(n) for n in (
            "loaded", "summed", "less_last", "turned", "lined"))
        self.stored, self.tiled, self.flipped = sem("lines_stored"), sem("tiled"), [sem("flipped_kq"), sem("flipped_qk")]
        self.high, self.cast, self.low = sem("high"), sem("cast"), sem("low")
        self.split_done, self.copied = sem("split"), sem("copied")
        self.tables = sb("tables", [P, 3, P])
        self.sums = sb("sums", [P, 3, HEADS])
        self.line = sb("line", [HEADS, 2, self.L])
        self.tiles = sb("tiles", [P, 2, HEADS, 2 * P])
        self.rest = sb("rest", [P, 2, 2, 2 * P])

    def load(self, sp):
        a = self.g.a
        for k, src in enumerate((a["l0_rel"], a["l0_rel_back"], a["l0_rel"][P - 1, :].partition_broadcast(P))):
            sp.dma_start(self.tables[:, k, :], src).then_inc(self.loaded, 16)

    def sum_heads(self, v):
        nc, line = self.g.nc, self.line
        nc.vector.memset(line[:, 0, 0:P], MASKED)
        nc.vector.memset(line[:, 0, 2 * P:self.L], 0.0)
        nc.vector.memset(line[:, 1, 0:P], 0.0)
        nc.vector.memset(line[:, 1, 2 * P:self.L], MASKED)
        v.wait_ge(self.loaded, 48)
        nc.vector.tensor_reduce(self.sums[:].rearrange("p k h -> p (k h)"),
                                self.tables[:].rearrange("p k (h d) -> p (k h) d", d=HD), axis=AX, op=ALU.add
                                ).then_inc(self.summed, 1)
        v.wait_ge(self.summed, 1)
        nc.vector.tensor_tensor(self.sums[:, 0:2, :], self.sums[:, 0:2, :],
                                self.sums[:, 2:3, :].to_broadcast([P, 2, HEADS]), ALU.subtract).then_inc(self.less_last, 1)

    def turn(self, pe, bank):
        pe.wait_ge(self.less_last, 1)
        for way in range(2):
            mm = self.g.nc.tensor.transpose(bank[0:HEADS, way * P:(way + 1) * P], self.sums[:, way, :], self.g.ident[:])
        mm.then_inc(self.turned, 1)

    def copy_lines(self, act, bank):
        act.wait_ge(self.turned, 1)
        for way in range(2):
            self.g.nc.scalar.copy(self.line[:, way, P:2 * P], bank[0:HEADS, way * P:(way + 1) * P]).then_inc(self.lined, 1)

    def store_lines(self, act):
        act.wait_ge(self.lined, 2)
        act.dma_start(self.g.bias_lines.rearrange("h (w l) -> h w l", l=self.L), self.line[:]).then_inc(self.stored, 16)

    def load_tiles(self, act):
        act.wait_ge(self.stored, 16)
        for way in range(2):
            windows = bass.AP(self.g.bias_lines.tensor, way * self.L + 1 - way, [[1, P], [2 * self.L, HEADS], [1, 2 * P]])
            act.dma_start(self.tiles[:, way, :, :], windows).then_inc(self.tiled, 16)

    def flip(self, pe, banks):
        pe.wait_ge(self.tiled, 32)
        for k in range(HEADS // 2):
            for way in range(2):
                if k >= 2:
                    pe.wait_ge(self.copied if way else self.split_done, k - 1)
                self.g.nc.tensor.matmul(banks[way][k % 2][:], self.g.flip[:],
                                        self.tiles[:, way, 2 * k:2 * k + 2, :].rearrange("p h c -> p (h c)"),
                                        start=True, stop=True).then_inc(self.flipped[way], 1)

    def split(self, v, banks):
        nc = self.g.nc
        for k in range(HEADS // 2):
            part = lambda n: self.kq[:, 2 * k:2 * k + 2, n, :]
            tile, rest = banks[0][k % 2][:].rearrange("p (h c) -> p h c", h=2), self.rest[:, k % 2, :, :]
            v.wait_ge(self.high, k + 1)
            if k >= 2:
                v.wait_ge(self.low, k - 1)
            nc.vector.tensor_tensor(rest, tile, part(0), ALU.subtract).then_inc(self.split_done, 1)
            if k >= 1:
                self.split_low(v, k - 1)
        self.split_low(v, HEADS // 2 - 1)

    def split_low(self, v, k):
        part = lambda n: self.kq[:, 2 * k:2 * k + 2, n, :]
        v.wait_ge(self.cast, k + 1)
        self.g.nc.vector.tensor_tensor(part(2), self.rest[:, k % 2, :, :], part(1), ALU.subtract).then_inc(self.low, 1)

    def copy(self, act, banks):
        nc = self.g.nc
        for k in range(HEADS // 2):
            act.wait_ge(self.flipped[0], k + 1)
            nc.scalar.copy(self.kq[:, 2 * k:2 * k + 2, 0, :], banks[0][k % 2][:].rearrange("p (h c) -> p h c", h=2)
                           ).then_inc(self.high, 1)
            act.wait_ge(self.flipped[1], k + 1)
            nc.scalar.copy(self.qk[:, 2 * k:2 * k + 2, :].rearrange("p h c -> p (h c)"), banks[1][k % 2][:]
                           ).then_inc(self.copied, 1)
            act.wait_ge(self.split_done, k + 1)
            nc.scalar.copy(self.kq[:, 2 * k:2 * k + 2, 1, :], self.rest[:, k % 2, :, :]).then_inc(self.cast, 1)


class AttentionWeights:
    def __init__(self, g, ctx, kind):
        sb = lambda n, shape: ctx.enter_context(g.nc.sbuf_tensor(f"att{kind}_{n}", shape, F32))
        self.g, self.layer, self.projected_apart = g, f"l{kind}", kind != 1
        self.loaded = semaphores(g, f"att{kind}")("weights_loaded")
        self.wo, self.bo = sb("wo", [P, D]), sb("bo", [P, D])
        if self.projected_apart:
            self.wq, self.wk, self.wv = sb("wq", [P, P]), sb("wk", [P, P]), sb("wv", [P, P])
            self.bq, self.bk, self.bv = sb("bq", [P, 1]), sb("bk", [P, 1]), sb("bv", [P, D])
            self.loads = 16 * 8
        else:
            self.wqk = sb("wqk", [P, T])
            self.loads = 16 * 3

    def load(self, sp):
        part = lambda n: self.g.a[f"{self.layer}_{n}"]
        if self.projected_apart:
            pairs = [(self.wq, part("wq")), (self.wk, part("wk")), (self.wv, part("wv")), (self.bq, part("bq")),
                     (self.bk, part("bk")), (self.bv, part("bv").partition_broadcast(P))]
        else:
            pairs = [(self.wqk, part("wqk"))]
        for dst, src in pairs + [(self.wo, part("wo")), (self.bo, part("bo").partition_broadcast(P))]:
            sp.dma_start(dst[:], src).then_inc(self.loaded, 16)


def attention(g, name, kind, weights, gate, bias=None):
    nc, a = g.nc, g.a
    causal = kind != 3
    split = kind != 1
    scale = HD ** -0.5 if split else KR ** -0.5
    first_query = [P * s if causal else 0 for s in range(GROUP)]
    width = [T - f for f in first_query]
    units = [[0], [1, 3], [2]] if causal else [[0], [1], [2], [3]]
    offset, unit_at, at = {}, [], 0
    for u in units:
        unit_at.append(at)
        for s in u:
            offset[s], at = at, at + width[s]
    prob_width, U = at, len(units)
    keys_seen = [P * (i + 1) if causal else T for i in range(GROUP)]
    group_units, group_tiles = GH * U, GH * GROUP

    with ExitStack() as ctx:
        sem = semaphores(g, name)
        sb = lambda n, shape, dt=F32: ctx.enter_context(nc.sbuf_tensor(f"{name}_{n}", shape, dt))
        if kind == 0:
            bias_kq, bias_qk = bias
        ln = LayerNormSems(sem, gate=gate)
        loaded, wo, bo = weights.loaded, weights.wo, weights.bo
        prepared, zeroed, spare_rows, values_zeroed = (sem(n) for n in (
            "selectors_placed", "zeros_made", "zeros_placed", "values_zeroed"))
        proj, taken, hi_ready, rem_ready, mid_ready, parts_ready = (sem(n) for n in (
            "projected", "projections_taken", "high_parts", "remainders", "middle_parts", "parts"))
        v_psum, v_ready = sem("values_psum"), sem("values")
        written = sem("terms_written")
        op_loaded = [sem(f"operands{i}") for i in range(RING)]
        rows_psum, rows_taken = sem("rows_pass"), sem("rows_taken")
        max_step, max_split, max_psum, max_cols, max_loaded = (sem(n) for n in (
            "max_step", "max_split", "max_psum", "max_columns", "max_loaded"))
        cols_psum, probs_ready = sem("columns_pass"), sem("probs")
        o_psum, o_copied, t_psum, t_norm = sem("context_psum"), sem("context"), sem("context_turned"), sem("context_rows")
        norm_step = sem("norm_step")
        c_psum, c_ready, y_psum, added = sem("rows_turned"), sem("context_columns"), sem("out_psum"), sem("added")

        columns_of = lambda b: g.xnt[:, b * T:(b + 1) * T]
        values = sb("values", [P, 2, GROUP, HEADS, VW])
        probs = sb("probs", [P, 2, GH, prob_width])
        maxima = sb("maxima", [P, 2, GROUP, GH])
        far = sb("far", [P, 2, GROUP, GH])
        max_rest = sb("max_rest", [P, GROUP, GH])
        max_parts = sb("max_parts", [P, GROUP, PARTS, GH], BF16)
        max_t = sb("max_t", [MAX_ROWS, T], BF16)
        context_t = sb("context_t", [P, T])
        recip = sb("recip", [P, GROUP, GH])
        context = sb("context", [P, GROUP, D])
        columns = sb("columns", [P, T])
        out = sb("out", [P, GROUP, D])
        if split:
            wq, wk, wv, bq, bk, bv = weights.wq, weights.wk, weights.wv, weights.bq, weights.bk, weights.bv
            rest = sb("qk", [P, 2, T])
            parts = sb("parts", [P, 2, PARTS, T], BF16)
            q_op, k_op = sb("queries", [P, RING, GH, T], BF16), sb("keys", [P, RING, GH, T], BF16)
            zeros = sb("zeros", [P, T], BF16)
            op_loads = 3
        else:
            wqk = weights.wqk
            pj = sb("pj", [P, 2, GROUP, T])
            outer = sb("outer", [P, 2, 2, GROUP, P])
            rest = sb("rest", [P, 2, T])
            parts = sb("parts", [P, 2, 2, PARTS, T], BF16)
            q_op, k_op = sb("queries", [P, RING, 2, GH, T], BF16), sb("keys", [P, RING, 2, GH, T], BF16)
            op_loads = 6
            outer_ready, outer_psum = sem("outer_products"), sem("outer_products_turned")
        rows_bank, cols_bank = g.bank[0:2], g.bank[2:5]
        o_bank, prep_bank, misc_bank = g.bank[5], g.bank[6], g.bank[7]
        block = ctx.enter_context(nc.Block(no_gpsimd_drain=True))

        def make_outer(engine, ops, G):
            b, c = G // GROUPS, G % GROUPS
            engine.wait_ge(taken, GROUP * (b + 1))
            if G >= 2:
                engine.wait_ge(outer_psum, 2 * (G - 1))
            for side in range(2):
                for t in range(GROUP):
                    at1 = side * HEADS * R1 + c * GH * R1
                    at2 = 2 * HEADS * R1 + side * HEADS * R2 + c * GH * R2
                    one = pj[:, b % 2, t, at1:at1 + GH * R1].rearrange("p (j r) -> p r j", r=R1)
                    two = pj[:, b % 2, t, at2:at2 + GH * R2].rearrange("p (j s) -> p s j", s=R2)
                    wide = [P, R1, R2, GH]
                    ins = ops.tensor_tensor(outer[:, G % 2, side, t, :].rearrange("p (r s j) -> p r s j", r=R1, s=R2),
                                                  one[:, :, None, :].to_broadcast(wide),
                                                  two[:, None, :, :].to_broadcast(wide), ALU.mult)
                ins.then_inc(outer_ready, 1)

        @block.sync
        def _(sp):
            if split:
                sp.wait_ge(zeroed, 1)
                pad = slice(TERMS * HD, K_ROWS)
                sp.dma_start(q_op[pad, :, :, :].rearrange("p i j t -> p (i j) t"),
                             zeros[pad, None, :].to_broadcast([K_ROWS - TERMS * HD, RING * GH, T])).then_inc(spare_rows, 16)
                pad = slice(TERMS * HD, MAX_AT)
                sp.dma_start(k_op[pad, :, :, :].rearrange("p i j t -> p (i j) t"),
                             zeros[pad, None, :].to_broadcast([MAX_AT - TERMS * HD, RING * GH, T])).then_inc(spare_rows, 16)

            def write_terms(b):
                if b >= 2:
                    for i in range(RING):
                        sp.wait_ge(op_loaded[i], 16 * op_loads * (b - 1))
                for side in range(2):
                    sp.wait_ge(parts_ready, 2 * b + side + 1)
                    dst = g.terms[b % 2][side]
                    if side == 0:
                        for at, part, times in ((0, 0, 3), (3, 1, 2), (5, 2, 1)):
                            sp.dma_start(dst[at:at + times].rearrange("j r t -> r j t"),
                                         parts[:, 0, part:part + 1, :].to_broadcast([P, times, T])).then_inc(written, 16)
                    else:
                        for at, times in ((0, 3), (3, 2), (5, 1)):
                            sp.dma_start(dst[at:at + times].rearrange("j r t -> r j t"),
                                         parts[:, 1, 0:times, :]).then_inc(written, 16)

            def write_parts(G):
                if G >= 2:
                    sp.wait_ge(op_loaded[(G - 2) % RING], 16 * op_loads * ((G - 2) // RING + 1))
                for side in range(2):
                    sp.wait_ge(parts_ready, 2 * G + side + 1)
                    sp.dma_start(g.terms[G % 2][side][0:PARTS].rearrange("k r t -> r k t"),
                                 parts[:, G % 2, side, :, :]).then_inc(written, 16)

            def load_operands(G):
                i, b, q = G % RING, G // GROUPS, G % GROUPS
                if G >= RING:
                    sp.wait_ge(cols_psum, group_units * (G - RING + 1))
                if split:
                    if G == 0:
                        sp.wait_ge(spare_rows, 32)
                    sp.wait_ge(written, 16 * 6 * (b + 1))
                    for side, op in enumerate((q_op, k_op)):
                        sp.dma_start(op[0:TERMS * HD, i, :, :],
                                     g.terms[b % 2][side].rearrange("j (d h) t -> (j d) h t", h=HEADS)[:, GH * q:GH * (q + 1), :]
                                     ).then_inc(op_loaded[i], 16)
                    sp.dma_start(q_op[MAX_AT:MAX_AT + MAX_ROWS, i, :, :], zeros[MAX_AT:MAX_AT + MAX_ROWS, None, :]
                                 .to_broadcast([MAX_ROWS, GH, T])).then_inc(op_loaded[i], 16)
                else:
                    sp.wait_ge(written, 32 * (G + 1))
                    stored = [g.terms[G % 2][side].rearrange("k (r j) t -> (k r) j t", j=GH) for side in range(2)]
                    part = lambda side, k: stored[side][KR * k:KR * (k + 1)]
                    sp.dma_start(q_op[0:KR, i, 0, :, :], part(0, 0)).then_inc(op_loaded[i], 16)
                    sp.dma_start(q_op[KR:3 * KR, i, 0, :, :], stored[0][0:2 * KR]).then_inc(op_loaded[i], 16)
                    sp.dma_start(q_op[0:3 * KR, i, 1, :, :], stored[0][0:3 * KR]).then_inc(op_loaded[i], 16)
                    sp.dma_start(k_op[0:KR, i, 0, :, :], part(1, 2)).then_inc(op_loaded[i], 16)
                    sp.dma_start(k_op[KR:3 * KR, i, 0, :, :], stored[1][KR:3 * KR]).then_inc(op_loaded[i], 16)
                    sp.dma_start(k_op[0:3 * KR, i, 1, :, :], stored[1][0:3 * KR]).then_inc(op_loaded[i], 16)

            def load_maxima(G):
                sp.wait_ge(max_cols, G + 1)
                dst = q_op[MAX_AT:MAX_AT + MAX_ROWS, G % RING, :, :] if split else \
                    q_op[MAX_AT1:MAX_AT1 + MAX_ROWS, G % RING, 1, :, :]
                sp.dma_start(dst, max_t[:, None, :].to_broadcast([MAX_ROWS, GH, T])).then_inc(max_loaded, 16)

            for n, b, q in slots():
                if 0 <= n + 1 < NG:
                    load_maxima(n + 1)
                if 0 <= n + 3 < NG:
                    load_operands(n + 3)
                if not split and 0 <= n + 4 < NG:
                    write_parts(n + 4)
                if split and q == 0 and 0 <= b + 1 < B:
                    write_terms(b + 1)
                if kind == 0 and n == NG - 3:
                    write_untaken(g, sp, (1, 2, 3))
            sp.wait_ge(max_loaded, 16 * NG)

        @block.tensor
        def _(pe):
            misc_last, prep_last = [], []

            def bank_free(last, *reader):
                for s, value in last:
                    pe.wait_ge(s, value)
                last[:] = [reader]

            def columns_unit(G, j, u):
                i, k = G % RING, G * group_units + j * U + u
                h = GH * (G % GROUPS) + j
                if k >= 3:
                    pe.wait_ge(probs_ready, k - 2)
                bank = cols_bank[k % 3]
                c0 = 0
                for s in units[u]:
                    dst = bank[:, c0:c0 + width[s]]
                    q0 = first_query[s]
                    key = slice(s * P, (s + 1) * P)
                    if split:
                        mm = nc.tensor.matmul(dst, k_op[0:K_ROWS, i, j, key], q_op[0:K_ROWS, i, j, q0:T],
                                              start=True, stop=kind == 3)
                    else:
                        nc.tensor.matmul(dst, k_op[0:3 * KR, i, 0, j, key], q_op[0:3 * KR, i, 0, j, q0:T],
                                         start=True, stop=False)
                        nc.tensor.matmul(dst, k_op[0:MAX_AT1 + MAX_ROWS, i, 1, j, key],
                                         q_op[0:MAX_AT1 + MAX_ROWS, i, 1, j, q0:T], start=False, stop=False)
                        mm = nc.tensor.matmul(bank[:, c0:c0 + P], g.identb[:], g.mask_kq[:], start=False, stop=True)
                    if kind == 0:
                        w = min(2 * P, width[s])
                        for p in range(3):
                            mm = nc.tensor.matmul(bank[:, c0:c0 + w], g.identb[:], bias_kq[:, h, p, 0:w],
                                                  start=False, stop=p == 2)
                    c0 += width[s]
                mm.then_inc(cols_psum, 1)

            def rows_tile(G, j, t):
                i, k = G % RING, G * group_tiles + j * GROUP + t
                if k >= 2:
                    pe.wait_ge(rows_taken, k - 1)
                query = slice(t * P, (t + 1) * P)
                dst = rows_bank[k % 2][:, 0:keys_seen[t]]
                if split:
                    mm = nc.tensor.matmul(dst, q_op[0:K_ROWS, i, j, query], k_op[0:K_ROWS, i, j, 0:keys_seen[t]],
                                          start=True, stop=True)
                else:
                    mm = nc.tensor.matmul(dst, q_op[0:3 * KR, i, 0, j, query], k_op[0:3 * KR, i, 0, j, 0:keys_seen[t]],
                                          start=True, stop=True)
                mm.then_inc(rows_psum, 1)

            def context_step(G, s):
                b = G // GROUPS
                if s == 0:
                    pe.wait_ge(probs_ready, group_units * (G + 1))
                    pe.wait_ge(v_ready, b + 1)
                    if G >= 1:
                        pe.wait_ge(o_copied, G)
                for j in range(GH):
                    mm = nc.tensor.matmul(o_bank[VW * j:VW * (j + 1), first_query[s]:T],
                                          values[:, b % 2, s, GH * (G % GROUPS) + j, :],
                                          probs[:, G % 2, j, offset[s]:offset[s] + width[s]],
                                          start=(s == 0), stop=(s == GROUP - 1))
                if s == GROUP - 1:
                    mm.then_inc(o_psum, 1)

            def turn_context(G):
                pe.wait_ge(o_copied, G + 1)
                bank_free(misc_last, t_norm, G + 1)
                for t in range(GROUP):
                    mm = nc.tensor.transpose(misc_bank[:, t * P:(t + 1) * P], context_t[:, t * P:(t + 1) * P], g.ident[:])
                mm.then_inc(t_psum, 1)

            def turn_rows(b):
                pe.wait_ge(t_norm, GROUPS * (b + 1))
                bank_free(misc_last, c_ready, b + 1)
                for t in range(GROUP):
                    mm = nc.tensor.transpose(misc_bank[:, t * P:(t + 1) * P], context[:, t, :], g.ident[:])
                mm.then_inc(c_psum, 1)

            def project_out(b):
                pe.wait_ge(c_ready, b + 1)
                bank_free(misc_last, added, b + 1)
                for t in range(GROUP):
                    mm = nc.tensor.matmul(misc_bank[:, t * D:(t + 1) * D], columns[:, t * P:(t + 1) * P], wo[:],
                                          start=True, stop=True)
                mm.then_inc(y_psum, 1)

            def turn_maxima(G):
                pe.wait_ge(max_split, G + 1)
                bank_free(misc_last, max_cols, G + 1)
                bank = misc_bank[:].bitcast(BF16)
                for t in range(GROUP):
                    mm = nc.tensor.transpose(bank[0:MAX_ROWS, t * P:(t + 1) * P],
                                             max_parts[:, t, :, :].rearrange("p k h -> p (k h)"), g.identb[:])
                mm.then_inc(max_psum, 1)

            def turn_norm(b):
                bank_free(prep_last, *((ln.xnt, b + 1) if gate is None else (ln.logits, b + 1)))
                ln_transpose(g, pe, ln, b, prep_bank)

            def project_qk(b, side):
                pe.wait_ge(loaded, weights.loads)
                bank_free(prep_last, taken, 2 * b + side + 1)
                nc.tensor.matmul(prep_bank[:], (wq, wk)[side][:], columns_of(b), start=True, stop=True).then_inc(proj, 1)

            def first_projections():
                pe.wait_ge(loaded, weights.loads)
                for side, bank in enumerate((prep_bank, misc_bank)):
                    nc.tensor.matmul(bank[:], (wq, wk)[side][:], columns_of(0), start=True, stop=True).then_inc(proj, 1)
                prep_last[:] = [(taken, 1)]
                misc_last[:] = [(taken, 2)]

            def project_values(b):
                bank_free(prep_last, v_ready, b + 1)
                for t in range(GROUP):
                    mm = nc.tensor.matmul(prep_bank[:, t * D:(t + 1) * D], columns_of(b)[:, t * P:(t + 1) * P], wv[:],
                                          start=True, stop=True)
                mm.then_inc(v_psum, 1)

            def project_tile(b, t):
                pe.wait_ge(loaded, weights.loads)
                bank = misc_bank if b == 0 and t % 2 else prep_bank
                bank_free(misc_last if b == 0 and t % 2 else prep_last, taken, GROUP * b + t + 1)
                nc.tensor.matmul(bank[:], columns_of(b)[:, t * P:(t + 1) * P], wqk[:], start=True, stop=True
                                 ).then_inc(proj, 1)

            def turn_outer(G, side):
                pe.wait_ge(outer_ready, 2 * G + side + 1)
                bank_free(prep_last, rem_ready, 2 * G + side + 1)
                for t in range(GROUP):
                    mm = nc.tensor.transpose(prep_bank[:, t * P:(t + 1) * P], outer[:, G % 2, side, t, :], g.ident[:])
                mm.then_inc(outer_psum, 1)

            for n, b, q in slots():
                C, R = 0 <= n < NG, 0 <= n + 2 < NG
                if C:
                    pe.wait_ge(max_loaded, 16 * (n + 1))
                if R:
                    pe.wait_ge(op_loaded[(n + 2) % RING], 16 * op_loads * ((n + 2) // RING + 1))
                    if n + 2 < RING:
                        pe.wait_ge(prepared, 1)
                if not split and 0 <= n + 5 < NG:
                    turn_outer(n + 5, 0)
                for j in range(GH):
                    for t in range(GROUP):
                        if C and t < U:
                            columns_unit(n, j, t)
                        if R:
                            rows_tile(n + 2, j, t)
                        if t == 1 and 0 <= n - 1 < NG:
                            context_step(n - 1, j)
                    if j == 0:
                        if 0 <= n + 1 < NG:
                            turn_maxima(n + 1)
                        if not split and q == 1 and 0 <= b + 2 < B:
                            project_tile(b + 2, 0)
                        if not split and q == 2 and 0 <= b + 2 < B:
                            project_tile(b + 2, 3)
                    elif j == 1:
                        if 0 <= n - 2 < NG:
                            turn_context(n - 2)
                        if split and n == -2 * GROUPS + 2:
                            first_projections()
                        elif split and q in (2, 3) and 1 <= b + 2 < B:
                            project_qk(b + 2, q - 2)
                        if not split and 0 <= n + 5 < NG:
                            turn_outer(n + 5, 1)
                    elif j == 2:
                        if (n - 3) % GROUPS == GROUPS - 1 and 0 <= n - 3 < NG:
                            project_out((n - 3) // GROUPS)
                        if split and q == 0 and 0 <= b + 1 < B:
                            project_values(b + 1)
                        if q == 3 and 0 <= b - 1 < B:
                            turn_norm(b - 1)
                        if not split and q == 1 and 0 <= b + 2 < B:
                            project_tile(b + 2, 1)
                    else:
                        if q == 3 and 0 <= b - 1 < B:
                            ln_logits(g, pe, ln, b - 1, prep_bank)
                        if (n - 2) % GROUPS == GROUPS - 1 and 0 <= n - 2 < NG:
                            turn_rows((n - 2) // GROUPS)
                        if not split and q == 1 and 0 <= b + 2 < B:
                            project_tile(b + 2, 2)

        @block.scalar
        def _(act):
            def exponentials(G, j):
                for u, at in zip(range(U), unit_at):
                    k = G * group_units + j * U + u
                    w = sum(width[s] for s in units[u])
                    act.wait_ge(cols_psum, k + 1)
                    if G >= 2 and j == 0 and u == 0:
                        act.wait_ge(o_psum, G - 1)
                    nc.scalar.activation(probs[:, G % 2, j, at:at + w], cols_bank[k % 3][:, 0:w], ACT.Exp
                                         ).then_inc(probs_ready, 1)

            def copy_context(G):
                act.wait_ge(o_psum, G + 1)
                if G >= 1:
                    act.wait_ge(t_psum, G)
                nc.scalar.copy(context_t[:], o_bank[:]).then_inc(o_copied, 1)

            def copy_columns(b):
                act.wait_ge(c_psum, b + 1)
                if b >= 1:
                    act.wait_ge(y_psum, b)
                nc.scalar.copy(columns[:], misc_bank[:]).then_inc(c_ready, 1)

            def copy_maxima(G):
                act.wait_ge(max_psum, G + 1)
                if G >= 1:
                    act.wait_ge(max_loaded, 16 * G)
                nc.scalar.copy(max_t[:], misc_bank[:].bitcast(BF16)[0:MAX_ROWS, 0:T]).then_inc(max_cols, 1)

            def high_part(b, side):
                act.wait_ge(taken, 2 * b + side + 1)
                if b >= 1:
                    act.wait_ge(written, 16 * 6 * b)
                nc.scalar.copy(parts[:, side, 0, :], rest[:, side, :]).then_inc(hi_ready, 1)

            def first_parts():
                for side in range(2):
                    high_part(0, side)
                for side in range(2):
                    act.wait_ge(rem_ready, side + 1)
                    nc.scalar.copy(parts[:, side, 1, :], rest[:, side, :]).then_inc(mid_ready, 1)

            def take_tile(b, t):
                act.wait_ge(proj, GROUP * b + t + 1)
                if b >= 2:
                    act.wait_ge(outer_ready, 2 * GROUPS * (b - 1))
                    act.wait_ge(v_ready, b - 1)
                bank = misc_bank if b == 0 and t % 2 else prep_bank
                nc.scalar.mul(pj[:, b % 2, t, 0:HEADS * R1], bank[:, 0:HEADS * R1], scale)
                nc.scalar.copy(pj[:, b % 2, t, HEADS * R1:T], bank[:, HEADS * R1:T]).then_inc(taken, 1)

            def high_outer(G, side):
                act.wait_ge(outer_psum, 2 * G + side + 1)
                if G >= 2:
                    act.wait_ge(written, 32 * (G - 1))
                nc.scalar.copy(parts[:, G % 2, side, 2 * side, :], prep_bank[:]).then_inc(hi_ready, 1)

            def middle_outer(G, side):
                act.wait_ge(rem_ready, 2 * G + side + 1)
                nc.scalar.copy(parts[:, G % 2, side, 1, :], rest[:, side, :]).then_inc(mid_ready, 1)

            for n, b, q in slots():
                C, O = 0 <= n < NG, 0 <= n + 5 < NG
                if 0 <= n - 2 < NG:
                    copy_context(n - 2)
                if not split and O:
                    high_outer(n + 5, 0)
                for j in range(GH):
                    if C:
                        exponentials(n, j)
                    if j == 0:
                        if (n - 3) % GROUPS == GROUPS - 1 and 0 <= n - 3 < NG:
                            copy_columns((n - 3) // GROUPS)
                        if not split and q == 1 and 0 <= b + 2 < B:
                            take_tile(b + 2, 0)
                        if not split and q == 2 and 0 <= b + 2 < B:
                            take_tile(b + 2, 3)
                    elif j == 1:
                        if 0 <= n + 1 < NG:
                            copy_maxima(n + 1)
                        if not split and O:
                            middle_outer(n + 5, 0)
                            high_outer(n + 5, 1)
                    elif j == 2:
                        if q == 3 and 0 <= b - 1 < B:
                            ln_columns(g, act, ln, b - 1, prep_bank)
                        if split and n == -2 * GROUPS + 2:
                            first_parts()
                        elif split and q in (2, 3) and 1 <= b + 2 < B:
                            high_part(b + 2, q - 2)
                        if not split and q == 1 and 0 <= b + 2 < B:
                            take_tile(b + 2, 1)
                    else:
                        if q == 3 and 0 <= b - 1 < B:
                            ln_copy_logits(g, act, ln, b - 1, prep_bank)
                        if not split and O:
                            middle_outer(n + 5, 1)
                        if not split and q == 1 and 0 <= b + 2 < B:
                            take_tile(b + 2, 2)

        @block.vector
        def _(v):
            steps = [0]

            def after(ins):
                steps[0] += 1
                ins.then_inc(norm_step, 1)
                v.wait_ge(norm_step, steps[0])

            def row_maxima(G, j):
                h = GH * (G % GROUPS) + j
                for t in range(GROUP):
                    k = G * group_tiles + j * GROUP + t
                    v.wait_ge(rows_psum, k + 1)
                    bank = rows_bank[k % 2]
                    best = maxima[:, G % 2, t, j:j + 1]
                    w = keys_seen[t]
                    if kind == 3:
                        ins = nc.vector.tensor_reduce(best, bank[:], axis=AX, op=ALU.max)
                    elif kind == 1:
                        ins = nc.vector.tensor_tensor_reduce(out=bank[:, 0:w], in0=bank[:, 0:w], in1=g.mask_qk[:, T - w:T],
                                                             scale=1.0, scalar=-3.0e38, op0=ALU.add, op1=ALU.max, accum_out=best)
                    else:
                        near = min(2 * P, w)
                        if t >= 2:
                            nc.vector.tensor_reduce(far[:, G % 2, t, j:j + 1], bank[:, 0:w - near], axis=AX, op=ALU.max)
                        ins = nc.vector.tensor_tensor_reduce(out=bank[:, w - near:w], in0=bank[:, w - near:w],
                                                             in1=bias_qk[:, h, 2 * P - near:2 * P], scale=1.0, scalar=-3.0e38,
                                                             op0=ALU.add, op1=ALU.max, accum_out=best)
                    ins.then_inc(rows_taken, 1)

            def split_maxima(G):
                v.wait_ge(rows_taken, group_tiles * (G + 1))
                best = maxima[:, G % 2, :, :]
                if G >= 1:
                    v.wait_ge(max_psum, G)
                if kind == 0:
                    after(nc.vector.tensor_tensor(maxima[:, G % 2, 2:GROUP, :], maxima[:, G % 2, 2:GROUP, :],
                                                  far[:, G % 2, 2:GROUP, :], ALU.max))
                part = lambda k: max_parts[:, :, k, :]
                after(nc.vector.tensor_scalar(part(0), best, -1.0, None, ALU.mult))
                after(nc.vector.scalar_tensor_tensor(max_rest[:], best, -1.0, part(0), ALU.mult, ALU.subtract))
                after(nc.vector.tensor_copy(part(1), max_rest[:]))
                nc.vector.tensor_tensor(part(2), max_rest[:], part(1), ALU.subtract).then_inc(max_split, 1)

            def normalise(G):
                v.wait_ge(t_psum, G + 1)
                q = G % GROUPS
                by_head = misc_bank[:].rearrange("p (t j w) -> p t j w", t=GROUP, j=GH)
                after(nc.vector.reciprocal(recip[:], by_head[:, :, :, HD]))
                if q == 0 and G >= GROUPS:
                    v.wait_ge(c_psum, G // GROUPS)
                dst = context[:, :, GH * q * HD:GH * (q + 1) * HD].rearrange("p t (j d) -> p t j d", d=HD)
                nc.vector.tensor_tensor(dst, by_head[:, :, :, 0:HD], recip[:, :, :, None].to_broadcast([P, GROUP, GH, HD]),
                                        ALU.mult).then_inc(t_norm, 1)

            def add_out(b):
                v.wait_ge(y_psum, b + 1)
                after(nc.vector.tensor_tensor(out[:], misc_bank[:].rearrange("p (t d) -> p t d", d=D),
                                              bo[:, None, :].to_broadcast([P, GROUP, D]), ALU.add))
                tiles = slice(GROUP * b, GROUP * (b + 1))
                nc.vector.tensor_tensor(g.x[:, tiles, :], g.x[:, tiles, :], out[:], ALU.add).then_inc(added, 1)
                v.wait_ge(added, b + 1)

            def first_parts():
                for side, bank in enumerate((prep_bank, misc_bank)):
                    take_qk(0, side, bank)
                for side in range(2):
                    v.wait_ge(hi_ready, side + 1)
                    nc.vector.tensor_tensor(rest[:, side, :], rest[:, side, :], parts[:, side, 0, :], ALU.subtract
                                            ).then_inc(rem_ready, 1)
                for side in range(2):
                    v.wait_ge(mid_ready, side + 1)
                    nc.vector.tensor_tensor(parts[:, side, 2, :], rest[:, side, :], parts[:, side, 1, :], ALU.subtract
                                            ).then_inc(parts_ready, 1)

            def take_qk(b, side, bank=prep_bank):
                v.wait_ge(proj, 2 * b + side + 1)
                if b >= 1:
                    v.wait_ge(parts_ready, 2 * (b - 1) + side + 1)
                if side == 0:
                    ins = nc.vector.tensor_scalar(rest[:, 0, :], bank[:], bq[:], scale, ALU.add, ALU.mult)
                else:
                    ins = nc.vector.tensor_scalar(rest[:, 1, :], bank[:], bk[:], None, ALU.add)
                ins.then_inc(taken, 1)

            def take_values(b):
                v.wait_ge(v_psum, b + 1)
                if b == 0:
                    v.wait_ge(values_zeroed, 2)
                if b >= 2:
                    v.wait_ge(o_psum, GROUPS * (b - 1))
                nc.vector.tensor_tensor(values[:, b % 2, :, :, 0:HD],
                                        prep_bank[:].rearrange("p (t h d) -> p t h d", t=GROUP, h=HEADS),
                                        bv[:].rearrange("p (h d) -> p h d", d=HD)[:, None, :, :]
                                        .to_broadcast([P, GROUP, HEADS, HD]), ALU.add).then_inc(v_ready, 1)

            def outer_rest(G, side):
                v.wait_ge(hi_ready, 2 * G + side + 1)
                if G >= 1:
                    v.wait_ge(parts_ready, 2 * (G - 1) + side + 1)
                nc.vector.tensor_tensor(rest[:, side, :], prep_bank[:], parts[:, G % 2, side, 2 * side, :], ALU.subtract
                                        ).then_inc(rem_ready, 1)

            def place_selectors():
                if split:
                    dst, rows = k_op[MAX_AT:K_ROWS, :, :, :], g.head_selector[MAX_AT:K_ROWS]
                else:
                    dst, rows = k_op[MAX_AT1:P, :, 1, :, :], g.head_selector1[MAX_AT1:P]
                nc.vector.tensor_copy(dst, rows[:, None, :, None].to_broadcast([dst.shape[0], RING, GH, T])).then_inc(prepared, 1)

            if split:
                nc.vector.memset(zeros[:].bitcast(F32), 0.0).then_inc(zeroed, 1)
            for n, b, q in slots():
                if n == -GROUPS:
                    place_selectors()
                if not split and 0 <= n + 6 < GROUPS:
                    make_outer(v, nc.vector, n + 6)
                if 0 <= n + 1 < NG:
                    split_maxima(n + 1)
                for j in range(GH):
                    if 0 <= n + 2 < NG:
                        row_maxima(n + 2, j)
                    if j == 0:
                        if split and q == 1 and 0 <= b + 1 < B:
                            take_values(b + 1)
                        if q == 3 and 0 <= b - 1 < B:
                            ln_rows(g, v, ln, b - 1)
                        if not split and 0 <= n + 5 < NG:
                            outer_rest(n + 5, 0)
                    elif j == 2:
                        if 0 <= n - 2 < NG:
                            normalise(n - 2)
                        if split and n == -2 * GROUPS + 2:
                            first_parts()
                        elif split and q in (2, 3) and 1 <= b + 2 < B:
                            take_qk(b + 2, q - 2)
                        if not split and 0 <= n + 5 < NG:
                            outer_rest(n + 5, 1)
                    elif j == 3:
                        if (n - 3) % GROUPS == GROUPS - 1 and 0 <= n - 3 < NG:
                            add_out((n - 3) // GROUPS)
                            ln_stats(g, v, ln, (n - 3) // GROUPS)

        @block.gpsimd
        def _(pool):
            def low_outer(G, side):
                pool.wait_ge(mid_ready, 2 * G + side + 1)
                nc.gpsimd.tensor_tensor(parts[:, G % 2, side, 2 - 2 * side, :], rest[:, side, :], parts[:, G % 2, side, 1, :],
                                        ALU.subtract).then_inc(parts_ready, 1)

            def low_parts(b, side):
                k = 2 * b + side
                pool.wait_ge(hi_ready, k + 1)
                nc.gpsimd.tensor_tensor(rest[:, side, :], rest[:, side, :], parts[:, side, 0, :], ALU.subtract
                                        ).then_inc(rem_ready, 1)
                pool.wait_ge(rem_ready, k + 1)
                nc.gpsimd.tensor_copy(parts[:, side, 1, :], rest[:, side, :]).then_inc(mid_ready, 1)
                pool.wait_ge(mid_ready, k + 1)
                nc.gpsimd.tensor_tensor(parts[:, side, 2, :], rest[:, side, :], parts[:, side, 1, :], ALU.subtract
                                        ).then_inc(parts_ready, 1)

            def copy_values(b):
                pool.wait_ge(taken, GROUP * (b + 1))
                if b >= 2:
                    pool.wait_ge(o_psum, GROUPS * (b - 1))
                nc.gpsimd.tensor_copy(values[:, b % 2, :, :, 0:HD],
                                      pj[:, b % 2, :, T - D:T].rearrange("p t (h d) -> p t h d", d=HD)).then_inc(v_ready, 1)

            for n, b, q in slots():
                if n == -GROUPS:
                    nc.gpsimd.memset(values[:], 0.0).then_inc(values_zeroed, 1)
                    pool.wait_ge(values_zeroed, 1)
                    nc.gpsimd.memset(values[:, :, :, :, HD:HD + 1].rearrange("p b t h w -> p (b t h) w"), 1.0
                                     ).then_inc(values_zeroed, 1)
                    pool.wait_ge(values_zeroed, 2)
                if not split and GROUPS <= n + 6 < NG:
                    make_outer(pool, nc.gpsimd, n + 6)
                if not split and 0 <= n + 5 < NG:
                    for side in range(2):
                        low_outer(n + 5, side)
                if not split and (n + 3) % GROUPS == 0 and 0 <= n + 3 < NG:
                    copy_values((n + 3) // GROUPS)
                if q == 2 and 0 <= b - 1 < B:
                    ln_rstd(g, pool, ln, b - 1)
                if split and q in (2, 3) and 1 <= b + 2 < B:
                    low_parts(b + 2, q - 2)


class Shared:
    def __init__(self, nc, a):
        sb = lambda n, shape, dt=F32: nc.alloc_sbuf_tensor(n, shape, dt)
        self.nc = nc
        self.a = a
        self.spent = []
        self.x = sb("x_rows", [P, TILES, D])
        self.xn = sb("normalised_rows", [P, TILES, D + 1])
        self.xnt = sb("normalised_columns", [P, TOKENS])
        self.gates = sb("gates", [P, 4, E])
        self.logits = sb("logits", [P, TILES, E])
        self.gamma_beta = sb("gamma_beta", [P, 2])
        self.untaken = sb("untaken", [P, D + 1])
        self.token_i = sb("token_numbers_i", [P, 2 * TILES], U32)
        self.token = sb("token_numbers", [P, 2 * TILES])
        self.expert_selector = sb("expert_selector", [P, E // 2, P], BF16)
        self.stats = sb("stats", [P, TILES, 6])
        self.moments = sb("moments", [P, TILES, 2])
        self.var_eps = sb("var_eps", [P, TILES])
        self.rstd = sb("rstd", [P, TILES])
        self.neg_half = sb("neg_half", [P, TILES])
        self.ident = sb("ident", [P, P])
        self.flip = sb("flip", [P, P])
        self.identb = sb("identb", [P, P], BF16)
        self.onesb = sb("onesb", [P, P], BF16)
        self.beforeb = sb("beforeb", [P, P], BF16)
        self.mask_kq = sb("mask_kq", [P, P], BF16)
        self.mask_qk = sb("mask_qk", [P, T])
        self.rev = sb("rev", [P, TILES, E])
        self.scan_keep = sb("scan_keep", [P, E, TILES])
        self.tie = sb("tie", [P, TILES])
        self.spare = sb("spare", [P, 1])
        self.bank = [nc.alloc_psum_tensor(f"bank{i}", [P, T], F32) for i in range(8)]
        self.head_selector = sb("head_selector", [P, GH], BF16)
        self.head_selector1 = sb("head_selector1", [P, GH], BF16)
        self.terms = [[nc.dram_tensor(f"score_terms{i}_{side}", (TERMS, P, T), BF16).ap() for side in range(2)]
                      for i in range(2)]
        self.bias_lines = nc.dram_tensor("bias_lines", (HEADS, 2 * 3 * P), F32).ap()
        self.dispatched = [nc.dram_tensor(f"dispatched{n}", (slots, D + 1), F32).ap()
                           for n, slots in enumerate((E * CAP0, E * CAP0, E * CAP3, E * CAP3))]
        self.returned = nc.dram_tensor("returned", (2 * TOKENS, D), F32).ap()
        self.untaken_written = [nc.alloc_semaphore(f"untaken_written{n}") for n in range(4)]
        self.returned_zeroed = nc.alloc_semaphore("returned_zeroed")


def program(nc, a, out, wanted=range(12)):
    g = Shared(nc, a)
    gate = [g.gates[:, layer, :] for layer in range(4)]
    mixture = lambda n, name, layer, choices, cap, **more: moe_capacity(
        g, name, n, choices, cap, a[layer + "_w1"], a[layer + "_b1"], a[layer + "_w2"], a[layer + "_b2"], **more)
    with ExitStack() as ctx:
        weights = AttentionWeights(g, ctx, 0)
        bias_kq = ctx.enter_context(nc.sbuf_tensor("bias_kq", [P, HEADS, 3, 2 * P], BF16))
        bias_qk = ctx.enter_context(nc.sbuf_tensor("bias_qk", [P, HEADS, 2 * P], F32))
        with ExitStack() as beside:
            bias = RelativeBias(g, beside, "bias", bias_kq, bias_qk)
            setup(g, bias)
            mixture(0, "moe0_0", "l0", 1, CAP0, beside=bias, prefetch=weights)
        attention(g, "att0", 0, weights, gate[0], (bias_kq, bias_qk))
    mixture(1, "moe0_1", "l0", 1, CAP0, gate=gate[1])
    clear_semaphores(g)
    with ExitStack() as ctx:
        weights = AttentionWeights(g, ctx, 1)
        ffn1(g, "ffn1_0", prefetch=weights)
        attention(g, "att1", 1, weights, gate[1])
    with nc.sbuf_tensor("products2", [P, 2, 4 * D], F32) as products:
        with ExitStack() as beside:
            ffn1(g, "ffn1_1", gate[2], ExpertProducts(g, beside, "products2", products))
        clear_semaphores(g)
        ffn2(g, "ffn2_0", products)
        recurrence2(g, "rec2", gate[2])
        ffn2(g, "ffn2_1", products, gate[3])
    clear_semaphores(g)
    with ExitStack() as ctx:
        weights = AttentionWeights(g, ctx, 3)
        mixture(2, "moe3_0", "l3", 2, CAP3, twice=True, prefetch=weights)
        attention(g, "att3", 3, weights, gate[3])
    mixture(3, "moe3_1", "l3", 2, CAP3, last=True)
    store(g, out)


def store(g, out):
    nc = g.nc
    with ExitStack() as ctx:
        stored = ctx.enter_context(nc.semaphore("x_stored"))
        block = ctx.enter_context(nc.Block(no_gpsimd_drain=True))

        @block.sync
        def _(sp):
            sp.dma_start(out.rearrange("(i p) d -> p i d", p=P), g.x[:]).then_inc(stored, 16)
            sp.wait_ge(stored, 16)


def lay_out(i):
    import numpy as np
    t = lambda a: np.ascontiguousarray(np.asarray(a).T)
    n = lambda a: np.ascontiguousarray(np.asarray(a))
    by_chunk = lambda b: n(np.asarray(b).reshape(E * CH, P).T)
    dh = lambda w: n(np.asarray(w).reshape(HEADS, HD, -1).transpose(1, 0, 2).reshape(HEADS * HD, -1).T)
    dhb = lambda b: n(np.asarray(b).reshape(HEADS, HD).T.reshape(P, 1))
    ins = {"x": n(np.asarray(i["L0_attn_x"]).reshape(TOKENS, D))}
    ins["l0_gate"] = t(i["L0_ffn_gate_w"])
    ins["l3_gate"] = n(i["L3_ffn_wg"])
    for layer, f in (("l0", "L0_ffn"), ("l3", "L3_ffn")):
        ins[layer + "_w1"] = n(np.asarray(i[f + "_w1"]).reshape(E * P, HID))
        ins[layer + "_b1"] = by_chunk(i[f + "_b1"])
        ins[layer + "_w2"] = n(np.asarray(i[f + "_w2"]).reshape(E * HID, D))
        ins[layer + "_b2"] = n(i[f + "_b2"])
    for layer, w, bias, wo, bo in (("l0", "L0_attn_qkv_w", "L0_attn_qkv_b", "L0_attn_proj_w", "L0_attn_proj_b"),
                                   ("l3", "L3_attn_W_qkv", "L3_attn_b_qkv", "L3_attn_W_out", "L3_attn_b_out")):
        q, k, v = np.split(np.asarray(i[w]), 3)
        bq, bk, bv = np.split(np.asarray(i[bias]), 3)
        ins[layer + "_wq"], ins[layer + "_wk"], ins[layer + "_wv"] = dh(q), dh(k), t(v)
        ins[layer + "_bq"], ins[layer + "_bk"], ins[layer + "_bv"] = dhb(bq), dhb(bk), n(bv)
        ins[layer + "_wo"], ins[layer + "_bo"] = t(i[wo]), n(i[bo])
    ins["l3_gamma_beta"] = n(np.stack([np.asarray(i["L3_attn_ln_gamma"]), np.asarray(i["L3_attn_ln_beta"])], axis=1))
    ins["l0_rel"] = n(np.asarray(i["L0_attn_rel_pos_emb"])[P - 1:2 * P - 1])
    ins["l0_rel_back"] = n(np.asarray(i["L0_attn_rel_pos_emb"])[P - 1:2 * P - 1][::-1])
    ins["l1_gate"] = t(i["L1_ffn_gate_weight"])
    for m, shared in (("gate", "ws_gate"), ("up", "ws_up")):
        ins["l1_" + m + "_w"] = n(np.concatenate([np.asarray(i["L1_ffn_w_" + m]).reshape(-1, D).T,
                                                  np.asarray(i["L1_ffn_" + shared]).T], axis=1))
    ins["l1_down_w"] = n(np.concatenate([np.asarray(i["L1_ffn_w_down"]).transpose(0, 2, 1).reshape(-1, D),
                                         np.asarray(i["L1_ffn_ws_down"]).T], axis=0))
    ins["l1_wqk"] = n(np.concatenate([np.asarray(i["L1_attn_" + w]).T for w in ("Wq1", "Wk1", "Wq2", "Wk2", "Wv")], axis=1))
    ins["l1_wo"], ins["l1_bo"] = t(i["L1_attn_Wo"]), n(i["L1_attn_bo"])
    ins["l2_gate"] = t(i["L2_ffn_w_gate"])
    ins["l2_w_in"] = n(np.asarray(i["L2_ffn_w_in"]).reshape(E * HID, D))
    ins["l2_w_out"] = n(np.asarray(i["L2_ffn_w_out"]).transpose(0, 2, 1).reshape(E * HID, D))
    ins["l2_win"], ins["l2_wout"] = n(i["L2_attn_W_in"]), n(i["L2_attn_W_out"])
    ins["l2_bin"] = n(np.asarray(i["L2_attn_b_in"]).reshape(2, P).T)
    ins["l2_bout"] = n(i["L2_attn_b_out"])
    return ins


def kernel(**inputs):
    import concourse.bacc as bacc
    from concourse.bass_utils import run_bass_kernel_spmd
    arrays = lay_out(inputs)
    nc = bacc.Bacc("TRN2", target_bir_lowering=False, num_devices=1)
    a = {n: nc.dram_tensor(n, v.shape, F32, kind="ExternalInput").ap() for n, v in arrays.items()}
    out = nc.dram_tensor("x_out", (TOKENS, D), F32, kind="ExternalOutput").ap()
    program(nc, a, out)
    got = run_bass_kernel_spmd(nc, [arrays], core_ids=[0]).results[0]["x_out"]
    return got.reshape(B, T, D)
```

```python
from contextlib import ExitStack

import concourse.bass as bass
from concourse import mybir
from concourse.bass import IndirectOffsetOnAxis

F32 = mybir.dt.float32
BF16 = mybir.dt.bfloat16
U32 = mybir.dt.uint32
ALU = mybir.AluOpType
ACT = mybir.ActivationFunctionType
AX = mybir.AxisListType.X

P = 128
B, T, D = 4, 512, 128
TOKENS = B * T
TILES = TOKENS // P
GROUP = T // P
E = 8
HID = 512
CH = HID // P
HEADS, HD = 16, 8
EPS = 1e-5
CAP0 = -(-5 * TOKENS // (4 * E))
CAP3 = 2 * -(-TOKENS // E)
OUT_OF_BOUNDS = 1.0e6
MASKED = -1.0e30


def semaphores(g, name):
    def sem(n):
        g.spent.append((name, g.nc.alloc_semaphore(f"{name}_{n}")))
        return g.spent[-1][1]

    return sem


def clear_semaphores(g, kept=()):
    g.nc.clear_and_free_semaphores([s for name, s in g.spent if name not in kept])
    g.nc.all_engine_barrier(sem_only=True)
    g.spent[:] = [(name, s) for name, s in g.spent if name in kept]


class LayerNormSems:
    def __init__(self, sem, twice=False, gate=None):
        self.stats, self.moments, self.var_eps = sem("ln_stats"), sem("ln_moments"), sem("ln_var_eps")
        self.rstd, self.xn = sem("ln_rstd"), sem("ln_rows")
        self.xnt_psum, self.xnt = sem("ln_rows_transposed"), sem("ln_columns")
        self.twice = twice
        self.gate = gate
        if gate is not None:
            self.logits_psum, self.logits = sem("ln_logits_psum"), sem("ln_logits")
        if twice:
            self.outer = LayerNormSems(lambda n: sem("outer_" + n))
            self.summed = sem("ln_summed")


def ln_stats(g, v, s, b, src=None):
    ln_tile_stats(g, v, s, b, src)
    ln_moments(g, v, s, b)


def ln_tile_stats(g, v, s, b, src=None):
    src = g.x if src is None else src
    for i in range(GROUP * b, GROUP * (b + 1)):
        g.nc.vector.bn_stats(g.stats[:, i, :], src[:, i, 0:D]).then_inc(s.stats, 1)


def ln_moments(g, v, s, b):
    nc = g.nc
    v.wait_ge(s.stats, GROUP * (b + 1))
    for i in range(GROUP * b, GROUP * (b + 1)):
        nc.vector.bn_aggr(g.moments[:, i, :], g.stats[:, i, :]).then_inc(s.moments, 1)
    v.wait_ge(s.moments, GROUP * (b + 1))
    nc.vector.tensor_scalar(g.var_eps[:, GROUP * b:GROUP * (b + 1)],
                            g.moments[:, GROUP * b:GROUP * (b + 1), 1],
                            EPS, None, ALU.add).then_inc(s.var_eps, 1)


def ln_rstd(g, pool, s, b):
    cols = slice(GROUP * b, GROUP * (b + 1))
    pool.wait_ge(s.var_eps, b + 1)
    g.nc.gpsimd.tensor_tensor(g.rstd[:, cols], g.var_eps[:, cols], g.neg_half[:, cols],
                              ALU.pow).then_inc(s.rstd, 1)


def ln_rows(g, v, s, b, src=None):
    src = g.x if src is None else src
    v.wait_ge(s.rstd, b + 1)
    for i in range(GROUP * b, GROUP * (b + 1)):
        g.nc.vector.tensor_scalar(g.xn[:, i, 0:D], src[:, i, 0:D], g.moments[:, i, 0:1],
                                  g.rstd[:, i:i + 1], ALU.subtract, ALU.mult).then_inc(s.xn, 1)


def ln_outer(g, v, s, b):
    ln_rows(g, v, s.outer, b)
    v.wait_ge(s.outer.xn, GROUP * (b + 1))
    tiles = slice(GROUP * b, GROUP * (b + 1))
    g.nc.vector.tensor_tensor(g.x[:, tiles, :], g.x[:, tiles, :], g.xn[:, tiles, 0:D], ALU.add).then_inc(s.summed, 1)
    ln_stats(g, v, s, b, src=g.xn)


def ln_inner(g, v, s, b):
    v.wait_ge(s.summed, b + 1)
    ln_rows(g, v, s, b, src=g.xn)


def ln_transpose(g, pe, s, b, bank, one_bank=False):
    pe.wait_ge(s.xn, GROUP * (b + 1))
    if one_bank and b >= 1:
        pe.wait_ge(s.xnt if s.gate is None else s.logits, b)
    for j in range(GROUP):
        mm = g.nc.tensor.transpose(bank[:, j * P:(j + 1) * P], g.xn[:, GROUP * b + j, 0:D], g.ident[:])
    mm.then_inc(s.xnt_psum, 1)


def ln_columns(g, act, s, b, bank):
    act.wait_ge(s.xnt_psum, b + 1)
    dst = g.xnt[:, b * T:(b + 1) * T]
    if s.twice:
        g.nc.scalar.activation(dst, bank[:], ACT.Identity, bias=g.gamma_beta[:, 1:2], scale=g.gamma_beta[:, 0:1]
                               ).then_inc(s.xnt, 1)
    else:
        g.nc.scalar.copy(dst, bank[:]).then_inc(s.xnt, 1)


def ln_logits(g, pe, s, b, bank):
    if s.gate is None:
        return
    pe.wait_ge(s.xnt, b + 1)
    for j in range(GROUP):
        i = GROUP * b + j
        mm = g.nc.tensor.matmul(bank[:, j * E:(j + 1) * E], g.xnt[:, i * P:(i + 1) * P], s.gate, start=True, stop=True)
    mm.then_inc(s.logits_psum, 1)


def ln_copy_logits(g, act, s, b, bank):
    if s.gate is None:
        return
    act.wait_ge(s.logits_psum, b + 1)
    g.nc.scalar.copy(g.logits[:, GROUP * b:GROUP * (b + 1), :],
                     bank[:, 0:GROUP * E].rearrange("p (t e) -> p t e", e=E)).then_inc(s.logits, 1)


def ln_columns_and_logits(g, act, s, groups, banks):
    for b in groups:
        ln_columns(g, act, s, b, banks(b))
        if b - 1 in groups:
            ln_copy_logits(g, act, s, b - 1, banks(b - 1))
    ln_copy_logits(g, act, s, groups[-1], banks(groups[-1]))


def ln_transpose_and_logits(g, pe, s, groups, banks):
    for b in groups:
        ln_transpose(g, pe, s, b, banks(b))
        if b - 1 in groups:
            ln_logits(g, pe, s, b - 1, banks(b - 1))
    ln_logits(g, pe, s, groups[-1], banks(groups[-1]))


def write_untaken(g, queue, mixtures):
    for n in mixtures:
        rows = g.dispatched[n]
        queue.dma_start(rows.rearrange("(p j) d -> p j d", p=P),
                        g.untaken[:, None, :].to_broadcast([P, rows.shape[0] // P, D + 1])).then_inc(g.untaken_written[n], 16)


def setup(g, beside):
    nc = g.nc
    with ExitStack() as ctx:
        sem = semaphores(g, "setup")
        loaded = [sem(f"x_loaded{b}") for b in range(B)]
        small_loaded, made, ident_made, masked = sem("small_loaded"), sem("made"), sem("ident_made"), sem("masks")
        ln = LayerNormSems(sem, gate=g.gates[:, 0, :])
        block = ctx.enter_context(nc.Block(no_gpsimd_drain=True))

        @block.sync
        def _(sp):
            for b in range(B):
                sp.dma_start(g.x[:, GROUP * b:GROUP * (b + 1), :],
                             g.a["x"][b * T:(b + 1) * T, :].rearrange("(i p) d -> p i d", p=P)).then_inc(loaded[b], 16)
            for k, n in enumerate(("l0_gate", "l1_gate", "l2_gate", "l3_gate")):
                sp.dma_start(g.gates[:, k, :], g.a[n]).then_inc(small_loaded, 16)
            beside.load(sp)
            sp.dma_start(g.gamma_beta[:], g.a["l3_gamma_beta"]).then_inc(small_loaded, 16)
            sp.wait_ge(made, 2)
            write_untaken(g, sp, (0,))
            of_partition = g.returned.shape[0] // P
            sp.dma_start(g.returned.rearrange("(p j) d -> p j d", p=P),
                         g.untaken[:, None, 0:D].to_broadcast([P, of_partition, D])).then_inc(g.returned_zeroed, 16)
            sp.wait_ge(small_loaded, 16 * 5)

        @block.tensor
        def _(pe):
            pe.wait_ge(ident_made, 2)
            pe.wait_ge(small_loaded, 16 * 5)
            ln_transpose_and_logits(g, pe, ln, range(B), lambda b: g.bank[b])
            beside.turn(pe, g.bank[B])

        @block.scalar
        def _(act):
            ln_columns_and_logits(g, act, ln, range(B), lambda b: g.bank[b])
            beside.copy_lines(act, g.bank[B])
            beside.store_lines(act)
            act.wait_ge(masked, 7)
            nc.scalar.copy(g.xn[:, :, D], g.token[:, 0:TILES])

        @block.vector
        def _(v):
            nc.vector.memset(g.neg_half[:], -0.5)
            nc.vector.memset(g.untaken[:], 0.0).then_inc(made, 1)
            v.wait_ge(made, 1)
            nc.vector.memset(g.untaken[:, D:D + 1], OUT_OF_BOUNDS).then_inc(made, 1)
            for e in range(E):
                nc.vector.memset(g.rev[:, :, e], float(E - e))
            for b in range(B):
                v.wait_ge(loaded[b], 16)
                ln_stats(g, v, ln, b)
                if b >= 1:
                    ln_rows(g, v, ln, b - 1)
            ln_rows(g, v, ln, B - 1)
            beside.sum_heads(v)

        @block.gpsimd
        def _(pool):
            n = [0]

            def after(ins):
                n[0] += 1
                ins.then_inc(masked, 1)
                pool.wait_ge(masked, n[0])

            nc.gpsimd.memset(g.ident[:], 0.0).then_inc(ident_made, 1)
            pool.wait_ge(ident_made, 1)
            nc.gpsimd.affine_select(out=g.ident[:], in_=g.ident[:], compare_op=ALU.not_equal, fill=1.0,
                                    base=0, pattern=[[-1, P]], channel_multiplier=1).then_inc(ident_made, 1)
            pool.wait_ge(ident_made, 2)
            for b in range(B):
                ln_rstd(g, pool, ln, b)
            after(nc.gpsimd.tensor_copy(g.identb[:], g.ident[:]))
            after(nc.gpsimd.memset(g.flip[:], 0.0))
            after(nc.gpsimd.affine_select(out=g.flip[:], in_=g.flip[:], compare_op=ALU.not_equal, fill=1.0,
                                          base=1 - P, pattern=[[1, P]], channel_multiplier=1))
            after(nc.gpsimd.memset(g.onesb[:], 1.0))
            after(nc.gpsimd.affine_select(out=g.beforeb[:], in_=g.onesb[:], compare_op=ALU.is_ge, fill=0.0,
                                          base=-1, pattern=[[1, P]], channel_multiplier=-1))
            after(nc.gpsimd.iota(g.token_i[:], pattern=[[P, 2 * TILES]], base=0, channel_multiplier=1))
            after(nc.gpsimd.tensor_copy(g.token[:], g.token_i[:]))
            for t, base in ((g.head_selector, MAX_AT), (g.head_selector1, MAX_AT1)):
                after(nc.gpsimd.memset(t[:], 0.0))
                for part in range(PARTS):
                    after(nc.gpsimd.affine_select(out=t[:], in_=t[:], compare_op=ALU.not_equal, fill=1.0,
                                                  base=-(base + part * GH), pattern=[[-1, GH]], channel_multiplier=1))
            after(nc.gpsimd.memset(g.expert_selector[:], 0.0))
            chunks = g.expert_selector[:].rearrange("p c (h r) -> p c h r", h=2)
            for part in range(PARTS):
                after(nc.gpsimd.affine_select(out=chunks, in_=chunks, compare_op=ALU.not_equal, fill=1.0,
                                              base=-part * E, pattern=[[-2, E // 2], [-1, 2], [0, P // 2]], channel_multiplier=1))
            after(nc.gpsimd.memset(g.mask_kq[:], 0.0))
            after(nc.gpsimd.affine_select(out=g.mask_kq[:], in_=g.mask_kq[:], compare_op=ALU.is_ge, fill=MASKED,
                                          base=0, pattern=[[1, P]], channel_multiplier=-1))
            after(nc.gpsimd.memset(g.mask_qk[:], 0.0))
            after(nc.gpsimd.affine_select(out=g.mask_qk[:, T - P:T], in_=g.mask_qk[:, T - P:T],
                                          compare_op=ALU.is_ge, fill=MASKED,
                                          base=0, pattern=[[-1, P]], channel_multiplier=1))


def first_max(g, after, scores, best, work, onehot):
    for step in range(5):
        after(first_max_step(g, step, scores, best, work, onehot, g.tie[:]))


def first_max_step(g, step, scores, best, work, onehot, tie):
    v, tiles = g.nc.vector, scores.shape[1]
    wide = [P, tiles, E]
    if step == 0:
        return v.tensor_reduce(best, scores, axis=AX, op=ALU.max)
    if step == 1:
        return v.tensor_tensor(work, scores, best[:, :, None].to_broadcast(wide), ALU.is_equal)
    if step == 2:
        return v.tensor_tensor(work, work, g.rev[:, 0:tiles, :], ALU.mult)
    if step == 3:
        return v.tensor_reduce(tie, work, axis=AX, op=ALU.max)
    return v.tensor_tensor(onehot, work, tie[:, :, None].to_broadcast(wide), ALU.is_equal)


class Routing:
    CHOOSE, PLACE = 5, 7

    def __init__(self, g, ctx, name, n, choices, cap):
        sem = semaphores(g, name)
        sb = lambda n, shape, dt=F32: ctx.enter_context(g.nc.sbuf_tensor(f"{name}_{n}", shape, dt))
        self.g, self.choices, self.cap = g, choices, cap
        self.slots, self.dispatched, self.untaken_written = E * cap, g.dispatched[n], g.untaken_written[n]
        self.step, self.chosen, self.counted, self.taken, self.slots_ready, self.scattered = (sem(n) for n in (
            "routing_step", "chosen", "ranks_counted", "ranks_taken", "slots", "scattered"))
        self.steps = 0
        picks = choices * TILES
        self.best, self.tie = sb("best", [P, choices, TILES]), sb("expert_from_last", [P, choices, TILES])
        self.hot = sb("onehot", [P, choices, TILES, E], BF16)
        self.work, self.rest = sb("route_work", [P, GROUP, E]), sb("rest_logits", [P, GROUP, E])
        self.product = sb("rank_products", [P, TILES, E])
        self.base, self.rank, self.keep = sb("base", [P, picks]), sb("rank", [P, picks]), sb("keep", [P, picks])
        self.slot, self.scatter_i = sb("slot", [P, picks]), sb("scatter_i", [P, picks], U32)

    def mark(self, ins):
        self.steps += 1
        ins.then_inc(self.step, 1)

    def own_last(self, v):
        if self.steps:
            v.wait_ge(self.step, self.steps)

    def choose_step(self, v, step, c, b):
        g = self.g
        group = slice(GROUP * b, GROUP * (b + 1))
        self.own_last(v)
        if step == 0 and c == 1:
            v.wait_ge(self.chosen, self.choices * b + 1)
            self.mark(g.nc.vector.scalar_tensor_tensor(self.rest[:], self.hot[:, 0, group, :], MASKED, g.logits[:, group, :],
                                                       ALU.mult, ALU.add))
            self.own_last(v)
        ins = first_max_step(g, step, g.logits[:, group, :] if c == 0 else self.rest[:], self.best[:, c, group], self.work[:],
                             self.hot[:, c, group, :], self.tie[:, c, group])
        if step == self.CHOOSE - 1:
            ins.then_inc(self.chosen, 1)
        else:
            self.mark(ins)

    def choose(self, v, c, b):
        for step in range(self.CHOOSE):
            self.choose_step(v, step, c, b)

    def count(self, pe, b, bank):
        g, nc = self.g, self.g.nc
        pe.wait_ge(self.chosen, self.choices * b + 1)
        group = slice(GROUP * b, GROUP * (b + 1))
        nc.tensor.matmul(bank[:, 0:GROUP * E], g.beforeb[:], self.hot[:, 0, group, :].rearrange("p k e -> p (k e)"),
                         start=True, stop=False)
        for k in range(GROUP * (b + 1) - 1):
            t = max(0, k + 1 - GROUP * b)
            mm = nc.tensor.matmul(bank[:, t * E:GROUP * E], g.onesb[:],
                                  self.hot[:, 0, k:k + 1, :].to_broadcast([P, GROUP - t, E]),
                                  start=False, stop=k == GROUP * (b + 1) - 2)
        mm.then_inc(self.counted, 1)

    def count_second(self, pe, bank):
        g, nc = self.g, self.g.nc
        for k in range(TILES):
            if k % GROUP == 0:
                pe.wait_ge(self.chosen, 2 * (k // GROUP) + 1)
            nc.tensor.matmul(bank[:, 0:TILES * E], g.onesb[:], self.hot[:, 0, k:k + 1, :].to_broadcast([P, TILES, E]),
                             start=k == 0, stop=False)
        pe.wait_ge(self.chosen, 2 * B)
        nc.tensor.matmul(bank[:, 0:TILES * E], g.beforeb[:], self.hot[:, 1, :, :].rearrange("p k e -> p (k e)"),
                         start=False, stop=False)
        for k in range(TILES - 1):
            mm = nc.tensor.matmul(bank[:, (k + 1) * E:TILES * E], g.onesb[:],
                                  self.hot[:, 1, k:k + 1, :].to_broadcast([P, TILES - 1 - k, E]),
                                  start=False, stop=k == TILES - 2)
        mm.then_inc(self.counted, 1)

    def place_step(self, v, step, c, first, tiles, bank):
        ops = self.g.nc.vector
        nth = (first + tiles) // GROUP + c
        mine, here = slice(c * TILES + first, c * TILES + first + tiles), slice(first, first + tiles)
        self.own_last(v)
        if step == 0:
            self.mark(ops.tensor_scalar(self.base[:, mine], self.tie[:, c, here], -float(self.cap),
                                        float(self.slots) - OUT_OF_BOUNDS, ALU.mult, ALU.add))
        elif step == 1:
            v.wait_ge(self.chosen, self.choices * ((first + tiles) // GROUP - 1) + c + 1)
            v.wait_ge(self.counted, nth)
            ops.tensor_tensor(self.product[:, 0:tiles, :], bank[:, 0:tiles * E].rearrange("p (k e) -> p k e", e=E),
                              self.hot[:, c, here, :], ALU.mult).then_inc(self.taken, 1)
        elif step == 2:
            v.wait_ge(self.taken, nth)
            self.mark(ops.tensor_reduce(self.rank[:, mine], self.product[:, 0:tiles, :], axis=AX, op=ALU.add))
        elif step == 3:
            self.mark(ops.tensor_scalar(self.keep[:, mine], self.rank[:, mine], float(self.cap), None, ALU.is_lt))
        elif step == 4:
            self.mark(ops.tensor_tensor(self.slot[:, mine], self.base[:, mine], self.rank[:, mine], ALU.add))
        elif step == 5:
            self.mark(ops.tensor_tensor(self.slot[:, mine], self.slot[:, mine], self.keep[:, mine], ALU.mult))
        else:
            ops.tensor_scalar(self.scatter_i[:, mine], self.slot[:, mine], OUT_OF_BOUNDS, None, ALU.add
                              ).then_inc(self.slots_ready, 1)

    def place(self, v, c, first, tiles, bank):
        for step in range(self.PLACE):
            self.place_step(v, step, c, first, tiles, bank)

    def scatter(self, pool, c, first, tiles, rows):
        if c == 0 and first == 0:
            pool.wait_ge(self.untaken_written, 16)
        pool.wait_ge(self.slots_ready, (first + tiles) // GROUP + c)
        for k in range(first, first + tiles):
            at = c * TILES + k
            self.g.nc.gpsimd.indirect_dma_start(
                out=self.dispatched[0:self.slots, :],
                out_offset=IndirectOffsetOnAxis(ap=self.scatter_i[:, at:at + 1], axis=0),
                in_=rows[:, k, :], in_offset=None,
                bounds_check=self.slots - 1, oob_is_err=False).then_inc(self.scattered, 16)


def moe_capacity(g, name, routing, routed, w1, b1, w2, b2, last=False, twice=False, gate=None, beside=None, prefetch=None,
                 products=None):
    nc = g.nc
    choices, cap, dispatched = routing.choices, routing.cap, routing.dispatched
    full, rest = cap // P, cap % P
    sizes = [P] * full + [rest] * (rest > 0)
    nt = len(sizes)
    picks = choices * TILES
    tile_loads = 1 + (rest > 0)
    with ExitStack() as ctx:
        sem = semaphores(g, name)
        sb = lambda n, shape, dt=F32: ctx.enter_context(nc.sbuf_tensor(f"{name}_{n}", shape, dt))
        ln = None if last else LayerNormSems(sem, twice, gate)
        small_loaded = sem("biases_loaded")
        w_loaded = [sem("w_loaded0"), sem("w_loaded1")]
        d_loaded = [sem("slots_loaded0"), sem("slots_loaded1")]
        route, exp_in, exp_out = sem("route"), sem("exp_in"), sem("exp_out")
        dt_psum, dt_ready = sem("slots_transposed"), sem("slot_columns")
        h_psum, h_ready = sem("hidden_psum"), sem("hidden")
        o_psum, o_ready = sem("out_psum"), sem("out_rows")
        stored = [sem("stored0"), sem("stored1")]
        numbered, numbers_ready, added = sem("rows_numbered"), sem("slot_tokens"), sem("added")
        x_stored = sem("x_stored") if last else None
        returned = [sem(f"rows_returned{b}") for b in range(B)]

        xn2 = sb("second_rows", [P, TILES, D + 1]) if choices == 2 else None
        b1_sb = sb("b1", [P, E * CH])
        b2_sb = sb("b2", [P, E, D])
        w1_sb = [sb(f"w1_{i}", [P, HID]) for i in range(2)]
        w2_sb = [sb(f"w2_{i}", [P, CH, D]) for i in range(2)]
        d_sb = [sb(f"slots_{i}", [P, nt, D + 1]) for i in range(2)]
        dt_sb = [sb(f"slot_columns_{i}", [P, cap]) for i in range(2)]
        h_sb = [sb(f"hidden_{i}", [P, CH, cap]) for i in range(2)]
        o_sb = [sb(f"out_{i}", [P, nt, D]) for i in range(2)]
        slot_token = [sb(f"slot_tokens_{i}", [P, nt], U32) for i in range(2)]
        logits = g.logits
        best, keep = routing.best, routing.keep
        expd = sb("expd", [P, TILES, E])
        gates = sb("gates", [P, choices, TILES])
        denom = sb("denom", [P, TILES])
        weight = sb("weight", [P, picks])
        back = sb("back", [P, picks, D])

        xnt_bank = [g.bank[0], g.bank[1]]
        beside_banks = (g.bank[6:8], g.bank[0:2])
        rank_bank = g.bank[2:7]
        to_route = range(routed, B)
        h_bank = g.bank[2:6]
        o_bank = g.bank[6:8]
        block = ctx.enter_context(nc.Block(no_gpsimd_drain=True))

        @block.sync
        def _(sp):
            if prefetch:
                prefetch.load(sp)
            sp.dma_start(b1_sb[:], b1).then_inc(small_loaded, 16)
            sp.dma_start(b2_sb[:], b2.rearrange("e d -> (e d)").partition_broadcast(P)).then_inc(small_loaded, 16)

            def load_weights(e, i):
                sp.dma_start(w1_sb[i][:], w1[bass.ds(e * P, P), :]).then_inc(w_loaded[i], 16)
                sp.dma_start(w2_sb[i][:], w2[bass.ds(e * HID, HID), :].rearrange("(c p) d -> p c d", p=P)
                             ).then_inc(w_loaded[i], 16)

            def load_slots(e, i):
                sp.dma_start(d_sb[i][:, 0:full, :],
                             dispatched[bass.ds(e * cap, full * P), :].rearrange("(t p) d -> p t d", p=P)
                             ).then_inc(d_loaded[i], 16)
                if rest:
                    sp.dma_start(d_sb[i][0:rest, full, :], dispatched[bass.ds(e * cap + full * P, rest), :]
                                 ).then_inc(d_loaded[i], 16)

            for i in range(2):
                load_weights(i, i)
            sp.wait_ge(routing.scattered, 16 * picks)
            for i in range(2):
                load_slots(i, i)
            with sp.Fori(0, E // 2 - 1) as k:
                for i in range(2):
                    sp.wait_ge(dt_psum, 2 * k + i + 1)
                    sp.wait_ge(numbers_ready, 2 * k + i + 1)
                    load_slots(2 * k + i + 2, i)
                    sp.wait_ge(o_psum, 2 * k + i + 1)
                    load_weights(2 * k + i + 2, i)
            for i in range(2):
                sp.wait_ge(stored[i], 16 * nt * (E // 2))
            for b in range(B):
                for c in range(choices):
                    at = c * TILES + GROUP * b
                    sp.dma_start(back[:, at:at + GROUP, :],
                                 g.returned[c * TOKENS + b * T:c * TOKENS + (b + 1) * T, :].rearrange("(j p) d -> p j d", p=P)
                                 ).then_inc(returned[b], 16)
            if last:
                for b in range(B):
                    sp.wait_ge(added, choices * GROUP * (b + 1))
                    sp.dma_start(g.out[b * T:(b + 1) * T, :].rearrange("(i p) d -> p i d", p=P),
                                 g.x[:, GROUP * b:GROUP * (b + 1), :]).then_inc(x_stored, 16)
                sp.wait_ge(x_stored, 16 * B)

        @block.tensor
        def _(pe):
            for b in to_route:
                routing.count(pe, b, rank_bank[b])
            if choices == 2:
                routing.count_second(pe, rank_bank[B])
            pe.wait_ge(routing.taken, B + choices - 1)
            if beside:
                beside.flip(pe, beside_banks)

            def turn_slots(e, i, nth):
                pe.wait_ge(d_loaded[i], 16 * tile_loads * nth)
                for t, n in enumerate(sizes):
                    mm = nc.tensor.transpose(xnt_bank[i][:, t * P:t * P + n], d_sb[i][0:n, t, 0:D], g.ident[0:n, 0:n])
                mm.then_inc(dt_psum, 1)

            def hidden(e, i, nth):
                pe.wait_ge(dt_ready, e + 1)
                pe.wait_ge(w_loaded[i], 32 * nth)
                for c in range(CH):
                    nc.tensor.matmul(h_bank[c][:, 0:cap], w1_sb[i][:, c * P:(c + 1) * P], dt_sb[i][:],
                                     start=True, stop=True).then_inc(h_psum, 1)

            def output(e, i):
                pe.wait_ge(h_ready, CH * (e + 1))
                for t, n in enumerate(sizes):
                    for c in range(CH):
                        mm = nc.tensor.matmul(o_bank[i][0:n, t * D:(t + 1) * D],
                                              h_sb[i][:, c, t * P:t * P + n], w2_sb[i][:, c, :],
                                              start=(c == 0), stop=(c == CH - 1))
                mm.then_inc(o_psum, 1)

            if beside:
                pe.wait_ge(beside.copied, HEADS // 2)
                pe.wait_ge(beside.split_done, HEADS // 2)
            turn_slots(0, 0, 1)
            with pe.Fori(0, E // 2 - 1) as k:
                for i in range(2):
                    hidden(2 * k + i, i, k + 1)
                    turn_slots(2 * k + i + 1, 1 - i, k + 1 + i)
                    pe.wait_ge(o_ready, 2 * k + i + 1)
                    output(2 * k + i, i)
            for e in (E - 2, E - 1):
                hidden(e, e % 2, E // 2)
                if e == E - 2:
                    turn_slots(E - 1, 1, E // 2)
                pe.wait_ge(o_ready, e + 1)
                output(e, e % 2)
            if products:
                pe.wait_ge(dt_ready, E)
                products.multiply(pe, xnt_bank)
            if not last:
                ln_transpose_and_logits(g, pe, ln, range(B), lambda b: g.bank[2 + b])

        @block.scalar
        def _(act):
            if beside:
                beside.load_tiles(act)
            if choices == 2:
                nc.scalar.copy(xn2[:, :, 0:D], g.xn[:, :, 0:D])
                nc.scalar.copy(xn2[:, :, D], g.token[:, TILES:2 * TILES]).then_inc(numbered, 1)
            act.wait_ge(exp_in, 1)
            nc.scalar.activation(expd[:] if choices == 1 else expd[:, :, 0], expd[:] if choices == 1 else expd[:, :, 0],
                                 ACT.Exp).then_inc(exp_out, 1)
            if beside:
                beside.copy(act, beside_banks)
            act.wait_ge(small_loaded, 32)

            def copy_columns(e, i):
                act.wait_ge(dt_psum, e + 1)
                nc.scalar.copy(dt_sb[i][:], xnt_bank[i][:, 0:cap]).then_inc(dt_ready, 1)

            def hidden(e, i):
                for c in range(CH):
                    act.wait_ge(h_psum, CH * e + c + 1)
                    nc.scalar.activation(h_sb[i][:, c, :], h_bank[c][:, 0:cap], ACT.Relu,
                                         bias=b1_sb[:, bass.ds(e * CH + c, 1)]).then_inc(h_ready, 1)

            copy_columns(0, 0)
            if products:
                products.load(act)
            with act.Fori(0, E // 2 - 1) as k:
                for i in range(2):
                    hidden(2 * k + i, i)
                    copy_columns(2 * k + i + 1, 1 - i)
            hidden(E - 2, 0)
            copy_columns(E - 1, 1)
            hidden(E - 1, 1)
            if products:
                products.copy(act, xnt_bank)
            if not last:
                ln_columns_and_logits(g, act, ln, range(B), lambda b: g.bank[2 + b])

        @block.vector
        def _(v):
            n = [0]

            def after(ins):
                n[0] += 1
                ins.then_inc(route, 1)
                v.wait_ge(route, n[0])

            nc.vector.memset(g.spare[:], 0.0).then_inc(o_ready, 2)
            for b in to_route:
                routing.choose(v, 0, b)
                if choices == 2:
                    routing.choose(v, 1, b)
                routing.place(v, 0, GROUP * b, GROUP, rank_bank[b])
            if choices == 2:
                routing.place(v, 1, 0, TILES, rank_bank[B])
            if choices == 1:
                nc.vector.tensor_tensor(expd[:], logits[:], best[:, 0, :, None].to_broadcast([P, TILES, E]),
                                        ALU.subtract).then_inc(exp_in, 1)
                v.wait_ge(exp_out, 1)
                after(nc.vector.tensor_reduce(denom[:], expd[:], axis=AX, op=ALU.add))
                after(nc.vector.reciprocal(gates[:, 0, :], denom[:]))
            else:
                nc.vector.tensor_tensor(expd[:, :, 0], best[:, 1, :], best[:, 0, :], ALU.subtract).then_inc(exp_in, 1)
                v.wait_ge(exp_out, 1)
                after(nc.vector.tensor_scalar(denom[:], expd[:, :, 0], 1.0, None, ALU.add))
                after(nc.vector.reciprocal(gates[:, 0, :], denom[:]))
                after(nc.vector.tensor_tensor(gates[:, 1, :], expd[:, :, 0], gates[:, 0, :], ALU.mult))
            after(nc.vector.scalar_tensor_tensor(weight[:], gates[:].rearrange("p k t -> p (k t)"), 0.5, keep[:],
                                                 ALU.mult, ALU.mult))
            if beside:
                beside.split(v, beside_banks)
            v.wait_ge(small_loaded, 32)
            for e in range(E):
                i, nth = e % 2, e // 2 + 1
                if e >= 2:
                    v.wait_ge(stored[i], 16 * nt * (nth - 1))
                v.wait_ge(d_loaded[i], 16 * tile_loads * nth)
                if rest:
                    nc.vector.tensor_copy(slot_token[i][0:rest, full:nt], d_sb[i][0:rest, full:nt, D])
                nc.vector.tensor_copy(slot_token[i][:, 0:full], d_sb[i][:, 0:full, D]).then_inc(numbers_ready, 1)
                v.wait_ge(o_psum, e + 1)
                if rest:
                    nc.vector.tensor_tensor(o_sb[i][0:rest, full, :], o_bank[i][0:rest, full * D:(full + 1) * D],
                                            b2_sb[0:rest, e, :], ALU.add)
                nc.vector.tensor_tensor(o_sb[i][:, 0:full, :], o_bank[i][:, 0:full * D].rearrange("p (t d) -> p t d", d=D),
                                        b2_sb[:, e:e + 1, :].to_broadcast([P, full, D]), ALU.add).then_inc(o_ready, 1)

            def add_rows(b):
                v.wait_ge(returned[b], 16 * choices)
                for c in range(choices):
                    if c:
                        v.wait_ge(added, (choices * b + c) * GROUP)
                    for j in range(GROUP * b, GROUP * (b + 1)):
                        k = c * TILES + j
                        nc.vector.scalar_tensor_tensor(g.x[:, j, :], back[:, k, :], weight[:, k:k + 1],
                                                       g.x[:, j, :], ALU.mult, ALU.add).then_inc(added, 1)

            for b in range(B + 2):
                if b < B:
                    add_rows(b)
                    if not last:
                        v.wait_ge(added, choices * GROUP * (b + 1))
                        ln_stats(g, v, ln.outer if twice else ln, b)
                if twice:
                    if 0 <= b - 1 < B:
                        ln_outer(g, v, ln, b - 1)
                    if 0 <= b - 2 < B:
                        ln_inner(g, v, ln, b - 2)
                elif not last and 0 <= b - 1 < B:
                    ln_rows(g, v, ln, b - 1)

        @block.gpsimd
        def _(pool):
            for b in to_route:
                routing.scatter(pool, 0, GROUP * b, GROUP, g.xn)
            if choices == 2:
                pool.wait_ge(numbered, 1)
                routing.scatter(pool, 1, 0, TILES, xn2)
            pool.wait_ge(g.returned_zeroed, 16)
            for e in range(E):
                pool.wait_ge(o_ready, e + 3)
                for t, m in enumerate(sizes):
                    nc.gpsimd.indirect_dma_start(
                        out=g.returned[0:choices * TOKENS, :],
                        out_offset=IndirectOffsetOnAxis(ap=slot_token[e % 2][0:m, t:t + 1], axis=0),
                        in_=o_sb[e % 2][0:m, t, :], in_offset=None,
                        bounds_check=choices * TOKENS - 1, oob_is_err=False).then_inc(stored[e % 2], 16)
            if not last:
                for b in range(B + 1):
                    if b < B:
                        ln_rstd(g, pool, ln.outer if twice else ln, b)
                    if twice and b >= 1:
                        ln_rstd(g, pool, ln, b - 1)


def ffn1(g, name, gate=None, prefetch=None):
    nc, a = g.nc, g.a
    routed, chunks = 4, 5
    wide = chunks * P
    with ExitStack() as ctx:
        sem = semaphores(g, name)
        sb = lambda n, shape, dt=F32: ctx.enter_context(nc.sbuf_tensor(f"{name}_{n}", shape, dt))
        ln = LayerNormSems(sem, gate=gate)
        loaded = sem("weights_loaded")
        scores_done, route = sem("scores_done"), sem("route")
        weights_ready, turned, columns_ready = sem("combine_ready"), sem("combine_turned"), sem("combine_columns")
        g_psum, u_psum, cb_psum, y_psum = sem("gate_psum"), sem("up_psum"), sem("combine_psum"), sem("y_psum")
        silu_done, gated, hidden, summed = sem("silu_done"), sem("gated"), sem("hidden"), sem("summed")

        xnt = g.xnt
        wg_sb, wu_sb = sb("wg", [P, wide]), sb("wu", [P, wide])
        wd_sb = sb("wd", [P, chunks, D])
        scores, others, work = (sb(n, [P, TILES, E]) for n in ("scores", "others", "work"))
        best = sb("best", [P, 2, TILES])
        onehot = sb("onehot", [P, 2, TILES, E])
        denom = sb("denom", [P, TILES])
        combine = sb("combine", [P, TILES, E])
        combine_parts = sb("combine_parts", [P, TILES, P], BF16)
        combine_t = sb("combine_t", [P, TOKENS], BF16)
        silu = sb("silu", [P, 2, T])
        prod = sb("prod", [P, 2, T])
        hid = sb("hid", [P, 2, chunks, T])

        xnt_bank, turn_bank = g.bank[0], g.bank[1]
        g_bank, u_bank = g.bank[2:4], g.bank[4:6]
        cb_bank, y_bank = g.bank[6], g.bank[7]
        units = [(b, c) for b in range(B) for c in range(chunks)]
        block = ctx.enter_context(nc.Block(no_gpsimd_drain=True))

        @block.sync
        def _(sp):
            sp.dma_start(wg_sb[:], a["l1_gate_w"]).then_inc(loaded, 16)
            sp.dma_start(wu_sb[:], a["l1_up_w"]).then_inc(loaded, 16)
            sp.dma_start(wd_sb[:], a["l1_down_w"].rearrange("(c p) d -> p c d", p=P)).then_inc(loaded, 16)
            if prefetch:
                prefetch.load(sp)

        @block.tensor
        def _(pe):
            pe.wait_ge(loaded, 48)

            def down(b):
                pe.wait_ge(hidden, chunks * (b + 1))
                if b >= 1:
                    pe.wait_ge(summed, b)
                for i in range(GROUP):
                    for c in range(chunks):
                        mm = nc.tensor.matmul(y_bank[:, i * D:(i + 1) * D], hid[:, b % 2, c, i * P:(i + 1) * P],
                                              wd_sb[:, c, :], start=(c == 0), stop=(c == chunks - 1))
                mm.then_inc(y_psum, 1)

            def gate_up(k):
                b, c = units[k]
                columns = xnt[:, b * T:(b + 1) * T]
                if k >= 2:
                    pe.wait_ge(silu_done, k - 1)
                    pe.wait_ge(gated, k - 1)
                nc.tensor.matmul(g_bank[k % 2][:], wg_sb[:, c * P:(c + 1) * P], columns,
                                 start=True, stop=True).then_inc(g_psum, 1)
                nc.tensor.matmul(u_bank[k % 2][:], wu_sb[:, c * P:(c + 1) * P], columns,
                                 start=True, stop=True).then_inc(u_psum, 1)

            gate_up(0)
            gate_up(1)
            pe.wait_ge(weights_ready, 2)
            for i in range(TILES):
                if i == 8:
                    pe.wait_ge(columns_ready, 1)
                mm = nc.tensor.transpose(turn_bank[:].bitcast(BF16)[:, (i % 8) * P:(i % 8 + 1) * P],
                                         combine_parts[:, i, :], g.identb[:])
                if i % 8 == 7:
                    mm.then_inc(turned, 1)
            for k, (b, c) in enumerate(units):
                if 2 <= k + 1 < len(units):
                    gate_up(k + 1)
                if c < routed:
                    pe.wait_ge(columns_ready, 1 + b // 2)
                    if k >= 1:
                        pe.wait_ge(hidden, k)
                    nc.tensor.matmul(cb_bank[:], g.expert_selector[:, c, :], combine_t[:, b * T:(b + 1) * T],
                                     start=True, stop=True).then_inc(cb_psum, 1)
                if c == 1 and b >= 1:
                    down(b - 1)
                if c == 0 and b >= 2:
                    ln_transpose(g, pe, ln, b - 2, xnt_bank, one_bank=True)
                if c == 2 and b >= 2:
                    ln_logits(g, pe, ln, b - 2, xnt_bank)
            ln_transpose(g, pe, ln, B - 2, xnt_bank, one_bank=True)
            down(B - 1)
            ln_logits(g, pe, ln, B - 2, xnt_bank)
            ln_transpose(g, pe, ln, B - 1, xnt_bank, one_bank=True)
            ln_logits(g, pe, ln, B - 1, xnt_bank)

        @block.scalar
        def _(act):
            nc.scalar.activation(scores[:], g.logits[:], ACT.Sigmoid).then_inc(scores_done, 1)

            def copy_combine(half):
                act.wait_ge(turned, half + 1)
                nc.scalar.copy(combine_t[:, half * 2 * T:(half + 1) * 2 * T], turn_bank[:].bitcast(BF16)
                               ).then_inc(columns_ready, 1)

            for k, (b, c) in enumerate(units):
                act.wait_ge(g_psum, k + 1)
                if k >= 2:
                    act.wait_ge(gated, k - 1)
                nc.scalar.activation(silu[:, k % 2, :], g_bank[k % 2][:], ACT.Silu).then_inc(silu_done, 1)
                if k == 1:
                    copy_combine(0)
                    copy_combine(1)
                if c == 1 and b >= 2:
                    ln_columns(g, act, ln, b - 2, xnt_bank)
                if c == 3 and b >= 2:
                    ln_copy_logits(g, act, ln, b - 2, xnt_bank)
            ln_columns(g, act, ln, B - 2, xnt_bank)
            ln_copy_logits(g, act, ln, B - 2, xnt_bank)
            ln_columns(g, act, ln, B - 1, xnt_bank)
            ln_copy_logits(g, act, ln, B - 1, xnt_bank)

        @block.vector
        def _(v):
            n = [0]

            def after(ins):
                n[0] += 1
                ins.then_inc(route, 1)
                v.wait_ge(route, n[0])

            nc.vector.memset(combine_parts[:].bitcast(F32), 0.0).then_inc(weights_ready, 1)
            v.wait_ge(scores_done, 1)
            first_max(g, after, scores[:], best[:, 0, :], work[:], onehot[:, 0, :, :])
            after(nc.vector.scalar_tensor_tensor(others[:], onehot[:, 0, :, :], MASKED, scores[:], ALU.mult, ALU.add))
            first_max(g, after, others[:], best[:, 1, :], work[:], onehot[:, 1, :, :])
            after(nc.vector.tensor_tensor(denom[:], best[:, 0, :], best[:, 1, :], ALU.add))
            after(nc.vector.tensor_scalar(denom[:], denom[:], 1e-20, None, ALU.add))
            after(nc.vector.reciprocal(denom[:], denom[:]))
            after(nc.vector.tensor_tensor(work[:], onehot[:, 0, :, :], onehot[:, 1, :, :], ALU.add))
            after(nc.vector.scalar_tensor_tensor(work[:], scores[:], 2.5, work[:], ALU.mult, ALU.mult))
            after(nc.vector.tensor_tensor(combine[:], work[:], denom[:, :, None].to_broadcast([P, TILES, E]), ALU.mult))
            part = lambda k: combine_parts[:, :, k * E:(k + 1) * E]
            v.wait_ge(weights_ready, 1)
            after(nc.vector.tensor_copy(part(0), combine[:]))
            after(nc.vector.tensor_tensor(combine[:], combine[:], part(0), ALU.subtract))
            after(nc.vector.tensor_copy(part(1), combine[:]))
            nc.vector.tensor_tensor(part(2), combine[:], part(1), ALU.subtract).then_inc(weights_ready, 1)

            def add(b):
                v.wait_ge(y_psum, b + 1)
                rows = g.x[:, GROUP * b:GROUP * (b + 1), :].rearrange("p t d -> p (t d)")
                nc.vector.scalar_tensor_tensor(rows, y_bank[:], 0.5, rows, ALU.mult, ALU.add).then_inc(summed, 1)
                v.wait_ge(summed, b + 1)

            m = 0
            for k, (b, c) in enumerate(units):
                v.wait_ge(silu_done, k + 1)
                v.wait_ge(u_psum, k + 1)
                dst = hid[:, b % 2, c, :]
                if c == 0 and b >= 2:
                    v.wait_ge(y_psum, b - 1)
                if c < routed:
                    if k >= 2:
                        v.wait_ge(hidden, k - 1)
                    nc.vector.tensor_tensor(prod[:, k % 2, :], silu[:, k % 2, :], u_bank[k % 2][:],
                                            ALU.mult).then_inc(gated, 1)
                    m += 1
                    v.wait_ge(gated, k + 1)
                    v.wait_ge(cb_psum, m)
                    nc.vector.tensor_tensor(dst, prod[:, k % 2, :], cb_bank[:], ALU.mult).then_inc(hidden, 1)
                else:
                    nc.vector.tensor_tensor(dst, silu[:, k % 2, :], u_bank[k % 2][:], ALU.mult).then_inc(hidden, 1)
                    nc.vector.memset(g.spare[:], 0.0).then_inc(gated, 1)
                if c == 2 and b >= 1:
                    add(b - 1)
                if c == 3 and b >= 1:
                    ln_stats(g, v, ln, b - 1)
                if c == 4 and b >= 1:
                    ln_rows(g, v, ln, b - 1)
            add(B - 1)
            ln_stats(g, v, ln, B - 1)
            ln_rows(g, v, ln, B - 1)

        @block.gpsimd
        def _(pool):
            for b in range(B):
                ln_rstd(g, pool, ln, b)


class ExpertProducts:
    def __init__(self, g, ctx, name, products):
        sem = semaphores(g, name)
        self.g, self.products = g, products
        self.loaded = [sem(f"loaded{i}") for i in range(2)]
        self.product, self.copied = sem("product"), sem("copied")
        self.w_in = ctx.enter_context(g.nc.sbuf_tensor(f"{name}_in", [P, 2, 4 * CH, D], F32))
        self.w_out = ctx.enter_context(g.nc.sbuf_tensor(f"{name}_out", [P, 2, 4 * CH, D], F32))

    def load(self, act):
        a = self.g.a
        for i in range(2):
            rows = slice(i * 4 * HID, (i + 1) * 4 * HID)
            for dst, src in ((self.w_in, a["l2_w_in"]), (self.w_out, a["l2_w_out"])):
                act.dma_start(dst[:, i, :, :], src[rows, :].rearrange("(c p) d -> p c d", p=P)).then_inc(self.loaded[i], 16)

    def multiply(self, pe, banks):
        for i in range(2):
            pe.wait_ge(self.loaded[i], 32)
            for e in range(4):
                for c in range(CH):
                    mm = self.g.nc.tensor.matmul(banks[i][:, e * D:(e + 1) * D], self.w_in[:, i, e * CH + c, :],
                                                 self.w_out[:, i, e * CH + c, :], start=(c == 0), stop=(c == CH - 1))
            mm.then_inc(self.product, 1)

    def copy(self, act, banks):
        for i in range(2):
            act.wait_ge(self.product, i + 1)
            self.g.nc.scalar.copy(self.products[:, i, :], banks[i][:]).then_inc(self.copied, 1)


def ffn2(g, name, products, gate=None, prefetch=None):
    nc, a = g.nc, g.a
    with ExitStack() as ctx:
        sem = semaphores(g, name)
        sb = lambda n, shape, dt=F32: ctx.enter_context(nc.sbuf_tensor(f"{name}_{n}", shape, dt))
        ln = LayerNormSems(sem, gate=gate)
        route, partial = sem("route"), sem("partial_sums")
        exp_in, exp_out, y_psum, weighted = sem("exp_in"), sem("exp_out"), sem("y_psum"), sem("weights")
        scaled, halved, summed, added = sem("scaled"), sem("halved"), sem("scaled_summed"), sem("added")
        xnt, logits = g.xnt, g.logits
        others, work = sb("others", [P, TILES, E]), sb("work", [P, TILES, E])
        best = sb("best", [P, 2, TILES])
        onehot = sb("onehot", [P, 2, TILES, E])
        delta, denom = sb("delta", [P, TILES]), sb("denom", [P, TILES])
        gates = sb("gates", [P, 2, TILES])
        weight = sb("weight", [P, TILES, E])
        by_act = ((0, 1), (1, 1), (2, 1))
        order = ((0, 0), (1, 0), (0, 1), (2, 0), (3, 0), (1, 1), (3, 1), (2, 1))
        by_dve = (((0, 0), (1, 0)), ((2, 0), (3, 0)), ((3, 1),))
        units = [(b, u) for b in range(B) for u in order]
        shares = sb("scaled_outputs", [P, 2, len(by_act), GROUP, D])
        read, count = {}, {"dve": 0, "act": 0}
        for b in range(B):
            for turn in by_dve:
                for e in range(GROUP):
                    for u in turn:
                        count["dve"] += 1
                        read[b, u] = partial, count["dve"]
            for u in by_act:
                count["act"] += GROUP
                read[b, u] = scaled, count["act"]
        y_bank, xnt_bank = g.bank[0:7], g.bank[7]
        Y = len(y_bank)
        block = ctx.enter_context(nc.Block(no_gpsimd_drain=True))

        @block.sync
        def _(sp):
            if prefetch:
                prefetch.load(sp)

        @block.tensor
        def _(pe):
            for k, (b, u) in enumerate(units):
                i, half = GROUP * b + u[0], u[1]
                if k >= Y:
                    pe.wait_ge(*read[units[k - Y]])
                nc.tensor.matmul(y_bank[k % Y][:], xnt[:, i * P:(i + 1) * P], products[:, half, :],
                                 start=True, stop=True).then_inc(y_psum, 1)
                at = k % len(order)
                if at == 5 and b >= 2:
                    ln_transpose(g, pe, ln, b - 2, xnt_bank, one_bank=True)
                if at == 7 and b >= 2:
                    ln_logits(g, pe, ln, b - 2, xnt_bank)
            for b in range(B - 2, B):
                ln_transpose(g, pe, ln, b, xnt_bank, one_bank=True)
                ln_logits(g, pe, ln, b, xnt_bank)

        @block.scalar
        def _(act):
            act.wait_ge(exp_in, 1)
            nc.scalar.activation(delta[:], delta[:], ACT.Exp).then_inc(exp_out, 1)

            def next_columns(b):
                ln_columns(g, act, ln, b, xnt_bank)
                ln_copy_logits(g, act, ln, b, xnt_bank)

            act.wait_ge(weighted, 1)
            for b in range(B):
                if b >= 2:
                    act.wait_ge(added, b - 1)
                for n, u in enumerate(by_act):
                    act.wait_ge(y_psum, len(order) * b + order.index(u) + 1)
                    bank = y_bank[(len(order) * b + order.index(u)) % Y]
                    for e in range(GROUP):
                        nc.scalar.activation(shares[:, b % 2, n, e, :], bank[:, e * D:(e + 1) * D], ACT.Identity,
                                             scale=weight[:, GROUP * b + u[0], u[1] * GROUP + e:u[1] * GROUP + e + 1]
                                             ).then_inc(scaled, 1)
                if b >= 2:
                    next_columns(b - 2)
            for b in range(B - 2, B):
                next_columns(b)

        @block.vector
        def _(v):
            n = [0]

            def after(ins):
                n[0] += 1
                ins.then_inc(route, 1)
                v.wait_ge(route, n[0])

            first_max(g, after, logits[:], best[:, 0, :], work[:], onehot[:, 0, :, :])
            after(nc.vector.scalar_tensor_tensor(others[:], onehot[:, 0, :, :], MASKED, logits[:], ALU.mult, ALU.add))
            first_max(g, after, others[:], best[:, 1, :], work[:], onehot[:, 1, :, :])
            nc.vector.tensor_tensor(delta[:], best[:, 1, :], best[:, 0, :], ALU.subtract).then_inc(exp_in, 1)
            v.wait_ge(exp_out, 1)
            after(nc.vector.tensor_scalar(denom[:], delta[:], 1.0, None, ALU.add))
            after(nc.vector.reciprocal(gates[:, 0, :], denom[:]))
            after(nc.vector.tensor_tensor(gates[:, 1, :], delta[:], gates[:, 0, :], ALU.mult))
            spread = lambda c: gates[:, c, :, None].to_broadcast([P, TILES, E])
            after(nc.vector.scalar_tensor_tensor(work[:], onehot[:, 0, :, :], 0.5, spread(0), ALU.mult, ALU.mult))
            after(nc.vector.scalar_tensor_tensor(others[:], onehot[:, 1, :, :], 0.5, spread(1), ALU.mult, ALU.mult))
            nc.vector.tensor_tensor(weight[:], work[:], others[:], ALU.add).then_inc(weighted, 1)
            v.wait_ge(weighted, 1)
            sums, last = 0, {}

            def add_unit(turn, e, b):
                nonlocal sums
                for u in turn:
                    i, half = GROUP * b + u[0], u[1]
                    k = len(order) * b + order.index(u)
                    if e == 0:
                        v.wait_ge(y_psum, k + 1)
                    if i in last:
                        v.wait_ge(partial, last[i])
                    nc.vector.scalar_tensor_tensor(g.x[:, i, :], y_bank[k % Y][:, e * D:(e + 1) * D],
                                                   weight[:, i, half * GROUP + e:half * GROUP + e + 1], g.x[:, i, :],
                                                   ALU.mult, ALU.add).then_inc(partial, 1)
                    sums += 1
                    last[i] = sums

            def add_shares(b):
                v.wait_ge(summed, b + 1)
                v.wait_ge(partial, (b + 1) * (sum(len(turn) for turn in by_dve) * GROUP))
                tiles = slice(GROUP * b, GROUP * b + len(by_act))
                nc.vector.tensor_tensor(g.x[:, tiles, :], g.x[:, tiles, :], shares[:, b % 2, :, 0, :], ALU.add).then_inc(added, 1)
                v.wait_ge(added, b + 1)
                ln_stats(g, v, ln, b)

            for b in range(B):
                for n, turn in enumerate(by_dve):
                    for e in range(GROUP):
                        add_unit(turn, e, b)
                    if n == 0 and b >= 1:
                        add_shares(b - 1)
                    if n == 1 and b >= 1:
                        ln_rows(g, v, ln, b - 1)
            add_shares(B - 1)
            ln_rows(g, v, ln, B - 1)

        @block.gpsimd
        def _(pool):
            for b in range(B):
                pool.wait_ge(scaled, len(by_act) * GROUP * (b + 1))
                share = lambda lo, hi: shares[:, b % 2, :, lo:hi, :]
                nc.gpsimd.tensor_tensor(share(0, 2), share(0, 2), share(2, 4), ALU.add).then_inc(halved, 1)
                pool.wait_ge(halved, b + 1)
                nc.gpsimd.tensor_tensor(share(0, 1), share(0, 1), share(1, 2), ALU.add).then_inc(summed, 1)
                ln_rstd(g, pool, ln, b)


class RecurrenceWeights:
    def __init__(self, g, ctx):
        sb = lambda n, shape: ctx.enter_context(g.nc.sbuf_tensor(f"rec2_{n}", shape, F32))
        self.g, self.loaded = g, semaphores(g, "rec2")("weights_loaded")
        self.win, self.wout = sb("win", [P, 2 * D]), sb("wout", [P, D])
        self.bin, self.bout = sb("bin", [P, 2]), sb("bout", [P, D])

    def load(self, sp):
        a = self.g.a
        for dst, src in ((self.win, a["l2_win"]), (self.wout, a["l2_wout"]), (self.bin, a["l2_bin"]),
                         (self.bout, a["l2_bout"].partition_broadcast(P))):
            sp.dma_start(dst[:], src).then_inc(self.loaded, 16)


def recurrence2(g, name, weights, gate):
    nc, a = g.nc, g.a
    with ExitStack() as ctx:
        sem = semaphores(g, name)
        sb = lambda n, shape, dt=F32: ctx.enter_context(nc.sbuf_tensor(f"{name}_{n}", shape, dt))
        ln = LayerNormSems(sem, gate=gate)
        proj, sig, step = sem("projected"), sem("sigmoids"), sem("step")
        loaded, win, wout, bin_sb, bout = weights.loaded, weights.win, weights.wout, weights.bin, weights.bout
        used, scanned, y_psum, added = sem("banks_used"), sem("scanned"), sem("y_psum"), sem("added")
        xnt = g.xnt
        sg, sh = sb("sig_gate", [P, 2, T]), sb("sig_hidden", [P, 2, T])
        silu, drive, states = sb("silu", [P, 2, T]), sb("drive", [P, 2, T]), sb("states", [P, 2, T])
        out = sb("out", [P, T])
        decay = sb("decay", [P, T])
        xnt_bank, gate_bank, hid_bank, y_bank = g.bank[0:2], g.bank[2:4], g.bank[4:6], g.bank[6:8]
        block = ctx.enter_context(nc.Block(no_gpsimd_drain=True))

        @block.tensor
        def _(pe):
            def project_out(b):
                pe.wait_ge(scanned, b + 1)
                if b >= 2:
                    pe.wait_ge(added, b - 1)
                for i in range(GROUP):
                    mm = nc.tensor.matmul(y_bank[b % 2][:, i * D:(i + 1) * D], states[:, b % 2, i * P:(i + 1) * P],
                                          wout[:], start=True, stop=True)
                mm.then_inc(y_psum, 1)

            for b in range(B):
                if b == 0:
                    pe.wait_ge(loaded, 64)
                if b >= 2:
                    pe.wait_ge(used, b - 1)
                columns = xnt[:, b * T:(b + 1) * T]
                nc.tensor.matmul(gate_bank[b % 2][:], win[:, 0:D], columns, start=True, stop=True)
                nc.tensor.matmul(hid_bank[b % 2][:], win[:, D:2 * D], columns, start=True, stop=True).then_inc(proj, 1)
                if b >= 1:
                    project_out(b - 1)
                if b >= 2:
                    ln_transpose(g, pe, ln, b - 2, xnt_bank[b % 2])
                if b >= 3:
                    ln_logits(g, pe, ln, b - 3, xnt_bank[(b + 1) % 2])
            project_out(B - 1)
            for b in (B - 2, B - 1):
                ln_logits(g, pe, ln, b - 1, xnt_bank[(b + 1) % 2])
                pe.wait_ge(ln.logits, b - 1)
                ln_transpose(g, pe, ln, b, xnt_bank[b % 2])
            ln_logits(g, pe, ln, B - 1, xnt_bank[(B - 1) % 2])

        @block.scalar
        def _(act):
            for b in range(B):
                act.wait_ge(proj, b + 1)
                act.wait_ge(loaded, 64)
                if b >= 2:
                    act.wait_ge(scanned, b - 1)
                nc.scalar.activation(sg[:, b % 2, :], gate_bank[b % 2][:], ACT.Sigmoid, bias=bin_sb[:, 0:1])
                nc.scalar.activation(sh[:, b % 2, :], hid_bank[b % 2][:], ACT.Sigmoid, bias=bin_sb[:, 1:2]).then_inc(sig, 1)
                if b >= 2:
                    ln_columns(g, act, ln, b - 2, xnt_bank[b % 2])
                if b >= 3:
                    ln_copy_logits(g, act, ln, b - 3, xnt_bank[(b + 1) % 2])
            for b in (B - 2, B - 1):
                ln_copy_logits(g, act, ln, b - 1, xnt_bank[(b + 1) % 2])
                ln_columns(g, act, ln, b, xnt_bank[b % 2])
            ln_copy_logits(g, act, ln, B - 1, xnt_bank[(B - 1) % 2])

        @block.vector
        def _(v):
            n = [0]

            def after(ins):
                n[0] += 1
                ins.then_inc(step, 1)
                v.wait_ge(step, n[0])

            def add(b):
                v.wait_ge(y_psum, b + 1)
                rows = g.x[:, GROUP * b:GROUP * (b + 1), :]
                after(nc.vector.tensor_tensor(out[:].rearrange("p (t d) -> p t d", d=D),
                                              y_bank[b % 2][:].rearrange("p (t d) -> p t d", d=D),
                                              bout[:, None, :].to_broadcast([P, GROUP, D]), ALU.add))
                nc.vector.tensor_tensor(rows, rows, out[:].rearrange("p (t d) -> p t d", d=D), ALU.add).then_inc(added, 1)
                v.wait_ge(added, b + 1)
                ln_stats(g, v, ln, b)

            after(nc.vector.memset(decay[:], 0.9))
            for b in range(B):
                v.wait_ge(sig, b + 1)
                after(nc.vector.scalar_tensor_tensor(silu[:, b % 2, :], hid_bank[b % 2][:], bin_sb[:, 1:2],
                                                     sh[:, b % 2, :], ALU.add, ALU.mult))
                nc.vector.scalar_tensor_tensor(drive[:, b % 2, :], silu[:, b % 2, :], 0.1, sg[:, b % 2, :],
                                               ALU.mult, ALU.mult).then_inc(used, 1)
                v.wait_ge(used, b + 1)
                if b >= 2:
                    v.wait_ge(y_psum, b - 1)
                nc.vector.tensor_tensor_scan(states[:, b % 2, :], decay[:], drive[:, b % 2, :], 0.0,
                                             ALU.mult, ALU.add).then_inc(scanned, 1)
                if b >= 2:
                    ln_rows(g, v, ln, b - 2)
                if b >= 1:
                    add(b - 1)
            ln_rows(g, v, ln, B - 2)
            add(B - 1)
            ln_rows(g, v, ln, B - 1)

        @block.gpsimd
        def _(pool):
            for b in range(B):
                ln_rstd(g, pool, ln, b)


GROUPS = 4
GH = HEADS // GROUPS
NG = B * GROUPS
RING = 4
VW = 32
PARTS, TERMS = 3, 6
MAX_ROWS = PARTS * GH
MAX_AT, K_ROWS = 64, 96
MAX_AT1 = 96
R1, R2 = 4, 8
KR = R1 * R2


def slots():
    return [(n, n // GROUPS, n % GROUPS) for n in range(-2 * GROUPS + 1, NG + GROUPS)]


class RelativeBias:
    L = 3 * P

    def __init__(self, g, ctx, name, kq, qk):
        sem = semaphores(g, name)
        sb = lambda n, shape, dt=F32: ctx.enter_context(g.nc.sbuf_tensor(f"{name}_{n}", shape, dt))
        self.g, self.kq, self.qk = g, kq, qk
        self.loaded, self.summed, self.less_last, self.turned, self.lined = (sem(n) for n in (
            "loaded", "summed", "less_last", "turned", "lined"))
        self.stored, self.tiled, self.flipped = sem("lines_stored"), sem("tiled"), [sem("flipped_kq"), sem("flipped_qk")]
        self.high, self.cast, self.low = sem("high"), sem("cast"), sem("low")
        self.split_done, self.copied = sem("split"), sem("copied")
        self.tables = sb("tables", [P, 3, P])
        self.sums = sb("sums", [P, 3, HEADS])
        self.line = sb("line", [HEADS, 2, self.L])
        self.tiles = sb("tiles", [P, 2, HEADS, 2 * P])
        self.rest = sb("rest", [P, 2, 2, 2 * P])

    def load(self, sp):
        a = self.g.a
        for k, src in enumerate((a["l0_rel"], a["l0_rel_back"], a["l0_rel"][P - 1, :].partition_broadcast(P))):
            sp.dma_start(self.tables[:, k, :], src).then_inc(self.loaded, 16)

    def sum_heads(self, v):
        nc, line = self.g.nc, self.line
        nc.vector.memset(line[:, 0, 0:P], MASKED)
        nc.vector.memset(line[:, 0, 2 * P:self.L], 0.0)
        nc.vector.memset(line[:, 1, 0:P], 0.0)
        nc.vector.memset(line[:, 1, 2 * P:self.L], MASKED)
        v.wait_ge(self.loaded, 48)
        nc.vector.tensor_reduce(self.sums[:].rearrange("p k h -> p (k h)"),
                                self.tables[:].rearrange("p k (h d) -> p (k h) d", d=HD), axis=AX, op=ALU.add
                                ).then_inc(self.summed, 1)
        v.wait_ge(self.summed, 1)
        nc.vector.tensor_tensor(self.sums[:, 0:2, :], self.sums[:, 0:2, :],
                                self.sums[:, 2:3, :].to_broadcast([P, 2, HEADS]), ALU.subtract).then_inc(self.less_last, 1)

    def turn(self, pe, bank):
        pe.wait_ge(self.less_last, 1)
        for way in range(2):
            mm = self.g.nc.tensor.transpose(bank[0:HEADS, way * P:(way + 1) * P], self.sums[:, way, :], self.g.ident[:])
        mm.then_inc(self.turned, 1)

    def copy_lines(self, act, bank):
        act.wait_ge(self.turned, 1)
        for way in range(2):
            self.g.nc.scalar.copy(self.line[:, way, P:2 * P], bank[0:HEADS, way * P:(way + 1) * P]).then_inc(self.lined, 1)

    def store_lines(self, act):
        act.wait_ge(self.lined, 2)
        act.dma_start(self.g.bias_lines.rearrange("h (w l) -> h w l", l=self.L), self.line[:]).then_inc(self.stored, 16)

    def load_tiles(self, act):
        act.wait_ge(self.stored, 16)
        for way in range(2):
            windows = bass.AP(self.g.bias_lines.tensor, way * self.L + 1 - way, [[1, P], [2 * self.L, HEADS], [1, 2 * P]])
            act.dma_start(self.tiles[:, way, :, :], windows).then_inc(self.tiled, 16)

    def flip(self, pe, banks):
        pe.wait_ge(self.tiled, 32)
        for k in range(HEADS // 2):
            for way in range(2):
                if k >= 2:
                    pe.wait_ge(self.copied if way else self.split_done, k - 1)
                self.g.nc.tensor.matmul(banks[way][k % 2][:], self.g.flip[:],
                                        self.tiles[:, way, 2 * k:2 * k + 2, :].rearrange("p h c -> p (h c)"),
                                        start=True, stop=True).then_inc(self.flipped[way], 1)

    def split(self, v, banks):
        nc = self.g.nc
        for k in range(HEADS // 2):
            part = lambda n: self.kq[:, 2 * k:2 * k + 2, n, :]
            tile, rest = banks[0][k % 2][:].rearrange("p (h c) -> p h c", h=2), self.rest[:, k % 2, :, :]
            v.wait_ge(self.high, k + 1)
            if k >= 2:
                v.wait_ge(self.low, k - 1)
            nc.vector.tensor_tensor(rest, tile, part(0), ALU.subtract).then_inc(self.split_done, 1)
            if k >= 1:
                self.split_low(v, k - 1)
        self.split_low(v, HEADS // 2 - 1)

    def split_low(self, v, k):
        part = lambda n: self.kq[:, 2 * k:2 * k + 2, n, :]
        v.wait_ge(self.cast, k + 1)
        self.g.nc.vector.tensor_tensor(part(2), self.rest[:, k % 2, :, :], part(1), ALU.subtract).then_inc(self.low, 1)

    def copy(self, act, banks):
        nc = self.g.nc
        for k in range(HEADS // 2):
            act.wait_ge(self.flipped[0], k + 1)
            nc.scalar.copy(self.kq[:, 2 * k:2 * k + 2, 0, :], banks[0][k % 2][:].rearrange("p (h c) -> p h c", h=2)
                           ).then_inc(self.high, 1)
            act.wait_ge(self.flipped[1], k + 1)
            nc.scalar.copy(self.qk[:, 2 * k:2 * k + 2, :].rearrange("p h c -> p (h c)"), banks[1][k % 2][:]
                           ).then_inc(self.copied, 1)
            act.wait_ge(self.split_done, k + 1)
            nc.scalar.copy(self.kq[:, 2 * k:2 * k + 2, 1, :], self.rest[:, k % 2, :, :]).then_inc(self.cast, 1)


class AttentionWeights:
    def __init__(self, g, ctx, kind):
        sb = lambda n, shape: ctx.enter_context(g.nc.sbuf_tensor(f"att{kind}_{n}", shape, F32))
        self.g, self.layer, self.projected_apart = g, f"l{kind}", kind != 1
        self.loaded = semaphores(g, f"att{kind}")("weights_loaded")
        self.wo, self.bo = sb("wo", [P, D]), sb("bo", [P, D])
        if self.projected_apart:
            self.wq, self.wk, self.wv = sb("wq", [P, P]), sb("wk", [P, P]), sb("wv", [P, P])
            self.bq, self.bk, self.bv = sb("bq", [P, 1]), sb("bk", [P, 1]), sb("bv", [P, D])
            self.loads = 16 * 8
        else:
            self.wqk = sb("wqk", [P, T])
            self.loads = 16 * 3

    def load(self, sp):
        part = lambda n: self.g.a[f"{self.layer}_{n}"]
        if self.projected_apart:
            pairs = [(self.wq, part("wq")), (self.wk, part("wk")), (self.wv, part("wv")), (self.bq, part("bq")),
                     (self.bk, part("bk")), (self.bv, part("bv").partition_broadcast(P))]
        else:
            pairs = [(self.wqk, part("wqk"))]
        for dst, src in pairs + [(self.wo, part("wo")), (self.bo, part("bo").partition_broadcast(P))]:
            sp.dma_start(dst[:], src).then_inc(self.loaded, 16)


def attention(g, name, kind, weights, gate, bias=None, routing=None):
    nc, a = g.nc, g.a
    causal = kind != 3
    split = kind != 1
    scale = HD ** -0.5 if split else KR ** -0.5
    first_query = [P * s if causal else 0 for s in range(GROUP)]
    width = [T - f for f in first_query]
    units = [[0], [1, 3], [2]] if causal else [[0], [1], [2], [3]]
    offset, unit_at, at = {}, [], 0
    for u in units:
        unit_at.append(at)
        for s in u:
            offset[s], at = at, at + width[s]
    prob_width, U = at, len(units)
    keys_seen = [P * (i + 1) if causal else T for i in range(GROUP)]
    group_units, group_tiles = GH * U, GH * GROUP

    with ExitStack() as ctx:
        sem = semaphores(g, name)
        sb = lambda n, shape, dt=F32: ctx.enter_context(nc.sbuf_tensor(f"{name}_{n}", shape, dt))
        if kind == 0:
            bias_kq, bias_qk = bias
        ln = LayerNormSems(sem, gate=gate)
        loaded, wo, bo = weights.loaded, weights.wo, weights.bo
        prepared, zeroed, spare_rows, values_zeroed = (sem(n) for n in (
            "selectors_placed", "zeros_made", "zeros_placed", "values_zeroed"))
        proj, taken, hi_ready, rem_ready, mid_ready, parts_ready = (sem(n) for n in (
            "projected", "projections_taken", "high_parts", "remainders", "middle_parts", "parts"))
        v_psum, v_ready = sem("values_psum"), sem("values")
        written = sem("terms_written")
        op_loaded = [sem(f"operands{i}") for i in range(RING)]
        rows_psum, rows_taken = sem("rows_pass"), sem("rows_taken")
        max_step, max_split, max_psum, max_cols, max_loaded = (sem(n) for n in (
            "max_step", "max_split", "max_psum", "max_columns", "max_loaded"))
        cols_psum, probs_ready = sem("columns_pass"), sem("probs")
        o_psum, o_copied, t_psum, t_norm = sem("context_psum"), sem("context"), sem("context_turned"), sem("context_rows")
        norm_step = sem("norm_step")
        c_psum, c_ready, y_psum = sem("rows_turned"), sem("context_columns"), sem("out_psum")
        biased, added = sem("bias_added"), sem("added")

        columns_of = lambda b: g.xnt[:, b * T:(b + 1) * T]
        values = sb("values", [P, 2, GROUP, HEADS, VW])
        probs = sb("probs", [P, 2, GH, prob_width])
        maxima = sb("maxima", [P, 2, GROUP, GH])
        far = sb("far", [P, 2, GROUP, GH])
        max_rest = sb("max_rest", [P, GROUP, GH])
        max_parts = sb("max_parts", [P, GROUP, PARTS, GH], BF16)
        max_t = sb("max_t", [MAX_ROWS, T], BF16)
        context_t = sb("context_t", [P, T])
        recip = sb("recip", [P, GROUP, GH])
        context = sb("context", [P, GROUP, D])
        columns = sb("columns", [P, T])
        if split:
            wq, wk, wv, bq, bk, bv = weights.wq, weights.wk, weights.wv, weights.bq, weights.bk, weights.bv
            rest = sb("qk", [P, 2, T])
            parts = sb("parts", [P, 2, PARTS, T], BF16)
            q_op, k_op = sb("queries", [P, RING, GH, T], BF16), sb("keys", [P, RING, GH, T], BF16)
            zeros = sb("zeros", [P, T], BF16)
            op_loads = 3
        else:
            wqk = weights.wqk
            pj = sb("pj", [P, 2, GROUP, T])
            outer = sb("outer", [P, 2, 2, GROUP, P])
            rest = sb("rest", [P, 2, T])
            parts = sb("parts", [P, 2, 2, PARTS, T], BF16)
            q_op, k_op = sb("queries", [P, RING, 2, GH, T], BF16), sb("keys", [P, RING, 2, GH, T], BF16)
            op_loads = 6
            outer_ready, outer_psum = sem("outer_products"), sem("outer_products_turned")
        RB = 3
        rows_bank, cols_bank = g.bank[0:RB], g.bank[RB:5]
        CB = len(cols_bank)
        o_bank, prep_bank, misc_bank = g.bank[5], g.bank[6], g.bank[7]
        tiles_at = {}
        if not split:
            for t, (q, j) in enumerate(((1, 0), (1, 2), (1, 3), (2, 0))):
                tiles_at[-2, q, j] = 0, t, t % 2 == 1
            for r in range(1, B):
                for t, (b, q) in enumerate(((r - 3, 2), (r - 3, 3), (r - 2, 0), (r - 2, 1))):
                    tiles_at[b, q, GH - 1] = r, t, q in (3, 0)
        block = ctx.enter_context(nc.Block(no_gpsimd_drain=True))

        def make_outer(engine, ops, G):
            b, c = G // GROUPS, G % GROUPS
            engine.wait_ge(taken, GROUP * (b + 1))
            if G >= 2:
                engine.wait_ge(outer_psum, 2 * (G - 1))
            for side in range(2):
                for t in range(GROUP):
                    at1 = side * HEADS * R1 + c * GH * R1
                    at2 = 2 * HEADS * R1 + side * HEADS * R2 + c * GH * R2
                    one = pj[:, b % 2, t, at1:at1 + GH * R1].rearrange("p (j r) -> p r j", r=R1)
                    two = pj[:, b % 2, t, at2:at2 + GH * R2].rearrange("p (j s) -> p s j", s=R2)
                    wide = [P, R1, R2, GH]
                    ins = ops.tensor_tensor(outer[:, G % 2, side, t, :].rearrange("p (r s j) -> p r s j", r=R1, s=R2),
                                                  one[:, :, None, :].to_broadcast(wide),
                                                  two[:, None, :, :].to_broadcast(wide), ALU.mult)
                ins.then_inc(outer_ready, 1)

        @block.sync
        def _(sp):
            if split:
                sp.wait_ge(zeroed, 1)
                pad = slice(TERMS * HD, K_ROWS)
                sp.dma_start(q_op[pad, :, :, :].rearrange("p i j t -> p (i j) t"),
                             zeros[pad, None, :].to_broadcast([K_ROWS - TERMS * HD, RING * GH, T])).then_inc(spare_rows, 16)
                pad = slice(TERMS * HD, MAX_AT)
                sp.dma_start(k_op[pad, :, :, :].rearrange("p i j t -> p (i j) t"),
                             zeros[pad, None, :].to_broadcast([MAX_AT - TERMS * HD, RING * GH, T])).then_inc(spare_rows, 16)

            def write_terms(b):
                if b >= 2:
                    for i in range(RING):
                        sp.wait_ge(op_loaded[i], 16 * op_loads * (b - 1))
                for side in range(2):
                    sp.wait_ge(parts_ready, 2 * b + side + 1)
                    dst = g.terms[b % 2][side]
                    if side == 0:
                        for at, part, times in ((0, 0, 3), (3, 1, 2), (5, 2, 1)):
                            sp.dma_start(dst[at:at + times].rearrange("j r t -> r j t"),
                                         parts[:, 0, part:part + 1, :].to_broadcast([P, times, T])).then_inc(written, 16)
                    else:
                        for at, times in ((0, 3), (3, 2), (5, 1)):
                            sp.dma_start(dst[at:at + times].rearrange("j r t -> r j t"),
                                         parts[:, 1, 0:times, :]).then_inc(written, 16)

            def write_parts(G):
                if G >= 2:
                    sp.wait_ge(op_loaded[(G - 2) % RING], 16 * op_loads * ((G - 2) // RING + 1))
                for side in range(2):
                    sp.wait_ge(parts_ready, 2 * G + side + 1)
                    sp.dma_start(g.terms[G % 2][side][0:PARTS].rearrange("k r t -> r k t"),
                                 parts[:, G % 2, side, :, :]).then_inc(written, 16)

            def load_operands(G):
                i, b, q = G % RING, G // GROUPS, G % GROUPS
                if G >= RING:
                    sp.wait_ge(cols_psum, group_units * (G - RING + 1))
                if split:
                    if G == 0:
                        sp.wait_ge(spare_rows, 32)
                    sp.wait_ge(written, 16 * 6 * (b + 1))
                    for side, op in enumerate((q_op, k_op)):
                        sp.dma_start(op[0:TERMS * HD, i, :, :],
                                     g.terms[b % 2][side].rearrange("j (d h) t -> (j d) h t", h=HEADS)[:, GH * q:GH * (q + 1), :]
                                     ).then_inc(op_loaded[i], 16)
                    sp.dma_start(q_op[MAX_AT:MAX_AT + MAX_ROWS, i, :, :], zeros[MAX_AT:MAX_AT + MAX_ROWS, None, :]
                                 .to_broadcast([MAX_ROWS, GH, T])).then_inc(op_loaded[i], 16)
                else:
                    sp.wait_ge(written, 32 * (G + 1))
                    stored = [g.terms[G % 2][side].rearrange("k (r j) t -> (k r) j t", j=GH) for side in range(2)]
                    part = lambda side, k: stored[side][KR * k:KR * (k + 1)]
                    sp.dma_start(q_op[0:KR, i, 0, :, :], part(0, 0)).then_inc(op_loaded[i], 16)
                    sp.dma_start(q_op[KR:3 * KR, i, 0, :, :], stored[0][0:2 * KR]).then_inc(op_loaded[i], 16)
                    sp.dma_start(q_op[0:3 * KR, i, 1, :, :], stored[0][0:3 * KR]).then_inc(op_loaded[i], 16)
                    sp.dma_start(k_op[0:KR, i, 0, :, :], part(1, 2)).then_inc(op_loaded[i], 16)
                    sp.dma_start(k_op[KR:3 * KR, i, 0, :, :], stored[1][KR:3 * KR]).then_inc(op_loaded[i], 16)
                    sp.dma_start(k_op[0:3 * KR, i, 1, :, :], stored[1][0:3 * KR]).then_inc(op_loaded[i], 16)

            def load_maxima(G):
                sp.wait_ge(max_cols, G + 1)
                dst = q_op[MAX_AT:MAX_AT + MAX_ROWS, G % RING, :, :] if split else \
                    q_op[MAX_AT1:MAX_AT1 + MAX_ROWS, G % RING, 1, :, :]
                sp.dma_start(dst, max_t[:, None, :].to_broadcast([MAX_ROWS, GH, T])).then_inc(max_loaded, 16)

            for n, b, q in slots():
                if 0 <= n + 3 < NG:
                    load_operands(n + 3)
                if 0 <= n + 1 < NG:
                    load_maxima(n + 1)
                if not split and 0 <= n + 4 < NG:
                    write_parts(n + 4)
                if split and q == 0 and 0 <= b + 1 < B:
                    write_terms(b + 1)
                if kind == 0 and n == NG - 3:
                    write_untaken(g, sp, (2, 3))
            sp.wait_ge(max_loaded, 16 * NG)

        @block.tensor
        def _(pe):
            misc_last, prep_last = [], []

            def bank_free(last, *reader):
                for s, value in last:
                    pe.wait_ge(s, value)
                last[:] = [reader]

            def columns_unit(G, j, u):
                i, k = G % RING, G * group_units + j * U + u
                h = GH * (G % GROUPS) + j
                if k >= CB:
                    pe.wait_ge(probs_ready, k - CB + 1)
                bank = cols_bank[k % CB]
                c0 = 0
                for s in units[u]:
                    dst = bank[:, c0:c0 + width[s]]
                    q0 = first_query[s]
                    key = slice(s * P, (s + 1) * P)
                    if split:
                        mm = nc.tensor.matmul(dst, k_op[0:K_ROWS, i, j, key], q_op[0:K_ROWS, i, j, q0:T],
                                              start=True, stop=kind == 3)
                    else:
                        nc.tensor.matmul(dst, k_op[0:3 * KR, i, 0, j, key], q_op[0:3 * KR, i, 0, j, q0:T],
                                         start=True, stop=False)
                        nc.tensor.matmul(dst, k_op[0:MAX_AT1 + MAX_ROWS, i, 1, j, key],
                                         q_op[0:MAX_AT1 + MAX_ROWS, i, 1, j, q0:T], start=False, stop=False)
                        mm = nc.tensor.matmul(bank[:, c0:c0 + P], g.identb[:], g.mask_kq[:], start=False, stop=True)
                    if kind == 0:
                        w = min(2 * P, width[s])
                        for p in range(3):
                            mm = nc.tensor.matmul(bank[:, c0:c0 + w], g.identb[:], bias_kq[:, h, p, 0:w],
                                                  start=False, stop=p == 2)
                    c0 += width[s]
                mm.then_inc(cols_psum, 1)

            def rows_tile(G, j, t):
                i, k = G % RING, G * group_tiles + j * GROUP + t
                if k >= RB:
                    pe.wait_ge(rows_taken, k - RB + 1)
                query = slice(t * P, (t + 1) * P)
                dst = rows_bank[k % RB][:, 0:keys_seen[t]]
                if split:
                    mm = nc.tensor.matmul(dst, q_op[0:K_ROWS, i, j, query], k_op[0:K_ROWS, i, j, 0:keys_seen[t]],
                                          start=True, stop=True)
                else:
                    mm = nc.tensor.matmul(dst, q_op[0:3 * KR, i, 0, j, query], k_op[0:3 * KR, i, 0, j, 0:keys_seen[t]],
                                          start=True, stop=True)
                mm.then_inc(rows_psum, 1)

            def context_step(G, s):
                b = G // GROUPS
                if s == 0:
                    pe.wait_ge(probs_ready, group_units * (G + 1))
                    pe.wait_ge(v_ready, b + 1)
                    if G >= 1:
                        pe.wait_ge(o_copied, G)
                for j in range(GH):
                    mm = nc.tensor.matmul(o_bank[VW * j:VW * (j + 1), first_query[s]:T],
                                          values[:, b % 2, s, GH * (G % GROUPS) + j, :],
                                          probs[:, G % 2, j, offset[s]:offset[s] + width[s]],
                                          start=(s == 0), stop=(s == GROUP - 1))
                if s == GROUP - 1:
                    mm.then_inc(o_psum, 1)

            def turn_context(G):
                pe.wait_ge(o_copied, G + 1)
                bank_free(misc_last, t_norm, G + 1)
                for t in range(GROUP):
                    mm = nc.tensor.transpose(misc_bank[:, t * P:(t + 1) * P], context_t[:, t * P:(t + 1) * P], g.ident[:])
                mm.then_inc(t_psum, 1)

            def turn_rows(b):
                pe.wait_ge(t_norm, GROUPS * (b + 1))
                bank_free(misc_last, c_ready, b + 1)
                for t in range(GROUP):
                    mm = nc.tensor.transpose(misc_bank[:, t * P:(t + 1) * P], context[:, t, :], g.ident[:])
                mm.then_inc(c_psum, 1)

            def project_out(b):
                pe.wait_ge(c_ready, b + 1)
                bank_free(misc_last, added, b + 1)
                for t in range(GROUP):
                    mm = nc.tensor.matmul(misc_bank[:, t * D:(t + 1) * D], columns[:, t * P:(t + 1) * P], wo[:],
                                          start=True, stop=True)
                mm.then_inc(y_psum, 1)

            def turn_maxima(G):
                pe.wait_ge(max_split, G + 1)
                bank_free(misc_last, max_cols, G + 1)
                bank = misc_bank[:].bitcast(BF16)
                for t in range(GROUP):
                    mm = nc.tensor.transpose(bank[0:MAX_ROWS, t * P:(t + 1) * P],
                                             max_parts[:, t, :, :].rearrange("p k h -> p (k h)"), g.identb[:])
                mm.then_inc(max_psum, 1)

            def turn_norm(b):
                bank_free(prep_last, *((ln.xnt, b + 1) if gate is None else (ln.logits, b + 1)))
                ln_transpose(g, pe, ln, b, prep_bank)

            def project_qk(b, side):
                pe.wait_ge(loaded, weights.loads)
                bank_free(prep_last, taken, 2 * b + side + 1)
                nc.tensor.matmul(prep_bank[:], (wq, wk)[side][:], columns_of(b), start=True, stop=True).then_inc(proj, 1)

            def first_projections():
                pe.wait_ge(loaded, weights.loads)
                for side, bank in enumerate((prep_bank, misc_bank)):
                    nc.tensor.matmul(bank[:], (wq, wk)[side][:], columns_of(0), start=True, stop=True).then_inc(proj, 1)
                prep_last[:] = [(taken, 1)]
                misc_last[:] = [(taken, 2)]

            def project_values(b):
                bank_free(prep_last, v_ready, b + 1)
                for t in range(GROUP):
                    mm = nc.tensor.matmul(prep_bank[:, t * D:(t + 1) * D], columns_of(b)[:, t * P:(t + 1) * P], wv[:],
                                          start=True, stop=True)
                mm.then_inc(v_psum, 1)

            def project_tile(b, t, apart):
                pe.wait_ge(loaded, weights.loads)
                bank = misc_bank if apart else prep_bank
                bank_free(misc_last if apart else prep_last, taken, GROUP * b + t + 1)
                nc.tensor.matmul(bank[:], columns_of(b)[:, t * P:(t + 1) * P], wqk[:], start=True, stop=True
                                 ).then_inc(proj, 1)

            def turn_outer(G, side):
                pe.wait_ge(outer_ready, 2 * G + side + 1)
                bank_free(prep_last, rem_ready, 2 * G + side + 1)
                for t in range(GROUP):
                    mm = nc.tensor.transpose(prep_bank[:, t * P:(t + 1) * P], outer[:, G % 2, side, t, :], g.ident[:])
                mm.then_inc(outer_psum, 1)

            for n, b, q in slots():
                C, R = 0 <= n < NG, 0 <= n + 2 < NG
                if C:
                    pe.wait_ge(max_loaded, 16 * (n + 1))
                if R:
                    pe.wait_ge(op_loaded[(n + 2) % RING], 16 * op_loads * ((n + 2) // RING + 1))
                    if n + 2 < RING:
                        pe.wait_ge(prepared, n + 3)
                if not split and 0 <= n + 5 < NG:
                    turn_outer(n + 5, 0)
                for j in range(GH):
                    for t in range(GROUP):
                        if R and causal:
                            rows_tile(n + 2, j, t)
                        if C and t < U:
                            columns_unit(n, j, t)
                        if R and not causal:
                            rows_tile(n + 2, j, t)
                        if t == (2 if causal else 1) and 0 <= n - 1 < NG:
                            context_step(n - 1, j)
                    if j == 0:
                        if 0 <= n + 1 < NG:
                            turn_maxima(n + 1)
                    elif j == 1:
                        if 0 <= n - 2 < NG:
                            turn_context(n - 2)
                        if split and n == -2 * GROUPS + 2:
                            first_projections()
                        elif split and q in (2, 3) and 1 <= b + 2 < B:
                            project_qk(b + 2, q - 2)
                        if not split and 0 <= n + 5 < NG:
                            turn_outer(n + 5, 1)
                    elif j == 2:
                        if (n - 3) % GROUPS == GROUPS - 1 and 0 <= n - 3 < NG:
                            project_out((n - 3) // GROUPS)
                        if split and q == 0 and 0 <= b + 1 < B:
                            project_values(b + 1)
                        if q == 3 and 0 <= b - 1 < B:
                            turn_norm(b - 1)
                    else:
                        if q == 3 and 0 <= b - 1 < B:
                            ln_logits(g, pe, ln, b - 1, prep_bank)
                        if routing and q == 2 and 0 <= b - 2 < B - 1:
                            bank_free(prep_last, routing.taken, b - 1)
                            routing.count(pe, b - 2, prep_bank)
                        if (n - 2) % GROUPS == GROUPS - 1 and 0 <= n - 2 < NG:
                            turn_rows((n - 2) // GROUPS)
                    if (b, q, j) in tiles_at:
                        project_tile(*tiles_at[b, q, j])

        @block.scalar
        def _(act):
            def exponentials(G, j):
                for u, at in zip(range(U), unit_at):
                    k = G * group_units + j * U + u
                    w = sum(width[s] for s in units[u])
                    act.wait_ge(cols_psum, k + 1)
                    if G >= 2 and j == 0 and u == 0:
                        act.wait_ge(o_psum, G - 1)
                    nc.scalar.activation(probs[:, G % 2, j, at:at + w], cols_bank[k % CB][:, 0:w], ACT.Exp
                                         ).then_inc(probs_ready, 1)

            def copy_context(G):
                act.wait_ge(o_psum, G + 1)
                if G >= 1:
                    act.wait_ge(t_psum, G)
                nc.scalar.copy(context_t[:], o_bank[:]).then_inc(o_copied, 1)

            def copy_columns(b):
                act.wait_ge(c_psum, b + 1)
                if b >= 1:
                    act.wait_ge(y_psum, b)
                nc.scalar.copy(columns[:], misc_bank[:]).then_inc(c_ready, 1)

            def copy_maxima(G):
                act.wait_ge(max_psum, G + 1)
                if G >= 1:
                    act.wait_ge(max_loaded, 16 * G)
                nc.scalar.copy(max_t[:], misc_bank[:].bitcast(BF16)[0:MAX_ROWS, 0:T]).then_inc(max_cols, 1)

            def high_part(b, side):
                act.wait_ge(taken, 2 * b + side + 1)
                if b >= 1:
                    act.wait_ge(written, 16 * 6 * b)
                nc.scalar.copy(parts[:, side, 0, :], rest[:, side, :]).then_inc(hi_ready, 1)

            def first_parts():
                for side in range(2):
                    high_part(0, side)
                for side in range(2):
                    act.wait_ge(rem_ready, side + 1)
                    nc.scalar.copy(parts[:, side, 1, :], rest[:, side, :]).then_inc(mid_ready, 1)

            def take_tile(b, t, apart):
                act.wait_ge(proj, GROUP * b + t + 1)
                if b >= 2:
                    act.wait_ge(outer_ready, 2 * GROUPS * (b - 1))
                    act.wait_ge(v_ready, b - 1)
                bank = misc_bank if apart else prep_bank
                nc.scalar.mul(pj[:, b % 2, t, 0:HEADS * R1], bank[:, 0:HEADS * R1], scale)
                nc.scalar.copy(pj[:, b % 2, t, HEADS * R1:T], bank[:, HEADS * R1:T]).then_inc(taken, 1)

            def high_outer(G, side):
                act.wait_ge(outer_psum, 2 * G + side + 1)
                if G >= 2:
                    act.wait_ge(written, 32 * (G - 1))
                nc.scalar.copy(parts[:, G % 2, side, 2 * side, :], prep_bank[:]).then_inc(hi_ready, 1)

            def middle_outer(G, side):
                act.wait_ge(rem_ready, 2 * G + side + 1)
                nc.scalar.copy(parts[:, G % 2, side, 1, :], rest[:, side, :]).then_inc(mid_ready, 1)

            for n, b, q in slots():
                C, O = 0 <= n < NG, 0 <= n + 5 < NG
                if kind == 0 and n == 2:
                    write_untaken(g, act, (1,))
                if 0 <= n - 2 < NG:
                    copy_context(n - 2)
                if not split and O:
                    high_outer(n + 5, 0)
                for j in range(GH):
                    if C:
                        exponentials(n, j)
                    if j == 0:
                        if (n - 3) % GROUPS == GROUPS - 1 and 0 <= n - 3 < NG:
                            copy_columns((n - 3) // GROUPS)
                    elif j == 1:
                        if 0 <= n + 1 < NG:
                            copy_maxima(n + 1)
                        if not split and O:
                            middle_outer(n + 5, 0)
                            high_outer(n + 5, 1)
                    elif j == 2:
                        if q == 3 and 0 <= b - 1 < B:
                            ln_columns(g, act, ln, b - 1, prep_bank)
                        if split and n == -2 * GROUPS + 2:
                            first_parts()
                        elif split and q in (2, 3) and 1 <= b + 2 < B:
                            high_part(b + 2, q - 2)
                    else:
                        if q == 3 and 0 <= b - 1 < B:
                            ln_copy_logits(g, act, ln, b - 1, prep_bank)
                        if not split and O:
                            middle_outer(n + 5, 1)
                    if (b, q, j) in tiles_at:
                        take_tile(*tiles_at[b, q, j])

        @block.vector
        def _(v):
            steps = [0]

            def after(ins):
                steps[0] += 1
                ins.then_inc(norm_step, 1)
                v.wait_ge(norm_step, steps[0])

            def row_maxima(G, j):
                h = GH * (G % GROUPS) + j
                for t in range(GROUP):
                    k = G * group_tiles + j * GROUP + t
                    v.wait_ge(rows_psum, k + 1)
                    bank = rows_bank[k % RB]
                    best = maxima[:, G % 2, t, j:j + 1]
                    w = keys_seen[t]
                    if kind == 3:
                        ins = nc.vector.tensor_reduce(best, bank[:], axis=AX, op=ALU.max)
                    elif kind == 1:
                        ins = nc.vector.tensor_tensor_reduce(out=bank[:, 0:w], in0=bank[:, 0:w], in1=g.mask_qk[:, T - w:T],
                                                             scale=1.0, scalar=-3.0e38, op0=ALU.add, op1=ALU.max, accum_out=best)
                    else:
                        near = min(2 * P, w)
                        if t >= 2:
                            nc.vector.tensor_reduce(far[:, G % 2, t, j:j + 1], bank[:, 0:w - near], axis=AX, op=ALU.max)
                        ins = nc.vector.tensor_tensor_reduce(out=bank[:, w - near:w], in0=bank[:, w - near:w],
                                                             in1=bias_qk[:, h, 2 * P - near:2 * P], scale=1.0, scalar=-3.0e38,
                                                             op0=ALU.add, op1=ALU.max, accum_out=best)
                    ins.then_inc(rows_taken, 1)

            def split_maxima(G):
                v.wait_ge(rows_taken, group_tiles * (G + 1))
                best = maxima[:, G % 2, :, :]
                if G >= 1:
                    v.wait_ge(max_psum, G)
                if kind == 0:
                    after(nc.vector.tensor_tensor(maxima[:, G % 2, 2:GROUP, :], maxima[:, G % 2, 2:GROUP, :],
                                                  far[:, G % 2, 2:GROUP, :], ALU.max))
                part = lambda k: max_parts[:, :, k, :]
                after(nc.vector.tensor_scalar(part(0), best, -1.0, None, ALU.mult))
                after(nc.vector.scalar_tensor_tensor(max_rest[:], best, -1.0, part(0), ALU.mult, ALU.subtract))
                after(nc.vector.tensor_copy(part(1), max_rest[:]))
                nc.vector.tensor_tensor(part(2), max_rest[:], part(1), ALU.subtract).then_inc(max_split, 1)

            def normalise(G):
                v.wait_ge(t_psum, G + 1)
                q = G % GROUPS
                by_head = misc_bank[:].rearrange("p (t j w) -> p t j w", t=GROUP, j=GH)
                after(nc.vector.reciprocal(recip[:], by_head[:, :, :, HD]))
                if q == 0 and G >= GROUPS:
                    v.wait_ge(c_psum, G // GROUPS)
                dst = context[:, :, GH * q * HD:GH * (q + 1) * HD].rearrange("p t (j d) -> p t j d", d=HD)
                nc.vector.tensor_tensor(dst, by_head[:, :, :, 0:HD], recip[:, :, :, None].to_broadcast([P, GROUP, GH, HD]),
                                        ALU.mult).then_inc(t_norm, 1)

            rows_of = lambda b: g.x[:, GROUP * b:GROUP * (b + 1), :]

            def add_bias(b):
                nc.vector.tensor_tensor(rows_of(b), rows_of(b), bo[:, None, :].to_broadcast([P, GROUP, D]), ALU.add
                                        ).then_inc(biased, 1)

            def add_out(b):
                v.wait_ge(y_psum, b + 1)
                v.wait_ge(biased, b + 1)
                nc.vector.tensor_tensor(rows_of(b), rows_of(b), misc_bank[:].rearrange("p (t d) -> p t d", d=D), ALU.add
                                        ).then_inc(added, 1)
                v.wait_ge(added, b + 1)

            def first_parts():
                for side, bank in enumerate((prep_bank, misc_bank)):
                    take_qk(0, side, bank)
                for side in range(2):
                    v.wait_ge(hi_ready, side + 1)
                    nc.vector.tensor_tensor(rest[:, side, :], rest[:, side, :], parts[:, side, 0, :], ALU.subtract
                                            ).then_inc(rem_ready, 1)
                for side in range(2):
                    v.wait_ge(mid_ready, side + 1)
                    nc.vector.tensor_tensor(parts[:, side, 2, :], rest[:, side, :], parts[:, side, 1, :], ALU.subtract
                                            ).then_inc(parts_ready, 1)

            def take_qk(b, side, bank=prep_bank):
                v.wait_ge(proj, 2 * b + side + 1)
                if b >= 1:
                    v.wait_ge(parts_ready, 2 * (b - 1) + side + 1)
                if side == 0:
                    ins = nc.vector.tensor_scalar(rest[:, 0, :], bank[:], bq[:], scale, ALU.add, ALU.mult)
                else:
                    ins = nc.vector.tensor_scalar(rest[:, 1, :], bank[:], bk[:], None, ALU.add)
                ins.then_inc(taken, 1)

            def take_values(b):
                v.wait_ge(v_psum, b + 1)
                if b == 0:
                    v.wait_ge(values_zeroed, 2)
                if b >= 2:
                    v.wait_ge(o_psum, GROUPS * (b - 1))
                nc.vector.tensor_tensor(values[:, b % 2, :, :, 0:HD],
                                        prep_bank[:].rearrange("p (t h d) -> p t h d", t=GROUP, h=HEADS),
                                        bv[:].rearrange("p (h d) -> p h d", d=HD)[:, None, :, :]
                                        .to_broadcast([P, GROUP, HEADS, HD]), ALU.add).then_inc(v_ready, 1)

            def outer_rest(G, side):
                v.wait_ge(hi_ready, 2 * G + side + 1)
                if G >= 1:
                    v.wait_ge(parts_ready, 2 * (G - 1) + side + 1)
                nc.vector.tensor_tensor(rest[:, side, :], prep_bank[:], parts[:, G % 2, side, 2 * side, :], ALU.subtract
                                        ).then_inc(rem_ready, 1)

            def place_selectors(i):
                if split:
                    dst, rows = k_op[MAX_AT:K_ROWS, i, :, :], g.head_selector[MAX_AT:K_ROWS]
                else:
                    dst, rows = k_op[MAX_AT1:P, i, 1, :, :], g.head_selector1[MAX_AT1:P]
                nc.vector.tensor_copy(dst, rows[:, :, None].to_broadcast([dst.shape[0], GH, T])).then_inc(prepared, 1)

            if split:
                nc.vector.memset(zeros[:].bitcast(F32), 0.0).then_inc(zeroed, 1)
            def route_next(r, q, j):
                at = GROUPS * (q - 1) + j
                if at == 0:
                    v.wait_ge(ln.logits, r + 1)
                if at in range(5):
                    routing.choose_step(v, at, 0, r)
                elif at == 5 and routing.choices == 2:
                    for step in (0, 1):
                        routing.choose_step(v, step, 1, r)
                elif at == 6 and routing.choices == 2:
                    for step in (2, 3, 4):
                        routing.choose_step(v, step, 1, r)
                elif q == 3:
                    for step in ((0, 1), (2, 3), (4, 5), (6,))[j]:
                        routing.place_step(v, step, 0, GROUP * r, GROUP, prep_bank)

            for n, b, q in slots():
                for i in range(RING):
                    if n == -GROUPS + (0 if split else i):
                        place_selectors(i)
                if not split and 0 <= n + 6 < GROUPS:
                    make_outer(v, nc.vector, n + 6)
                if 0 <= n + 1 < NG:
                    split_maxima(n + 1)
                for j in range(GH):
                    if 0 <= n + 2 < NG:
                        row_maxima(n + 2, j)
                    if routing and 0 <= b - 2 < B - 1:
                        route_next(b - 2, q, j)
                    if j == 0:
                        if split and q == 1 and 0 <= b + 1 < B:
                            take_values(b + 1)
                        if q == 3 and 0 <= b - 1 < B:
                            ln_moments(g, v, ln, b - 1)
                        if not split and 0 <= n + 5 < NG:
                            outer_rest(n + 5, 0)
                    elif j == 1:
                        if q == 2 and 0 <= b - 1 < B:
                            add_bias(b - 1)
                        if q == 3 and 0 <= b - 1 < B:
                            ln_rows(g, v, ln, b - 1)
                    elif j == 2:
                        if 0 <= n - 2 < NG:
                            normalise(n - 2)
                        if split and n == -2 * GROUPS + 2:
                            first_parts()
                        elif split and q in (2, 3) and 1 <= b + 2 < B:
                            take_qk(b + 2, q - 2)
                        if not split and 0 <= n + 5 < NG:
                            outer_rest(n + 5, 1)
                    elif j == 3:
                        if (n - 3) % GROUPS == GROUPS - 1 and 0 <= n - 3 < NG:
                            add_out((n - 3) // GROUPS)
                            ln_tile_stats(g, v, ln, (n - 3) // GROUPS)

        @block.gpsimd
        def _(pool):
            def low_outer(G, side):
                pool.wait_ge(mid_ready, 2 * G + side + 1)
                nc.gpsimd.tensor_tensor(parts[:, G % 2, side, 2 - 2 * side, :], rest[:, side, :], parts[:, G % 2, side, 1, :],
                                        ALU.subtract).then_inc(parts_ready, 1)

            def low_parts(b, side):
                k = 2 * b + side
                pool.wait_ge(hi_ready, k + 1)
                nc.gpsimd.tensor_tensor(rest[:, side, :], rest[:, side, :], parts[:, side, 0, :], ALU.subtract
                                        ).then_inc(rem_ready, 1)
                pool.wait_ge(rem_ready, k + 1)
                nc.gpsimd.tensor_copy(parts[:, side, 1, :], rest[:, side, :]).then_inc(mid_ready, 1)
                pool.wait_ge(mid_ready, k + 1)
                nc.gpsimd.tensor_tensor(parts[:, side, 2, :], rest[:, side, :], parts[:, side, 1, :], ALU.subtract
                                        ).then_inc(parts_ready, 1)

            def copy_values(b):
                pool.wait_ge(taken, GROUP * (b + 1))
                if b >= 2:
                    pool.wait_ge(o_psum, GROUPS * (b - 1))
                nc.gpsimd.tensor_copy(values[:, b % 2, :, :, 0:HD],
                                      pj[:, b % 2, :, T - D:T].rearrange("p t (h d) -> p t h d", d=HD)).then_inc(v_ready, 1)

            for n, b, q in slots():
                if n == -GROUPS:
                    nc.gpsimd.memset(values[:], 0.0).then_inc(values_zeroed, 1)
                    pool.wait_ge(values_zeroed, 1)
                    nc.gpsimd.memset(values[:, :, :, :, HD:HD + 1].rearrange("p b t h w -> p (b t h) w"), 1.0
                                     ).then_inc(values_zeroed, 1)
                    pool.wait_ge(values_zeroed, 2)
                if q == 3 and 0 <= b - 1 < B:
                    ln_rstd(g, pool, ln, b - 1)
                if not split and GROUPS <= n + 6 < NG:
                    make_outer(pool, nc.gpsimd, n + 6)
                if not split and 0 <= n + 5 < NG:
                    for side in range(2):
                        low_outer(n + 5, side)
                if not split and (n + 3) % GROUPS == 0 and 0 <= n + 3 < NG:
                    copy_values((n + 3) // GROUPS)
                if split and q in (2, 3) and 1 <= b + 2 < B:
                    low_parts(b + 2, q - 2)
                if routing and q == 3 and 0 <= b - 2 < B - 1:
                    routing.scatter(pool, 0, GROUP * (b - 2), GROUP, g.xn)


class Shared:
    def __init__(self, nc, a, out):
        sb = lambda n, shape, dt=F32: nc.alloc_sbuf_tensor(n, shape, dt)
        self.nc = nc
        self.a, self.out = a, out
        self.spent = []
        self.x = sb("x_rows", [P, TILES, D])
        self.xn = sb("normalised_rows", [P, TILES, D + 1])
        self.xnt = sb("normalised_columns", [P, TOKENS])
        self.gates = sb("gates", [P, 4, E])
        self.logits = sb("logits", [P, TILES, E])
        self.gamma_beta = sb("gamma_beta", [P, 2])
        self.untaken = sb("untaken", [P, D + 1])
        self.token_i = sb("token_numbers_i", [P, 2 * TILES], U32)
        self.token = sb("token_numbers", [P, 2 * TILES])
        self.expert_selector = sb("expert_selector", [P, E // 2, P], BF16)
        self.stats = sb("stats", [P, TILES, 6])
        self.moments = sb("moments", [P, TILES, 2])
        self.var_eps = sb("var_eps", [P, TILES])
        self.rstd = sb("rstd", [P, TILES])
        self.neg_half = sb("neg_half", [P, TILES])
        self.ident = sb("ident", [P, P])
        self.flip = sb("flip", [P, P])
        self.identb = sb("identb", [P, P], BF16)
        self.onesb = sb("onesb", [P, P], BF16)
        self.beforeb = sb("beforeb", [P, P], BF16)
        self.mask_kq = sb("mask_kq", [P, P], BF16)
        self.mask_qk = sb("mask_qk", [P, T])
        self.rev = sb("rev", [P, TILES, E])
        self.tie = sb("tie", [P, TILES])
        self.spare = sb("spare", [P, 1])
        self.bank = [nc.alloc_psum_tensor(f"bank{i}", [P, T], F32) for i in range(8)]
        self.head_selector = sb("head_selector", [P, GH], BF16)
        self.head_selector1 = sb("head_selector1", [P, GH], BF16)
        self.terms = [[nc.dram_tensor(f"score_terms{i}_{side}", (TERMS, P, T), BF16).ap() for side in range(2)]
                      for i in range(2)]
        self.bias_lines = nc.dram_tensor("bias_lines", (HEADS, 2 * 3 * P), F32).ap()
        self.dispatched = [nc.dram_tensor(f"dispatched{n}", (slots, D + 1), F32).ap()
                           for n, slots in enumerate((E * CAP0, E * CAP0, E * CAP3, E * CAP3))]
        self.returned = nc.dram_tensor("returned", (2 * TOKENS, D), F32).ap()
        self.untaken_written = [nc.alloc_semaphore(f"untaken_written{n}") for n in range(4)]
        self.returned_zeroed = nc.alloc_semaphore("returned_zeroed")


def program(nc, a, out, wanted=range(12)):
    g = Shared(nc, a, out)
    gate = [g.gates[:, layer, :] for layer in range(4)]
    route = lambda ctx, n, name, choices, cap: Routing(g, ctx, name, n, choices, cap)
    mixture = lambda name, layer, routing, routed, **more: moe_capacity(
        g, name, routing, routed, a[layer + "_w1"], a[layer + "_b1"], a[layer + "_w2"], a[layer + "_b2"], **more)
    with nc.sbuf_tensor("products2", [P, 2, 4 * D], F32) as products:
        with ExitStack() as routes:
            first, second = route(routes, 0, "route0_0", 1, CAP0), route(routes, 1, "route0_1", 1, CAP0)
            with ExitStack() as ctx:
                weights = AttentionWeights(g, ctx, 0)
                bias_kq = ctx.enter_context(nc.sbuf_tensor("bias_kq", [P, HEADS, 3, 2 * P], BF16))
                bias_qk = ctx.enter_context(nc.sbuf_tensor("bias_qk", [P, HEADS, 2 * P], F32))
                with ExitStack() as beside:
                    bias = RelativeBias(g, beside, "bias", bias_kq, bias_qk)
                    setup(g, bias)
                    mixture("moe0_0", "l0", first, 0, beside=bias, prefetch=weights)
                clear_semaphores(g, ("att0", "route0_1"))
                attention(g, "att0", 0, weights, gate[0], (bias_kq, bias_qk), routing=second)
            with ExitStack() as ctx:
                mixture("moe0_1", "l0", second, B - 1, gate=gate[1], products=ExpertProducts(g, ctx, "products2", products))
        clear_semaphores(g)
        with ExitStack() as ctx:
            weights = AttentionWeights(g, ctx, 1)
            ffn1(g, "ffn1_0", prefetch=weights)
            attention(g, "att1", 1, weights, gate[1])
        ffn1(g, "ffn1_1", gate[2])
        clear_semaphores(g)
        with ExitStack() as ctx:
            weights = RecurrenceWeights(g, ctx)
            ffn2(g, "ffn2_0", products, prefetch=weights)
            recurrence2(g, "rec2", weights, gate[2])
        ffn2(g, "ffn2_1", products, gate[3])
    clear_semaphores(g)
    with ExitStack() as routes:
        first, second = route(routes, 2, "route3_0", 2, CAP3), route(routes, 3, "route3_1", 2, CAP3)
        with ExitStack() as ctx:
            weights = AttentionWeights(g, ctx, 3)
            mixture("moe3_0", "l3", first, 0, twice=True, prefetch=weights)
            attention(g, "att3", 3, weights, gate[3], routing=second)
        mixture("moe3_1", "l3", second, B - 1, last=True)


def lay_out(i):
    import numpy as np
    t = lambda a: np.ascontiguousarray(np.asarray(a).T)
    n = lambda a: np.ascontiguousarray(np.asarray(a))
    by_chunk = lambda b: n(np.asarray(b).reshape(E * CH, P).T)
    dh = lambda w: n(np.asarray(w).reshape(HEADS, HD, -1).transpose(1, 0, 2).reshape(HEADS * HD, -1).T)
    dhb = lambda b: n(np.asarray(b).reshape(HEADS, HD).T.reshape(P, 1))
    ins = {"x": n(np.asarray(i["L0_attn_x"]).reshape(TOKENS, D))}
    ins["l0_gate"] = t(i["L0_ffn_gate_w"])
    ins["l3_gate"] = n(i["L3_ffn_wg"])
    for layer, f in (("l0", "L0_ffn"), ("l3", "L3_ffn")):
        ins[layer + "_w1"] = n(np.asarray(i[f + "_w1"]).reshape(E * P, HID))
        ins[layer + "_b1"] = by_chunk(i[f + "_b1"])
        ins[layer + "_w2"] = n(np.asarray(i[f + "_w2"]).reshape(E * HID, D))
        ins[layer + "_b2"] = n(i[f + "_b2"])
    for layer, w, bias, wo, bo in (("l0", "L0_attn_qkv_w", "L0_attn_qkv_b", "L0_attn_proj_w", "L0_attn_proj_b"),
                                   ("l3", "L3_attn_W_qkv", "L3_attn_b_qkv", "L3_attn_W_out", "L3_attn_b_out")):
        q, k, v = np.split(np.asarray(i[w]), 3)
        bq, bk, bv = np.split(np.asarray(i[bias]), 3)
        ins[layer + "_wq"], ins[layer + "_wk"], ins[layer + "_wv"] = dh(q), dh(k), t(v)
        ins[layer + "_bq"], ins[layer + "_bk"], ins[layer + "_bv"] = dhb(bq), dhb(bk), n(bv)
        ins[layer + "_wo"], ins[layer + "_bo"] = t(i[wo]), n(i[bo])
    ins["l3_gamma_beta"] = n(np.stack([np.asarray(i["L3_attn_ln_gamma"]), np.asarray(i["L3_attn_ln_beta"])], axis=1))
    ins["l0_rel"] = n(np.asarray(i["L0_attn_rel_pos_emb"])[P - 1:2 * P - 1])
    ins["l0_rel_back"] = n(np.asarray(i["L0_attn_rel_pos_emb"])[P - 1:2 * P - 1][::-1])
    ins["l1_gate"] = t(i["L1_ffn_gate_weight"])
    for m, shared in (("gate", "ws_gate"), ("up", "ws_up")):
        ins["l1_" + m + "_w"] = n(np.concatenate([np.asarray(i["L1_ffn_w_" + m]).reshape(-1, D).T,
                                                  np.asarray(i["L1_ffn_" + shared]).T], axis=1))
    ins["l1_down_w"] = n(np.concatenate([np.asarray(i["L1_ffn_w_down"]).transpose(0, 2, 1).reshape(-1, D),
                                         np.asarray(i["L1_ffn_ws_down"]).T], axis=0))
    ins["l1_wqk"] = n(np.concatenate([np.asarray(i["L1_attn_" + w]).T for w in ("Wq1", "Wk1", "Wq2", "Wk2", "Wv")], axis=1))
    ins["l1_wo"], ins["l1_bo"] = t(i["L1_attn_Wo"]), n(i["L1_attn_bo"])
    ins["l2_gate"] = t(i["L2_ffn_w_gate"])
    ins["l2_w_in"] = n(np.asarray(i["L2_ffn_w_in"]).reshape(E * HID, D))
    ins["l2_w_out"] = n(np.asarray(i["L2_ffn_w_out"]).transpose(0, 2, 1).reshape(E * HID, D))
    ins["l2_win"], ins["l2_wout"] = n(i["L2_attn_W_in"]), n(i["L2_attn_W_out"])
    ins["l2_bin"] = n(np.asarray(i["L2_attn_b_in"]).reshape(2, P).T)
    ins["l2_bout"] = n(i["L2_attn_b_out"])
    return ins


def kernel(**inputs):
    import concourse.bacc as bacc
    from concourse.bass_utils import run_bass_kernel_spmd
    arrays = lay_out(inputs)
    nc = bacc.Bacc("TRN2", target_bir_lowering=False, num_devices=1)
    a = {n: nc.dram_tensor(n, v.shape, F32, kind="ExternalInput").ap() for n, v in arrays.items()}
    out = nc.dram_tensor("x_out", (TOKENS, D), F32, kind="ExternalOutput").ap()
    program(nc, a, out)
    got = run_bass_kernel_spmd(nc, [arrays], core_ids=[0]).results[0]["x_out"]
    return got.reshape(B, T, D)
```
